# Optimizing a Trainium2 kernel written in Bass

```python
import numpy as np
import jax
import jax.numpy as jnp

def _softmax(x, axis=-1):
    return jax.nn.softmax(x, axis=axis)

def _gelu(x):
    return jax.nn.gelu(x, approximate=True)

def _silu(x):
    return jax.nn.silu(x)

def _sigmoid(x):
    return jax.nn.sigmoid(x)

def _layernorm(x, axis=-1, eps=1e-05):
    m = jnp.mean(x, axis=axis, keepdims=True)
    v = jnp.var(x, axis=axis, keepdims=True)
    return (x - m) / jnp.sqrt(v + eps)

def _scatter_add(tgt, idx, src, axis=0):
    return tgt.at[idx].add(src)

def _segment_sum(src, seg, n):
    return jax.ops.segment_sum(src, seg, n)
kernel_name = 'mk_prb_d4_jaxref_r8_b79cc8'

def setup_inputs(seed: int=0):
    np.random.seed(seed)
    _w = jnp.asarray

    def _L0_attn_setup():
        import jax, jax.numpy as jnp
        import numpy as np
        N_EMBD = 128
        N_HEAD = 16
        B, T = (2, 256)
        key = jax.random.key(seed)
        ks = jax.random.split(key, 9)
        s = 1.0 / np.sqrt(N_EMBD)
        return {'x': jax.random.normal(ks[0], (B, T, N_EMBD), dtype=jnp.float32), 'Wq': jax.random.normal(ks[1], (N_EMBD, N_EMBD), dtype=jnp.float32) * s, 'bq': jax.random.normal(ks[2], (N_EMBD,), dtype=jnp.float32) * s, 'Wk': jax.random.normal(ks[3], (N_EMBD, N_EMBD), dtype=jnp.float32) * s, 'bk': jax.random.normal(ks[4], (N_EMBD,), dtype=jnp.float32) * s, 'Wv': jax.random.normal(ks[5], (N_EMBD, N_EMBD), dtype=jnp.float32) * s, 'bv': jax.random.normal(ks[6], (N_EMBD,), dtype=jnp.float32) * s, 'Wp': jax.random.normal(ks[7], (N_EMBD, N_EMBD), dtype=jnp.float32) * s, 'bp': jax.random.normal(ks[8], (N_EMBD,), dtype=jnp.float32) * s}
    _L0_attn_in = _L0_attn_setup()

    def _L0_ffn_setup():
        import jax, jax.numpy as jnp
        import numpy as np
        FEATURES = 128
        D_IN = 128

        def fp8_gemm_optimized(x, input_scale, kernel, kernel_scale):
            s_in = input_scale[0]
            s_k = kernel_scale[0]
            x_q = (x.astype(jnp.float32) / s_in).astype(jnp.float8_e4m3fn)
            k_q = (kernel.astype(jnp.float32) / s_k).astype(jnp.float8_e4m3fn)
            y = jnp.dot(x_q.astype(jnp.float32), k_q.astype(jnp.float32), preferred_element_type=jnp.float32)
            return y * (s_in * s_k)
        key = jax.random.key(seed)
        kx, kk, kb = jax.random.split(key, 3)
        x = jax.random.normal(kx, (4, 1024, D_IN), dtype=jnp.float32)
        limit = np.sqrt(6.0 / (D_IN + FEATURES)).astype(np.float32)
        kernel = jax.random.uniform(kk, (D_IN, FEATURES), dtype=jnp.float32, minval=-limit, maxval=limit).astype(jnp.bfloat16)
        input_scale = jnp.ones((1,), dtype=jnp.float32)
        kernel_scale = jnp.ones((1,), dtype=jnp.float32)
        bias = jnp.zeros((FEATURES,), dtype=jnp.bfloat16)
        return {'x': x, 'kernel': kernel, 'input_scale': input_scale, 'kernel_scale': kernel_scale, 'bias': bias}
    _L0_ffn_in = _L0_ffn_setup()

    def _L1_attn_setup():
        import jax, jax.numpy as jnp
        import numpy as np
        CHUNK = 64
        NORM_EPS = 1e-05
        DENOM_EPS = 1.0
        B, S, HID, H = (4, 512, 128, 8)
        D = HID // H

        def rmsnorm(x, w, eps=NORM_EPS):
            var = jnp.mean(x * x, axis=-1, keepdims=True)
            return x * jax.lax.rsqrt(var + eps) * w

        def chunked_linear_attn(q, k, v):
            b, s, h, d = q.shape
            n = s // CHUNK

            def to_chunks(x):
                return x.reshape(b, n, CHUNK, h, d).transpose(1, 0, 3, 2, 4)
            qc, kc, vc = (to_chunks(q), to_chunks(k), to_chunks(v))
            mask = jnp.tril(jnp.ones((CHUNK, CHUNK), dtype=q.dtype))

            def step(state, inp):
                qq, kk, vv = inp
                inter = jnp.einsum('bhcd,bhde->bhce', qq, state)
                scores = jnp.einsum('bhcd,bhed->bhce', qq, kk) * mask
                intra = jnp.einsum('bhce,bhed->bhcd', scores, vv)
                state = state + jnp.einsum('bhcd,bhce->bhde', kk, vv)
                return (state, inter + intra)
            init = jnp.zeros((b, h, d, d), dtype=q.dtype)
            _, o = jax.lax.scan(step, init, (qc, kc, vc))
            return o.transpose(1, 0, 3, 2, 4).reshape(b, s, h, d)
        key = jax.random.key(seed)
        k0, k1, k2, k3, k4 = jax.random.split(key, 5)
        hidden_states = jax.random.normal(k0, (B, S, HID), dtype=jnp.float32)
        Wq = jax.random.normal(k1, (HID, HID), dtype=jnp.float32) * 0.02
        Wk = jax.random.normal(k2, (HID, HID), dtype=jnp.float32) * 0.02
        Wv = jax.random.normal(k3, (HID, HID), dtype=jnp.float32) * 0.02
        Wo = jax.random.normal(k4, (HID, HID), dtype=jnp.float32) * 0.02
        norm_w = jnp.ones((D,), dtype=jnp.float32)
        return {'hidden_states': hidden_states, 'Wq': Wq, 'Wk': Wk, 'Wv': Wv, 'Wo': Wo, 'norm_w': norm_w}
    _L1_attn_in = _L1_attn_setup()

    def _L1_ffn_setup():
        import jax, jax.numpy as jnp
        import numpy as np
        D_MODEL, D_FF, RANK = (128, 512, 32)
        B, S = (4, 512)
        key = jax.random.key(seed)
        ks = jax.random.split(key, 7)
        return {'x': jax.random.normal(ks[0], (B, S, D_MODEL), dtype=jnp.float32), 'U1': jax.random.normal(ks[1], (D_MODEL, RANK), dtype=jnp.float32) * 0.02, 'V1': jax.random.normal(ks[2], (RANK, D_FF), dtype=jnp.float32) * 0.02, 'b1': jnp.zeros((D_FF,), dtype=jnp.float32), 'U2': jax.random.normal(ks[3], (D_FF, RANK), dtype=jnp.float32) * 0.02, 'V2': jax.random.normal(ks[4], (RANK, D_MODEL), dtype=jnp.float32) * 0.02, 'b2': jnp.zeros((D_MODEL,), dtype=jnp.float32)}
    _L1_ffn_in = _L1_ffn_setup()

    def _L2_attn_setup():
        import jax, jax.numpy as jnp
        import numpy as np
        B, N = (2, 256)
        H, R = (8, 64)
        IN_DIM, OUT_DIM = (64, 64)
        D = IN_DIM + OUT_DIM
        INIT = 1.0
        key = jax.random.key(seed)
        k1, k2, k3, k4 = jax.random.split(key, 4)
        x = jax.random.normal(k1, (B, N, D), dtype=jnp.float32)
        Wq = jax.random.normal(k2, (H * R, D), dtype=jnp.float32) * (INIT / np.sqrt(H * R * D))
        Wk = jax.random.normal(k3, (H * R, D), dtype=jnp.float32) * (INIT / np.sqrt(H * R * D))
        Wv = jax.random.normal(k4, (H * D, D), dtype=jnp.float32) * (INIT / np.sqrt(H * D * D))
        Wk = Wk.at[:, -1].set(0.0)
        rows = np.arange(1, H + 1) * D - 1
        Wv = Wv.at[rows, :IN_DIM].set(0.0)
        return {'x': x, 'Wq': Wq, 'Wk': Wk, 'Wv': Wv}
    _L2_attn_in = _L2_attn_setup()

    def _L2_ffn_setup():
        import jax, jax.numpy as jnp
        import numpy as np
        D_MODEL = 128
        DEPTH = 8
        M = 2 ** DEPTH
        N_INTERNAL = M - 1
        B, T = (8, 512)

        def _leaf_probs(gate):
            BT = gate.shape[0]
            lp = jnp.ones((BT, M), dtype=gate.dtype)
            for level in range(DEPTH):
                n = 2 ** level
                half = M // (2 * n)
                g = gate[:, n - 1:2 * n - 1]
                f = jnp.stack([1.0 - g, g], axis=-1)
                f = jnp.broadcast_to(f[..., None], (BT, n, 2, half))
                lp = lp * f.reshape(BT, M)
            return lp
        key = jax.random.key(seed)
        ks = jax.random.split(key, 7)
        x = jax.random.normal(ks[0], (B, T, D_MODEL), dtype=jnp.float32)
        Wq = jax.random.normal(ks[1], (D_MODEL, D_MODEL), dtype=jnp.float32) * 0.02
        routers = jax.random.normal(ks[2], (N_INTERNAL, D_MODEL), dtype=jnp.float32) * 0.02
        leaf_keys = jax.random.normal(ks[3], (M, D_MODEL), dtype=jnp.float32) * 0.02
        leaf_values = jax.random.normal(ks[4], (M, D_MODEL), dtype=jnp.float32) * 0.02
        Wout_w = jax.random.normal(ks[5], (D_MODEL, D_MODEL), dtype=jnp.float32) * 0.02
        Wout_b = jax.random.normal(ks[6], (D_MODEL,), dtype=jnp.float32) * 0.02
        return {'x': x, 'Wq': Wq, 'routers': routers, 'leaf_keys': leaf_keys, 'leaf_values': leaf_values, 'Wout_w': Wout_w, 'Wout_b': Wout_b}
    _L2_ffn_in = _L2_ffn_setup()

    def _L3_attn_setup():
        import jax, jax.numpy as jnp
        import numpy as np
        D_MODEL, D_STATE, D_CONV, EXPAND = (128, 16, 4, 2)
        D_INNER = EXPAND * D_MODEL
        DT_RANK = -(-D_MODEL // 16)
        B_SZ, L_SEQ = (2, 256)

        def _silu(x):
            return x * jax.nn.sigmoid(x)

        def _mamba_block(seq, ln_g, ln_b, in_proj_w, conv_w, conv_b, x_proj_w, dt_proj_w, dt_proj_b, A_log, D, out_proj_w, res_scale):
            B, L, _ = seq.shape
            mu = jnp.mean(seq, -1, keepdims=True)
            var = jnp.mean(jnp.square(seq - mu), -1, keepdims=True)
            xn = (seq - mu) * jax.lax.rsqrt(var + 1e-05) * ln_g + ln_b
            xz = jnp.einsum('bld,ed->ble', xn, in_proj_w)
            x, z = jnp.split(xz, 2, axis=-1)
            x_pad = jnp.pad(x, ((0, 0), (D_CONV - 1, 0), (0, 0)))
            xc = conv_b
            for k in range(D_CONV):
                xc = xc + x_pad[:, k:k + L, :] * conv_w[:, k]
            x = _silu(xc)
            x_dbl = jnp.einsum('bld,ed->ble', x, x_proj_w)
            dt = jax.nn.softplus(jnp.einsum('blr,dr->bld', x_dbl[..., :DT_RANK], dt_proj_w) + dt_proj_b)
            Bm = x_dbl[..., DT_RANK:DT_RANK + D_STATE]
            Cm = x_dbl[..., DT_RANK + D_STATE:]
            A = -jnp.exp(A_log)

            def step(h, inputs):
                dt_t, B_t, C_t, x_t = inputs
                dA = jnp.exp(dt_t[..., None] * A)
                h = h * dA + (dt_t * x_t)[..., None] * B_t[:, None, :]
                y = jnp.einsum('bds,bs->bd', h, C_t)
                return (h, y)
            h0 = jnp.zeros((B, D_INNER, D_STATE), x.dtype)
            _, ys = jax.lax.scan(step, h0, (jnp.swapaxes(dt, 0, 1), jnp.swapaxes(Bm, 0, 1), jnp.swapaxes(Cm, 0, 1), jnp.swapaxes(x, 0, 1)))
            y = jnp.swapaxes(ys, 0, 1) + D * x
            y = y * _silu(z)
            out = jnp.einsum('ble,de->bld', y, out_proj_w)
            return seq + res_scale * out
        key = jax.random.key(seed)
        ks = jax.random.split(key, 12)
        s = lambda k, shp, sc: jax.random.normal(k, shp, dtype=jnp.float32) * sc
        inp = {'seq': s(ks[0], (B_SZ, L_SEQ, D_MODEL), 1.0), 'ln_g': jnp.ones((D_MODEL,), jnp.float32), 'ln_b': jnp.zeros((D_MODEL,), jnp.float32), 'in_proj_w': s(ks[1], (2 * D_INNER, D_MODEL), 0.02), 'conv_w': s(ks[2], (D_INNER, D_CONV), 0.2), 'conv_b': jnp.zeros((D_INNER,), jnp.float32), 'x_proj_w': s(ks[3], (DT_RANK + 2 * D_STATE, D_INNER), 0.02), 'dt_proj_w': s(ks[4], (D_INNER, DT_RANK), 0.1), 'dt_proj_b': jnp.log(jnp.expm1(jax.random.uniform(ks[5], (D_INNER,), jnp.float32, 0.001, 0.1))), 'A_log': jnp.log(jnp.broadcast_to(jnp.arange(1, D_STATE + 1, dtype=jnp.float32), (D_INNER, D_STATE))), 'D': jnp.ones((D_INNER,), jnp.float32), 'out_proj_w': s(ks[6], (D_MODEL, D_INNER), 0.02), 'res_scale': jnp.float32(0.5)}
        return inp
    _L3_attn_in = _L3_attn_setup()

    def _L3_ffn_setup():
        import jax, jax.numpy as jnp
        import numpy as np
        DIM = 128
        DEPTH = 6
        HEADS = 16
        DIM_HEAD = 64
        WINDOW = 32
        INNER = HEADS * DIM_HEAD
        DIM_INNER = int(DIM * 4 * 2 / 3)
        QK_SCALE = 8.0

        def shift_tokens(t):
            a, s = jnp.split(t, 2, -1)
            s = jnp.pad(s, ((0, 0), (1, 0), (0, 0)))[:, :-1]
            return jnp.concatenate([a, s], -1)

        def l2norm(t):
            return t / jnp.maximum(jnp.linalg.norm(t, axis=-1, keepdims=True), 1e-12)

        def rotate_half(x):
            x1, x2 = jnp.split(x, 2, -1)
            return jnp.concatenate([-x2, x1], -1)

        def rotary_tables(n):
            half = jnp.arange(0, DIM_HEAD, 2, dtype=jnp.float32)
            inv_freq = 1.0 / 10000.0 ** (half / DIM_HEAD)
            t = jnp.arange(n, dtype=jnp.float32)
            freqs = t[:, None] * inv_freq[None, :]
            freqs = jnp.concatenate([freqs, freqs], -1)
            base_scale = (half + 0.4 * DIM_HEAD) / (1.4 * DIM_HEAD)
            power = (t - n // 2) / (WINDOW // 2)
            scale = base_scale[None, :] ** power[:, None]
            scale = jnp.concatenate([scale, scale], -1)
            return (freqs, scale)

        def local_attention(q, k, v):
            b, h, n, d = q.shape
            w = WINDOW
            nw = n // w
            bq = q.reshape(b, h, nw, w, d)
            bk = k.reshape(b, h, nw, w, d)
            bv = v.reshape(b, h, nw, w, d)

            def look(t):
                p = jnp.pad(t, ((0, 0), (0, 0), (1, 0), (0, 0), (0, 0)))
                return jnp.concatenate([p[:, :, :nw], p[:, :, 1:]], axis=3)
            bk2, bv2 = (look(bk), look(bv))
            seq = jnp.arange(n).reshape(nw, w)
            seq_p = jnp.pad(seq, ((1, 0), (0, 0)), constant_values=-1)
            jt = jnp.concatenate([seq_p[:nw], seq_p[1:]], axis=1)
            it = seq[:, :, None]
            jb = jt[:, None, :]
            mask = (it < jb) | (it > jb + w) | (jb == -1)
            sim = jnp.einsum('bhwie,bhwje->bhwij', bq, bk2) * QK_SCALE
            sim = jnp.where(mask, -jnp.finfo(sim.dtype).max, sim)
            attn = jax.nn.softmax(sim, -1)
            out = jnp.einsum('bhwij,bhwje->bhwie', attn, bv2)
            return out.reshape(b, h, n, d)

        def attn_layer(x, Wqkv, qs, ksc, Wo):
            b, n, _ = x.shape
            qkv = x @ Wqkv
            q, k, v = jnp.split(qkv, 3, -1)
            sh = lambda t: t.reshape(b, n, HEADS, DIM_HEAD).transpose(0, 2, 1, 3)
            q, k, v = (sh(q), sh(k), sh(v))
            q = l2norm(q) * qs
            k = l2norm(k) * ksc
            freqs, scale = rotary_tables(n)
            cos, sin = (jnp.cos(freqs), jnp.sin(freqs))
            q = q * cos * scale + rotate_half(q) * sin * scale
            inv = 1.0 / scale
            k = k * cos * inv + rotate_half(k) * sin * inv
            out = local_attention(q, k, v)
            out = out.transpose(0, 2, 1, 3).reshape(b, n, INNER)
            return out @ Wo

        def ffn_layer(x, g, bln, W1, b1, W2, b2):
            mu = x.mean(-1, keepdims=True)
            var = ((x - mu) ** 2).mean(-1, keepdims=True)
            xn = (x - mu) / jnp.sqrt(var + 1e-05) * g + bln
            hg = xn @ W1 + b1
            a, gate = jnp.split(hg, 2, -1)
            return a * jax.nn.gelu(gate, approximate=False) @ W2 + b2
        key = jax.random.key(seed)
        ks = jax.random.split(key, 8)
        B, N = (2, 256)
        init = lambda k, shape: jax.random.normal(k, shape, jnp.float32) * 0.02
        return {'x': jax.random.normal(ks[0], (B, N, DIM), jnp.float32), 'Wqkv': init(ks[1], (DEPTH, DIM, 3 * INNER)), 'q_scale': jnp.ones((DEPTH, DIM_HEAD), jnp.float32), 'k_scale': jnp.ones((DEPTH, DIM_HEAD), jnp.float32), 'Wo': init(ks[2], (DEPTH, INNER, DIM)), 'ln_g': jnp.ones((DEPTH, DIM), jnp.float32), 'ln_b': jnp.zeros((DEPTH, DIM), jnp.float32), 'W1': init(ks[3], (DEPTH, DIM, 2 * DIM_INNER)), 'b1': jnp.zeros((DEPTH, 2 * DIM_INNER), jnp.float32), 'W2': init(ks[4], (DEPTH, DIM_INNER, DIM)), 'b2': jnp.zeros((DEPTH, DIM), jnp.float32)}
    _L3_ffn_in = _L3_ffn_setup()
    _d = {'L0_attn_x': _L0_attn_in['x'], 'L0_attn_Wq': _L0_attn_in['Wq'], 'L0_attn_bq': _L0_attn_in['bq'], 'L0_attn_Wk': _L0_attn_in['Wk'], 'L0_attn_bk': _L0_attn_in['bk'], 'L0_attn_Wv': _L0_attn_in['Wv'], 'L0_attn_bv': _L0_attn_in['bv'], 'L0_attn_Wp': _L0_attn_in['Wp'], 'L0_attn_bp': _L0_attn_in['bp'], 'L0_ffn_kernel': _L0_ffn_in['kernel'], 'L0_ffn_input_scale': _L0_ffn_in['input_scale'], 'L0_ffn_kernel_scale': _L0_ffn_in['kernel_scale'], 'L0_ffn_bias': _L0_ffn_in['bias'], 'L1_attn_Wq': _L1_attn_in['Wq'], 'L1_attn_Wk': _L1_attn_in['Wk'], 'L1_attn_Wv': _L1_attn_in['Wv'], 'L1_attn_Wo': _L1_attn_in['Wo'], 'L1_attn_norm_w': _L1_attn_in['norm_w'], 'L1_ffn_U1': _L1_ffn_in['U1'], 'L1_ffn_V1': _L1_ffn_in['V1'], 'L1_ffn_b1': _L1_ffn_in['b1'], 'L1_ffn_U2': _L1_ffn_in['U2'], 'L1_ffn_V2': _L1_ffn_in['V2'], 'L1_ffn_b2': _L1_ffn_in['b2'], 'L2_attn_Wq': _L2_attn_in['Wq'], 'L2_attn_Wk': _L2_attn_in['Wk'], 'L2_attn_Wv': _L2_attn_in['Wv'], 'L2_ffn_Wq': _L2_ffn_in['Wq'], 'L2_ffn_routers': _L2_ffn_in['routers'], 'L2_ffn_leaf_keys': _L2_ffn_in['leaf_keys'], 'L2_ffn_leaf_values': _L2_ffn_in['leaf_values'], 'L2_ffn_Wout_w': _L2_ffn_in['Wout_w'], 'L2_ffn_Wout_b': _L2_ffn_in['Wout_b'], 'L3_attn_ln_g': _L3_attn_in['ln_g'], 'L3_attn_ln_b': _L3_attn_in['ln_b'], 'L3_attn_in_proj_w': _L3_attn_in['in_proj_w'], 'L3_attn_conv_w': _L3_attn_in['conv_w'], 'L3_attn_conv_b': _L3_attn_in['conv_b'], 'L3_attn_x_proj_w': _L3_attn_in['x_proj_w'], 'L3_attn_dt_proj_w': _L3_attn_in['dt_proj_w'], 'L3_attn_dt_proj_b': _L3_attn_in['dt_proj_b'], 'L3_attn_A_log': _L3_attn_in['A_log'], 'L3_attn_D': _L3_attn_in['D'], 'L3_attn_out_proj_w': _L3_attn_in['out_proj_w'], 'L3_attn_res_scale': _L3_attn_in['res_scale'], 'L3_ffn_Wqkv': _L3_ffn_in['Wqkv'], 'L3_ffn_q_scale': _L3_ffn_in['q_scale'], 'L3_ffn_k_scale': _L3_ffn_in['k_scale'], 'L3_ffn_Wo': _L3_ffn_in['Wo'], 'L3_ffn_ln_g': _L3_ffn_in['ln_g'], 'L3_ffn_ln_b': _L3_ffn_in['ln_b'], 'L3_ffn_W1': _L3_ffn_in['W1'], 'L3_ffn_b1': _L3_ffn_in['b1'], 'L3_ffn_W2': _L3_ffn_in['W2'], 'L3_ffn_b2': _L3_ffn_in['b2']}
    _x0 = _d['L0_attn_x']
    _d['L0_attn_x'] = jax.random.normal(jax.random.fold_in(jax.random.key(seed), 1), (16, 256, 128), dtype=_x0.dtype)
    del _x0
    return _d

def reference(L0_attn_x, L0_attn_Wq, L0_attn_bq, L0_attn_Wk, L0_attn_bk, L0_attn_Wv, L0_attn_bv, L0_attn_Wp, L0_attn_bp, L0_ffn_kernel, L0_ffn_input_scale, L0_ffn_kernel_scale, L0_ffn_bias, L1_attn_Wq, L1_attn_Wk, L1_attn_Wv, L1_attn_Wo, L1_attn_norm_w, L1_ffn_U1, L1_ffn_V1, L1_ffn_b1, L1_ffn_U2, L1_ffn_V2, L1_ffn_b2, L2_attn_Wq, L2_attn_Wk, L2_attn_Wv, L2_ffn_Wq, L2_ffn_routers, L2_ffn_leaf_keys, L2_ffn_leaf_values, L2_ffn_Wout_w, L2_ffn_Wout_b, L3_attn_ln_g, L3_attn_ln_b, L3_attn_in_proj_w, L3_attn_conv_w, L3_attn_conv_b, L3_attn_x_proj_w, L3_attn_dt_proj_w, L3_attn_dt_proj_b, L3_attn_A_log, L3_attn_D, L3_attn_out_proj_w, L3_attn_res_scale, L3_ffn_Wqkv, L3_ffn_q_scale, L3_ffn_k_scale, L3_ffn_Wo, L3_ffn_ln_g, L3_ffn_ln_b, L3_ffn_W1, L3_ffn_b1, L3_ffn_W2, L3_ffn_b2):

    def _L0_attn_ref(x, Wq, bq, Wk, bk, Wv, bv, Wp, bp):
        import jax, jax.numpy as jnp
        import numpy as np
        N_EMBD = 128
        N_HEAD = 16
        B, T = (2, 256)
        b, t, c = x.shape
        hd = c // N_HEAD

        def heads(W, bias):
            return (x @ W.T + bias).reshape(b, t, N_HEAD, hd).transpose(0, 2, 1, 3)
        q, k, v = (heads(Wq, bq), heads(Wk, bk), heads(Wv, bv))
        scale = 1.0 / np.sqrt(hd)
        att = jnp.einsum('bhqd,bhkd->bhqk', q, k) * scale
        causal = jnp.tril(jnp.ones((t, t), dtype=bool))
        att = jnp.where(causal[None, None], att, -jnp.inf)
        att = jax.nn.softmax(att, axis=-1)
        y = jnp.einsum('bhqk,bhkd->bhqd', att, v)
        y = y.transpose(0, 2, 1, 3).reshape(b, t, c)
        return y @ Wp.T + bp

    def _L0_ffn_ref(x, kernel, input_scale, kernel_scale, bias):
        import jax, jax.numpy as jnp
        import numpy as np
        FEATURES = 128
        D_IN = 128

        def fp8_gemm_optimized(x, input_scale, kernel, kernel_scale):
            s_in = input_scale[0]
            s_k = kernel_scale[0]
            x_q = (x.astype(jnp.float32) / s_in).astype(jnp.float8_e4m3fn)
            k_q = (kernel.astype(jnp.float32) / s_k).astype(jnp.float8_e4m3fn)
            y = jnp.dot(x_q.astype(jnp.float32), k_q.astype(jnp.float32), preferred_element_type=jnp.float32)
            return y * (s_in * s_k)
        dtype = jnp.bfloat16
        x = x.astype(dtype)
        orig_shape = x.shape
        x2 = x.reshape(-1, x.shape[-1])
        y = fp8_gemm_optimized(x2, input_scale, kernel, kernel_scale)
        y = y.astype(dtype) + bias
        return y.reshape(orig_shape[:-1] + (FEATURES,))

    def _L1_attn_ref(hidden_states, Wq, Wk, Wv, Wo, norm_w):
        import jax, jax.numpy as jnp
        import numpy as np
        CHUNK = 64
        NORM_EPS = 1e-05
        DENOM_EPS = 1.0
        B, S, HID, H = (4, 512, 128, 8)
        D = HID // H

        def rmsnorm(x, w, eps=NORM_EPS):
            var = jnp.mean(x * x, axis=-1, keepdims=True)
            return x * jax.lax.rsqrt(var + eps) * w

        def chunked_linear_attn(q, k, v):
            b, s, h, d = q.shape
            n = s // CHUNK

            def to_chunks(x):
                return x.reshape(b, n, CHUNK, h, d).transpose(1, 0, 3, 2, 4)
            qc, kc, vc = (to_chunks(q), to_chunks(k), to_chunks(v))
            mask = jnp.tril(jnp.ones((CHUNK, CHUNK), dtype=q.dtype))

            def step(state, inp):
                qq, kk, vv = inp
                inter = jnp.einsum('bhcd,bhde->bhce', qq, state)
                scores = jnp.einsum('bhcd,bhed->bhce', qq, kk) * mask
                intra = jnp.einsum('bhce,bhed->bhcd', scores, vv)
                state = state + jnp.einsum('bhcd,bhce->bhde', kk, vv)
                return (state, inter + intra)
            init = jnp.zeros((b, h, d, d), dtype=q.dtype)
            _, o = jax.lax.scan(step, init, (qc, kc, vc))
            return o.transpose(1, 0, 3, 2, 4).reshape(b, s, h, d)
        b, s, _ = hidden_states.shape
        q = jnp.einsum('bsd,ed->bse', hidden_states, Wq).reshape(b, s, H, D)
        k = jnp.einsum('bsd,ed->bse', hidden_states, Wk).reshape(b, s, H, D)
        v = jnp.einsum('bsd,ed->bse', hidden_states, Wv).reshape(b, s, H, D)
        o = chunked_linear_attn(q, k, v)
        z = jnp.cumsum(k, axis=1)
        denom = jnp.maximum(jnp.abs(jnp.sum(q * z, axis=-1)), DENOM_EPS)[..., None]
        o = o / denom
        o = rmsnorm(o, norm_w)
        o = o.reshape(b, s, H * D)
        return jnp.einsum('bse,de->bsd', o, Wo)

    def _L1_ffn_ref(x, U1, V1, b1, U2, V2, b2):
        import jax, jax.numpy as jnp
        import numpy as np
        D_MODEL, D_FF, RANK = (128, 512, 32)
        B, S = (4, 512)
        P = jnp.einsum('bsd,dr->bsr', x, U1)
        H = jax.nn.gelu(jnp.einsum('bsr,rf->bsf', P, V1) + b1)
        Q = jnp.einsum('bsf,fr->bsr', H, U2)
        return jnp.einsum('bsr,rd->bsd', Q, V2) + b2

    def _L2_attn_ref(x, Wq, Wk, Wv):
        import jax, jax.numpy as jnp
        import numpy as np
        B, N = (2, 256)
        H, R = (8, 64)
        IN_DIM, OUT_DIM = (64, 64)
        D = IN_DIM + OUT_DIM
        INIT = 1.0
        b, n, d = x.shape
        Q = (x @ Wq.T).reshape(b, n, H, R)
        K = (x @ Wk.T).reshape(b, n, H, R)
        V = (x @ Wv.T).reshape(b, n, H, d)
        attn = jnp.einsum('bnhr,bmhr->bhnm', Q, K)
        attn = jax.nn.softmax(attn, axis=-1)
        out = jnp.einsum('bhnm,bmhd->bnd', attn, V)
        return out

    def _L2_ffn_ref(x, Wq, routers, leaf_keys, leaf_values, Wout_w, Wout_b):
        import jax, jax.numpy as jnp
        import numpy as np
        D_MODEL = 128
        DEPTH = 8
        M = 2 ** DEPTH
        N_INTERNAL = M - 1
        B, T = (8, 512)

        def _leaf_probs(gate):
            BT = gate.shape[0]
            lp = jnp.ones((BT, M), dtype=gate.dtype)
            for level in range(DEPTH):
                n = 2 ** level
                half = M // (2 * n)
                g = gate[:, n - 1:2 * n - 1]
                f = jnp.stack([1.0 - g, g], axis=-1)
                f = jnp.broadcast_to(f[..., None], (BT, n, 2, half))
                lp = lp * f.reshape(BT, M)
            return lp
        Bv, Tv, d = x.shape
        q = jnp.einsum('btd,ed->bte', x, Wq)
        q_flat = q.reshape(Bv * Tv, d)
        gate = jax.nn.sigmoid(q_flat @ routers.T)
        leaf_prob = _leaf_probs(gate)
        ret = (leaf_prob @ leaf_values).reshape(Bv, Tv, d)
        return jnp.einsum('btd,ed->bte', ret, Wout_w) + Wout_b

    def _L3_attn_ref(seq, ln_g, ln_b, in_proj_w, conv_w, conv_b, x_proj_w, dt_proj_w, dt_proj_b, A_log, D, out_proj_w, res_scale):
        import jax, jax.numpy as jnp
        import numpy as np
        D_MODEL, D_STATE, D_CONV, EXPAND = (128, 16, 4, 2)
        D_INNER = EXPAND * D_MODEL
        DT_RANK = -(-D_MODEL // 16)
        B_SZ, L_SEQ = (2, 256)

        def _silu(x):
            return x * jax.nn.sigmoid(x)

        def _mamba_block(seq, ln_g, ln_b, in_proj_w, conv_w, conv_b, x_proj_w, dt_proj_w, dt_proj_b, A_log, D, out_proj_w, res_scale):
            B, L, _ = seq.shape
            mu = jnp.mean(seq, -1, keepdims=True)
            var = jnp.mean(jnp.square(seq - mu), -1, keepdims=True)
            xn = (seq - mu) * jax.lax.rsqrt(var + 1e-05) * ln_g + ln_b
            xz = jnp.einsum('bld,ed->ble', xn, in_proj_w)
            x, z = jnp.split(xz, 2, axis=-1)
            x_pad = jnp.pad(x, ((0, 0), (D_CONV - 1, 0), (0, 0)))
            xc = conv_b
            for k in range(D_CONV):
                xc = xc + x_pad[:, k:k + L, :] * conv_w[:, k]
            x = _silu(xc)
            x_dbl = jnp.einsum('bld,ed->ble', x, x_proj_w)
            dt = jax.nn.softplus(jnp.einsum('blr,dr->bld', x_dbl[..., :DT_RANK], dt_proj_w) + dt_proj_b)
            Bm = x_dbl[..., DT_RANK:DT_RANK + D_STATE]
            Cm = x_dbl[..., DT_RANK + D_STATE:]
            A = -jnp.exp(A_log)

            def step(h, inputs):
                dt_t, B_t, C_t, x_t = inputs
                dA = jnp.exp(dt_t[..., None] * A)
                h = h * dA + (dt_t * x_t)[..., None] * B_t[:, None, :]
                y = jnp.einsum('bds,bs->bd', h, C_t)
                return (h, y)
            h0 = jnp.zeros((B, D_INNER, D_STATE), x.dtype)
            _, ys = jax.lax.scan(step, h0, (jnp.swapaxes(dt, 0, 1), jnp.swapaxes(Bm, 0, 1), jnp.swapaxes(Cm, 0, 1), jnp.swapaxes(x, 0, 1)))
            y = jnp.swapaxes(ys, 0, 1) + D * x
            y = y * _silu(z)
            out = jnp.einsum('ble,de->bld', y, out_proj_w)
            return seq + res_scale * out
        return _mamba_block(seq, ln_g, ln_b, in_proj_w, conv_w, conv_b, x_proj_w, dt_proj_w, dt_proj_b, A_log, D, out_proj_w, res_scale)

    def _L3_ffn_ref(x, Wqkv, q_scale, k_scale, Wo, ln_g, ln_b, W1, b1, W2, b2):
        import jax, jax.numpy as jnp
        import numpy as np
        DIM = 128
        DEPTH = 6
        HEADS = 16
        DIM_HEAD = 64
        WINDOW = 32
        INNER = HEADS * DIM_HEAD
        DIM_INNER = int(DIM * 4 * 2 / 3)
        QK_SCALE = 8.0

        def shift_tokens(t):
            a, s = jnp.split(t, 2, -1)
            s = jnp.pad(s, ((0, 0), (1, 0), (0, 0)))[:, :-1]
            return jnp.concatenate([a, s], -1)

        def l2norm(t):
            return t / jnp.maximum(jnp.linalg.norm(t, axis=-1, keepdims=True), 1e-12)

        def rotate_half(x):
            x1, x2 = jnp.split(x, 2, -1)
            return jnp.concatenate([-x2, x1], -1)

        def rotary_tables(n):
            half = jnp.arange(0, DIM_HEAD, 2, dtype=jnp.float32)
            inv_freq = 1.0 / 10000.0 ** (half / DIM_HEAD)
            t = jnp.arange(n, dtype=jnp.float32)
            freqs = t[:, None] * inv_freq[None, :]
            freqs = jnp.concatenate([freqs, freqs], -1)
            base_scale = (half + 0.4 * DIM_HEAD) / (1.4 * DIM_HEAD)
            power = (t - n // 2) / (WINDOW // 2)
            scale = base_scale[None, :] ** power[:, None]
            scale = jnp.concatenate([scale, scale], -1)
            return (freqs, scale)

        def local_attention(q, k, v):
            b, h, n, d = q.shape
            w = WINDOW
            nw = n // w
            bq = q.reshape(b, h, nw, w, d)
            bk = k.reshape(b, h, nw, w, d)
            bv = v.reshape(b, h, nw, w, d)

            def look(t):
                p = jnp.pad(t, ((0, 0), (0, 0), (1, 0), (0, 0), (0, 0)))
                return jnp.concatenate([p[:, :, :nw], p[:, :, 1:]], axis=3)
            bk2, bv2 = (look(bk), look(bv))
            seq = jnp.arange(n).reshape(nw, w)
            seq_p = jnp.pad(seq, ((1, 0), (0, 0)), constant_values=-1)
            jt = jnp.concatenate([seq_p[:nw], seq_p[1:]], axis=1)
            it = seq[:, :, None]
            jb = jt[:, None, :]
            mask = (it < jb) | (it > jb + w) | (jb == -1)
            sim = jnp.einsum('bhwie,bhwje->bhwij', bq, bk2) * QK_SCALE
            sim = jnp.where(mask, -jnp.finfo(sim.dtype).max, sim)
            attn = jax.nn.softmax(sim, -1)
            out = jnp.einsum('bhwij,bhwje->bhwie', attn, bv2)
            return out.reshape(b, h, n, d)

        def attn_layer(x, Wqkv, qs, ksc, Wo):
            b, n, _ = x.shape
            qkv = x @ Wqkv
            q, k, v = jnp.split(qkv, 3, -1)
            sh = lambda t: t.reshape(b, n, HEADS, DIM_HEAD).transpose(0, 2, 1, 3)
            q, k, v = (sh(q), sh(k), sh(v))
            q = l2norm(q) * qs
            k = l2norm(k) * ksc
            freqs, scale = rotary_tables(n)
            cos, sin = (jnp.cos(freqs), jnp.sin(freqs))
            q = q * cos * scale + rotate_half(q) * sin * scale
            inv = 1.0 / scale
            k = k * cos * inv + rotate_half(k) * sin * inv
            out = local_attention(q, k, v)
            out = out.transpose(0, 2, 1, 3).reshape(b, n, INNER)
            return out @ Wo

        def ffn_layer(x, g, bln, W1, b1, W2, b2):
            mu = x.mean(-1, keepdims=True)
            var = ((x - mu) ** 2).mean(-1, keepdims=True)
            xn = (x - mu) / jnp.sqrt(var + 1e-05) * g + bln
            hg = xn @ W1 + b1
            a, gate = jnp.split(hg, 2, -1)
            return a * jax.nn.gelu(gate, approximate=False) @ W2 + b2
        for i in range(DEPTH):
            x = attn_layer(shift_tokens(x), Wqkv[i], q_scale[i], k_scale[i], Wo[i]) + x
            x = ffn_layer(shift_tokens(x), ln_g[i], ln_b[i], W1[i], b1[i], W2[i], b2[i]) + x
        return x
    x = L0_attn_x
    xn = _layernorm(x, axis=-1)
    x = x + _L0_attn_ref(xn, L0_attn_Wq, L0_attn_bq, L0_attn_Wk, L0_attn_bk, L0_attn_Wv, L0_attn_bv, L0_attn_Wp, L0_attn_bp) + _L0_ffn_ref(xn, L0_ffn_kernel, L0_ffn_input_scale, L0_ffn_kernel_scale, L0_ffn_bias)
    xn = _layernorm(x, axis=-1)
    x = x + _L1_attn_ref(xn, L1_attn_Wq, L1_attn_Wk, L1_attn_Wv, L1_attn_Wo, L1_attn_norm_w) + _L1_ffn_ref(xn, L1_ffn_U1, L1_ffn_V1, L1_ffn_b1, L1_ffn_U2, L1_ffn_V2, L1_ffn_b2)
    xn = _layernorm(x, axis=-1)
    x = x + _L2_attn_ref(xn, L2_attn_Wq, L2_attn_Wk, L2_attn_Wv) + _L2_ffn_ref(xn, L2_ffn_Wq, L2_ffn_routers, L2_ffn_leaf_keys, L2_ffn_leaf_values, L2_ffn_Wout_w, L2_ffn_Wout_b)
    xn = _layernorm(x, axis=-1)
    x = x + _L3_attn_ref(xn, L3_attn_ln_g, L3_attn_ln_b, L3_attn_in_proj_w, L3_attn_conv_w, L3_attn_conv_b, L3_attn_x_proj_w, L3_attn_dt_proj_w, L3_attn_dt_proj_b, L3_attn_A_log, L3_attn_D, L3_attn_out_proj_w, L3_attn_res_scale) + _L3_ffn_ref(xn, L3_ffn_Wqkv, L3_ffn_q_scale, L3_ffn_k_scale, L3_ffn_Wo, L3_ffn_ln_g, L3_ffn_ln_b, L3_ffn_W1, L3_ffn_b1, L3_ffn_W2, L3_ffn_b2)
    return x

_drawn_inputs = setup_inputs


def setup_inputs(seed=0):
    import zlib

    import numpy as np

    out = dict(_drawn_inputs(seed))
    spreads = {'L0_ffn_bias': (0.0, 0.1),
     'L1_attn_norm_w': (1.0, 0.2),
     'L1_ffn_b1': (0.0, 0.1),
     'L1_ffn_b2': (0.0, 0.1),
     'L3_attn_ln_g': (1.0, 0.2),
     'L3_attn_ln_b': (0.0, 0.1),
     'L3_attn_conv_b': (0.0, 0.1),
     'L3_attn_D': (1.0, 0.2),
     'L3_ffn_q_scale': (1.0, 0.2),
     'L3_ffn_k_scale': (1.0, 0.2),
     'L3_ffn_ln_g': (1.0, 0.2),
     'L3_ffn_ln_b': (0.0, 0.1),
     'L3_ffn_b1': (0.0, 0.1),
     'L3_ffn_b2': (0.0, 0.1)}
    factors = {}
    for name, (base, spread) in spreads.items():
        noise = np.random.default_rng([zlib.crc32(name.encode()), seed]).standard_normal(out[name].shape)
        drawn = base * np.exp(spread * noise) if base else spread * noise
        out[name] = jnp.asarray(drawn.astype(out[name].dtype))
    for name, factor in factors.items():
        out[name] = (out[name] * factor).astype(out[name].dtype)
    return out
```

```python
import numpy as np
import concourse.bass as bass
from concourse import mybir
from contextlib import ExitStack

F32 = mybir.dt.float32
BF16 = mybir.dt.bfloat16
I32 = mybir.dt.int32
ALU = mybir.AluOpType
ACT = mybir.ActivationFunctionType
AX = mybir.AxisListType

P = 128
NSEQ, SEQ = 16, 256
TILES = SEQ // P
NT = NSEQ * TILES
EPS = 1e-5
NEG = -1e30


class Stage:

    def __init__(self, nc, sems, dma_sems):
        self.nc, self.sems, self.dma_sems = nc, sems, dma_sems
        self.steps, self.mark, self.count = [], {}, {}

    def step(self, eng, name, fn, after=(), prev=(), dmas=0, dma="load", solo=False):
        assert name not in self.mark, name
        key, inc = (dma, 16 * dmas) if dmas else (eng, 1)
        self.count[key] = self.count.get(key, 0) + inc
        self.mark[name] = (key, self.count[key])
        self.steps.append((eng, name, fn, tuple(after), tuple(prev), bool(dmas), solo))

    def sem(self, key):
        return self.sems[key] if key in self.sems else self.dma_sems[key]

    def run(self, turns=1):
        nc = self.nc
        engines = {"pe": nc.tensor, "dve": nc.vector, "act": nc.scalar, "pool": nc.gpsimd, "sp": nc.sync}
        self.engines = engines
        if turns == 1:
            self._write(None)
        else:
            for key, n in self.count.items():
                (engines[key] if key in engines else nc.sync).sem_inc(self.sem(key), n)
            with nc.Fori(0, turns) as turn:
                self._write(turn)
        for key, n in self.count.items():
            if key not in engines:
                nc.sync.wait_ge(self.sem(key), n * (turns + (turns > 1)))
        nc.all_engine_barrier()
        for key in self.count:
            nc.sync.sem_clear(self.sem(key))
        nc.all_engine_barrier()

    def _write(self, turn):
        seen = {}
        for eng, name, fn, after, prev, is_dma, solo in self.steps:
            e = self.engines[eng]
            need = {}
            for n in after:
                key, v = self.mark[n]
                need[key] = max(need.get(key, -1 << 30), v)
            if turn is not None:
                for n in prev:
                    key, v = self.mark[n]
                    need[key] = max(need.get(key, -1 << 30), v - self.count[key])
            waited = False
            for key, v in need.items():
                if seen.get((eng, key), -1 << 30) >= v:
                    continue
                seen[(eng, key)] = v
                n = self.count[key]
                e.wait_ge(self.sem(key), v if turn is None else turn * n + (v + n))
                waited = True
            if waited and solo and turn is not None:
                e.sem_inc(self.sems["spare_" + eng], 1)
            out = fn(turn)
            if is_dma:
                for d in out:
                    d.then_inc(self.sem(self.mark[name][0]), 16)
            else:
                out.then_inc(self.sems[eng], 1)


def seq_tiles(ap, i):
    return ap[:, bass.ds(i * TILES, TILES), :]


def row(ap, n):
    return ap.rearrange("(a n) -> a n", a=1).broadcast_to((P, n))


class Kernel:
    def __init__(self, nc, d, out, stages):
        self.nc, self.d, self.out, self.stages = nc, d, out, stages

    def sb(self, name, shape, dt=F32):
        return self.ctx.enter_context(self.nc.sbuf_tensor(f"{self.tag}_{name}", shape, dt))

    def stage(self):
        return Stage(self.nc, self.sems, self.dma_sems)

    def build(self):
        nc, d = self.nc, self.d
        with ExitStack() as ctx:
            self.ctx, self.tag = ctx, "all"
            self.sems = {k: ctx.enter_context(nc.semaphore(f"done_{k}")) for k in ("pe", "dve", "act", "pool")}
            for k in ("pe", "dve", "act", "pool"):
                self.sems["spare_" + k] = ctx.enter_context(nc.semaphore(f"spare_{k}"))
            self.dma_sems = {k: ctx.enter_context(nc.semaphore(f"dma_{k}"))
                             for k in ("load", "vlow", "vhigh", "store", "w_attn", "w_ffn")}
            self.X = self.sb("x", [P, NT, P])
            self.Z = self.sb("z", [P, NT, P])
            self.ident = self.sb("ident", [P, P])
            self.identb = self.sb("identb", [P, P], BF16)
            self.PS = ctx.enter_context(nc.psum_tensor("ps", [P, 8, 512], F32))
            self.eps = self.sb("eps", [P, 1])
            s = self.stage()
            s.step("sp", "x", lambda i: [nc.sync.dma_start(self.X[:, :, :], d["L0_attn_x"].rearrange("b (t p) d -> p (b t) d", p=P))], dmas=1)
            s.step("sp", "ident", lambda i: [nc.sync.dma_start(self.ident[:, :], d["c_ident"])], dmas=1, dma="store")
            s.step("dve", "identb", lambda i: nc.vector.tensor_copy(self.identb[:, :], self.ident[:, :]), after=["ident"])
            s.step("dve", "eps", lambda i: nc.vector.memset(self.eps[:, :], EPS))
            s.run()
            for k in self.stages:
                with ExitStack() as self.ctx:
                    self.tag = k
                    {"L0": self.L0, "L1": self.L1, "L2": self.L2, "L3a": self.L3a, "L3f": self.L3f}[k]()
            s = self.stage()
            res = self.Z if "L3f" in self.stages else self.X
            s.step("sp", "out", lambda i: [nc.sync.dma_start(self.out.rearrange("b (t p) d -> p (b t) d", p=P), res[:, :, :])], dmas=1, dma="store")
            s.run()

    def layernorm(self, s, src, dst, name, after, prev=(), wprev=()):
        nc = self.nc
        st, mv, ls, rs = (self.sb(f"{name}_{n}", [P, TILES, w]) for n, w in (("st", 6), ("mv", 2), ("ls", 1), ("rs", 1)))
        for t in range(TILES):
            s.step("dve", f"{name}_st{t}", lambda i, t=t: nc.vector.bn_stats(st[:, t, :], src[:, t, :]),
                   after=after, prev=[f"{name}_mv{t}"])
            s.step("dve", f"{name}_mv{t}", lambda i, t=t: nc.vector.bn_aggr(mv[:, t, :], st[:, t, :]),
                   after=[f"{name}_st{t}"], prev=[f"{name}_out{t}"], solo=True)
        s.step("act", f"{name}_ln", lambda i: nc.scalar.activation(ls[:, :, 0], mv[:, :, 1], ACT.Ln, bias=self.eps[:, :]),
               after=[f"{name}_mv1"], prev=[f"{name}_rs"])
        s.step("act", f"{name}_rs", lambda i: nc.scalar.activation(rs[:, :, 0], ls[:, :, 0], ACT.Exp, scale=-0.5),
               after=[f"{name}_ln"], prev=["%s_out%d" % (name, TILES - 1)])
        for t in range(TILES):
            s.step("dve", f"{name}_out{t}", lambda i, t=t: nc.vector.tensor_scalar(
                dst[:, t, :], src[:, t, :], mv[:, t, 0:1], rs[:, t, :], ALU.subtract, ALU.mult),
                after=[f"{name}_rs"], prev=wprev)

    def L0(self):
        nc, d, PS, X = self.nc, self.d, self.PS, self.X
        H, HD = 16, 8
        G = 4
        wt = self.sb("wt", [P, 4, P])
        bqk = self.sb("bqk", [P, 2])
        bvp = self.sb("bvp", [P, 2, P])
        hmask = self.sb("hmask", [P, H])
        cmask = self.sb("cmask", [P, P])
        cmaskb = self.sb("cmaskb", [P, P], BF16)
        kb = self.sb("kb", [P, P], BF16)
        kf = self.sb("kf", [P, P])
        sc = self.sb("sc", [P, 2])
        rsc = self.sb("rsc", [P, 2])
        ssc = self.sb("ssc", [P, 1])
        fbias = self.sb("fbias", [P, P], BF16)
        kq = self.sb("kq", [P, P], BF16)
        vaug = self.sb("vaug", [P, TILES, H, HD + 1])
        qz = [self.sb(f"qz_{n}", [P, SEQ]) for n in ("p", "m", "r", "w")]

        def quantise(s, name, src, dst, w, scal, after, prev=(), first=None):
            xs, mg, r, t2 = (q[:, 0:w] for q in qz)
            s.step("dve", name + "0", lambda i: nc.vector.tensor_scalar(xs, src, scal, None, ALU.mult), after=after, prev=prev)
            s.step("dve", name + "1", lambda i: nc.vector.tensor_scalar(
                mg.bitcast(I32), xs.bitcast(I32), 0x7F800000, None, ALU.bitwise_and), after=[name + "0"])
            s.step("dve", name + "2", lambda i: nc.vector.tensor_scalar(
                mg, mg, 2.0 ** -6, 1.5 * 2.0 ** 20, ALU.max, ALU.mult), after=[name + "1"])
            s.step("dve", name + "3", lambda i: nc.vector.tensor_tensor(r, xs, mg, ALU.add), after=[name + "2"])
            s.step("dve", name + "4", lambda i: nc.vector.tensor_tensor(r, r, mg, ALU.subtract), after=[name + "3"])
            s.step("dve", name + "5", lambda i: nc.vector.tensor_tensor(t2, r, r, ALU.mult), after=[name + "4"])
            s.step("dve", name + "6", lambda i: nc.vector.tensor_scalar(
                t2, t2, 448.0 ** 2, -(448.0 ** 2), ALU.max, ALU.add), after=[name + "5"])
            s.step("dve", name + "7", lambda i: nc.vector.tensor_scalar(t2, t2, 2.0 ** 127, None, ALU.mult), after=[name + "6"])
            s.step("dve", name + "8", lambda i: nc.vector.tensor_tensor(t2, t2, t2, ALU.subtract), after=[name + "7"])
            s.step("dve", name + "9", lambda i: nc.vector.tensor_tensor(dst, r, t2, ALU.add), after=[name + "8"])

        s = self.stage()
        s.step("sp", "in", lambda i: [nc.sync.dma_start(wt[:, n, :], d["L0_attn_" + w + "_T"]) for n, w in enumerate(("Wq", "Wk", "Wv", "Wp"))]
               + [nc.sync.dma_start(bqk[:, n:n + 1], d["L0_attn_" + w].rearrange("(p a) -> p a", a=1)) for n, w in enumerate(("bq", "bk"))]
               + [nc.sync.dma_start(bvp[:, n, :], row(d["L0_attn_" + w], P)) for n, w in enumerate(("bv", "bp"))]
               + [nc.sync.dma_start(hmask[:, :], d["c_head16"]), nc.sync.dma_start(cmask[:, :], d["c_causal"]),
                  nc.sync.dma_start(kb[:, :], d["L0_ffn_kernel"]), nc.sync.dma_start(fbias[:, :], row(d["L0_ffn_bias"], P)),
                  nc.sync.dma_start(sc[:, 0:1], row(d["L0_ffn_input_scale"], 1)),
                  nc.sync.dma_start(sc[:, 1:2], row(d["L0_ffn_kernel_scale"], 1))], dmas=14)
        s.step("dve", "cmaskb", lambda i: nc.vector.tensor_copy(cmaskb[:, :], cmask[:, :]), after=["in"])
        s.step("dve", "kf", lambda i: nc.vector.tensor_copy(kf[:, :], kb[:, :]), after=["in"])
        s.step("dve", "rsc", lambda i: nc.vector.reciprocal(rsc[:, :], sc[:, :]), after=["in"])
        s.step("dve", "ssc", lambda i: nc.vector.tensor_tensor(ssc[:, :], sc[:, 0:1], sc[:, 1:2], ALU.mult), after=["in"])
        quantise(s, "kq", kf[:, :], kq[:, :], P, rsc[:, 1:2], ["kf", "rsc"])
        s.step("pool", "ones", lambda i: nc.gpsimd.memset(vaug[:, :, :, HD], 1.0))
        s.run()

        xs = self.sb("xs", [P, TILES, P])
        xn = self.sb("xn", [P, TILES, P])
        xnT = self.sb("xnT", [P, SEQ])
        xb = self.sb("xb", [P, SEQ], BF16)
        xq = self.sb("xq", [P, SEQ], BF16)
        yb = self.sb("yb", [P, TILES, P], BF16)
        qT = self.sb("qT", [P, SEQ])
        kT = self.sb("kT", [P, SEQ])
        qm = self.sb("qm", [P, H, SEQ])
        sm = self.sb("sm", [P, 2, G * SEQ])
        pT = self.sb("pT", [P, 2, G * SEQ])
        mx = self.sb("mx", [P, 2, G])
        ob = self.sb("ob", [P, TILES, H, HD])
        rl = self.sb("rl", [P, TILES, H])
        oT = self.sb("oT", [P, SEQ])

        s = self.stage()
        s.step("dve", "xs", lambda i: nc.vector.tensor_scalar(xs[:, :, :], seq_tiles(X, i), 1.0, None, ALU.mult), prev=["x_out"])
        self.layernorm(s, xs, xn, "ln", ["xs"], wprev=["xnT_pe"])
        s.step("pe", "xnT_pe", lambda i: [nc.tensor.transpose(PS[:, 4, t * P:t * P + P], xn[:, t, :], self.ident[:, :]) for t in range(TILES)][-1],
               after=["ln_out1"], prev=["oT"])
        s.step("act", "xnT", lambda i: nc.scalar.activation(xnT[:, :], PS[:, 4, 0:SEQ], ACT.Copy), after=["xnT_pe"], prev=["v_pe", "xb"])
        for n, (w, to, b) in enumerate((("q", qT, 0), ("k", kT, 1))):
            s.step("pe", w + "_pe", lambda i, n=n, b=b: nc.tensor.matmul(PS[:, b, 0:SEQ], wt[:, n, :], xnT[:, :], start=True, stop=True),
                   after=["xnT"], prev=["s_sub%d" % (2 * H // G - 2)])
            s.step("act", w, lambda i, n=n, to=to, b=b: nc.scalar.activation(to[:, :], PS[:, b, 0:SEQ], ACT.Identity, bias=bqk[:, n:n + 1]),
                   after=[w + "_pe"], prev=["qm15", "s_pe%d" % (2 * H // G - 1)])
        s.step("pe", "v_pe", lambda i: [nc.tensor.matmul(PS[:, 5, t * P:t * P + P], xnT[:, t * P:t * P + P], wt[:, 2, :], start=True, stop=True)
                                        for t in range(TILES)][-1], after=["xnT"], prev=["x_out"])
        for t in range(TILES):
            s.step("dve", f"v{t}", lambda i, t=t: nc.vector.tensor_tensor(
                vaug[:, t, :, 0:HD], PS[:, 5, t * P:t * P + P].rearrange("p (h e) -> p h e", e=HD),
                bvp[:, 0, :].rearrange("p (h e) -> p h e", e=HD), ALU.add), after=["v_pe"], prev=["o_pe%d" % (2 * H // G - 1)])
        for h in range(H):
            s.step("dve", f"qm{h}", lambda i, h=h: nc.vector.tensor_scalar(qm[:, h, :], qT[:, :], hmask[:, h:h + 1], None, ALU.mult),
                   after=["q"], prev=["s_pe%d" % (2 * H // G - 1)])

        units = [(qt, g) for g in range(H // G) for qt in range(TILES)]

        def view(t, qt):
            return t[:, 0:G * P * (qt + 1)].rearrange("p (h k) -> p h k", h=G)

        def bank(u, qt):
            b = 2 * (u % 2)
            return PS[:, b:b + 2, :].rearrange("p b k -> p (b k)") if qt else PS[:, b, :]

        def scores(u, qt, g):
            n = P * (qt + 1)

            def go(i):
                for h in range(G):
                    o = bank(u, qt)[:, h * n:h * n + n]
                    nc.tensor.matmul(o, qm[:, g * G + h, qt * P:qt * P + P], kT[:, 0:n], start=True, stop=False)
                    mm = nc.tensor.matmul(o[:, n - P:n], self.identb[:, :], cmaskb[:, :], start=False, stop=True)
                return mm
            s.step("pe", f"s_pe{u}", go, after=["k", f"qm{g * G + G - 1}"] + ([f"s_sub{u - 2}"] if u >= 2 else []) + ["q", "k"])

        def softmax(u, qt):
            n = P * (qt + 1)
            a = u % 2
            src = view(bank(u, qt), qt)
            sv = view(sm[:, a, :], qt)
            s.step("dve", f"s_max{u}", lambda i: nc.vector.tensor_reduce(mx[:, a, :], src, AX.X, ALU.max),
                   after=[f"s_pe{u}"] + ([f"s_sub{u - 2}"] if u >= 2 else []), prev=[f"s_sub{len(units) - 2 + a}"])
            s.step("dve", f"s_sub{u}", lambda i: nc.vector.tensor_tensor(
                sv, src, mx[:, a, :].unsqueeze(2).broadcast_to((P, G, n)), ALU.subtract),
                after=[f"s_max{u}"] + ([f"t_pe{u - 2}"] if u >= 2 else []), prev=[f"t_pe{len(units) - 2 + a}"])
            s.step("act", f"s_exp{u}", lambda i: nc.scalar.activation(
                sm[:, a, 0:G * n], sm[:, a, 0:G * n], ACT.Exp, scale=float(HD) ** -0.5), after=[f"s_sub{u}"])

        def turn(u, qt):
            n = P * (qt + 1)
            a = u % 2

            def go(i):
                for h in range(G):
                    for k in range(qt + 1):
                        c = h * (qt + 1) + k
                        mm = nc.tensor.transpose(PS[:, 4 + c // 4, (c % 4) * P:(c % 4 + 1) * P],
                                                 sm[:, a, h * n + k * P:h * n + k * P + P], self.ident[:, :])
                return mm
            s.step("pe", f"t_pe{u}", go, after=[f"s_exp{u}"] + ([f"t{u - 1}"] if u else ["v1", "xnT"]))
            s.step("act", f"t{u}", lambda i: nc.scalar.activation(
                pT[:, a, 0:G * n], PS[:, 4:6, :].rearrange("p b k -> p (b k)")[:, 0:G * n], ACT.Copy),
                after=[f"t_pe{u}"] + ([f"o_pe{u - 2}"] if u >= 2 else []), prev=[f"o_pe{len(units) - 2 + a}"])

        def output(u, qt, g):
            def go(i):
                for h in range(G):
                    hh = g * G + h
                    for k in range(qt + 1):
                        c = h * (qt + 1) + k
                        mm = nc.tensor.matmul(PS[:, 6 + qt, hh * (HD + 1):(hh + 1) * (HD + 1)], pT[:, u % 2, c * P:c * P + P],
                                              vaug[:, k, hh, :], start=(k == 0), stop=(k == qt))
                return mm
            s.step("pe", f"o_pe{u}", go, after=[f"t{u}", "v1"], prev=["ob1"])

        for n in range(len(units) + 2):
            if n < len(units):
                scores(n, *units[n])
                softmax(n, units[n][0])
            if 1 <= n <= len(units):
                turn(n - 1, units[n - 1][0])
            if n >= 2:
                output(n - 2, *units[n - 2])
        last = len(units) - 1
        s.step("dve", "xb", lambda i: nc.vector.tensor_copy(xb[:, :], xnT[:, :]), after=["xnT"], prev=["xq0"])
        quantise(s, "xq", xb[:, :], xq[:, :], SEQ, rsc[:, 0:1], ["xb"], prev=["y_pe"])
        for t in range(TILES):
            o = PS[:, 6 + t, 0:H * (HD + 1)].rearrange("p (h e) -> p h e", e=HD + 1)
            s.step("dve", f"rl{t}", lambda i, t=t, o=o: nc.vector.reciprocal(rl[:, t, :], o[:, :, HD]),
                   after=[f"o_pe{last}"], prev=[f"ob{t}"])
            s.step("dve", f"ob{t}", lambda i, t=t, o=o: nc.vector.tensor_tensor(
                ob[:, t, :, :], o[:, :, 0:HD], rl[:, t, :].unsqueeze(2).broadcast_to((P, H, HD)), ALU.mult),
                after=[f"rl{t}"], prev=["oT_pe"])
        s.step("pe", "oT_pe", lambda i: [nc.tensor.transpose(PS[:, 4, t * P:t * P + P], ob[:, t, :, :].rearrange("p h e -> p (h e)"),
                                                             self.ident[:, :]) for t in range(TILES)][-1], after=["ob1", f"t{last}"])
        s.step("act", "oT", lambda i: nc.scalar.activation(oT[:, :], PS[:, 4, 0:SEQ], ACT.Copy), after=["oT_pe"], prev=["p_pe"])
        s.step("pe", "p_pe", lambda i: [nc.tensor.matmul(PS[:, 5, t * P:t * P + P], oT[:, t * P:t * P + P], wt[:, 3, :], start=True, stop=True)
                                        for t in range(TILES)][-1], after=["oT", f"t{last}"])
        s.step("pe", "y_pe", lambda i: [nc.tensor.matmul(PS[:, 2, t * P:t * P + P], xq[:, t * P:t * P + P], kq[:, :], start=True, stop=True)
                                        for t in range(TILES)][-1], after=["xq9", f"s_sub{last}"])
        s.step("dve", "y0", lambda i: nc.vector.tensor_scalar(yb[:, :, :].rearrange("p t d -> p (t d)"), PS[:, 2, 0:SEQ], ssc[:, :], None, ALU.mult), after=["y_pe"])
        s.step("dve", "y1", lambda i: nc.vector.tensor_tensor(yb[:, :, :], yb[:, :, :], fbias[:, :].unsqueeze(1).broadcast_to((P, TILES, P)), ALU.add), after=["y0"])
        s.step("dve", "x1", lambda i: nc.vector.tensor_tensor(xs[:, :, :], xs[:, :, :], yb[:, :, :], ALU.add), after=["y1"])
        s.step("dve", "x2", lambda i: nc.vector.tensor_tensor(xs[:, :, :], xs[:, :, :], bvp[:, 1, :].unsqueeze(1).broadcast_to((P, TILES, P)), ALU.add), after=["x1"])
        s.step("dve", "x_out", lambda i: nc.vector.tensor_tensor(seq_tiles(X, i), xs[:, :, :], PS[:, 5, 0:SEQ].rearrange("p (t d) -> p t d", t=TILES), ALU.add),
               after=["x2", "p_pe"])
        s.run(NSEQ)

    def L1(self):
        nc, d, PS, X = self.nc, self.d, self.PS, self.X
        H, HD = 8, 16
        FF, RANK = 512, 32
        FC = FF // P
        NB = 3
        wt = self.sb("wt", [P, 4, P])
        hmask = self.sb("hmask", [P, H])
        keep = self.sb("keep", [P, P])
        nw = self.sb("nw", [P, HD])
        u1 = self.sb("u1", [P, RANK])
        v1 = self.sb("v1", [RANK, FF])
        b1 = self.sb("b1", [P, FC])
        u2 = self.sb("u2", [P, FC, RANK])
        v2 = self.sb("v2", [RANK, P])
        b2 = self.sb("b2", [P, P])
        vaug = self.sb("vaug", [P, TILES, H, HD + 1])
        s = self.stage()
        s.step("sp", "in", lambda i: [nc.sync.dma_start(wt[:, n, :], d["L1_attn_" + w + "_T"]) for n, w in enumerate(("Wq", "Wk", "Wv", "Wo"))]
               + [nc.sync.dma_start(hmask[:, :], d["c_head8"]), nc.sync.dma_start(keep[:, :], d["c_causal01"]),
                  nc.sync.dma_start(nw[:, :], row(d["L1_attn_norm_w"], HD)), nc.sync.dma_start(u1[:, :], d["L1_ffn_U1"]),
                  nc.sync.dma_start(v1[:, :], d["L1_ffn_V1"]), nc.sync.dma_start(b1[:, :], d["L1_ffn_b1_T"]),
                  nc.sync.dma_start(u2[:, :, :], d["L1_ffn_U2"].rearrange("(c p) r -> p c r", p=P)),
                  nc.sync.dma_start(v2[:, :], d["L1_ffn_V2"]), nc.sync.dma_start(b2[:, :], row(d["L1_ffn_b2"], P))], dmas=13)
        s.step("pool", "ones", lambda i: nc.gpsimd.memset(vaug[:, :, :, HD], 1.0))
        s.run()

        xs = self.sb("xs", [P, TILES, P])
        xn = self.sb("xn", [P, TILES, P])
        xnT = self.sb("xnT", [P, SEQ])
        qT = self.sb("qT", [P, SEQ])
        kT = self.sb("kT", [P, SEQ])
        qm = self.sb("qm", [P, H, SEQ])
        sT = self.sb("sT", [P, H, NB, P])
        dn = self.sb("dn", [P, TILES, H])
        dr = self.sb("dr", [P, TILES, H])
        o1 = self.sb("o1", [P, TILES, H, HD])
        sq = self.sb("sq", [P, TILES, H, HD])
        ms = self.sb("ms", [P, TILES, H])
        oT = self.sb("oT", [P, SEQ])
        pr = self.sb("pr", [RANK, SEQ])
        hT = self.sb("hT", [P, FC, SEQ])
        qr = self.sb("qr", [RANK, SEQ])

        s = self.stage()
        s.step("dve", "xs", lambda i: nc.vector.tensor_scalar(xs[:, :, :], seq_tiles(X, i), 1.0, None, ALU.mult), prev=["x_out"])
        self.layernorm(s, xs, xn, "ln", ["xs"], wprev=["xnT_pe"])
        s.step("pe", "xnT_pe", lambda i: [nc.tensor.transpose(PS[:, 4, t * P:t * P + P], xn[:, t, :], self.ident[:, :]) for t in range(TILES)][-1],
               after=["ln_out1"], prev=["oT"])
        s.step("act", "xnT", lambda i: nc.scalar.activation(xnT[:, :], PS[:, 4, 0:SEQ], ACT.Copy), after=["xnT_pe"], prev=["v_pe", "pr_pe"])
        for n, (w, to) in enumerate((("q", qT), ("k", kT))):
            s.step("pe", w + "_pe", lambda i, n=n: nc.tensor.matmul(PS[:, 5, n * SEQ:(n + 1) * SEQ], wt[:, n, :], xnT[:, :], start=True, stop=True),
                   after=["xnT"], prev=["x_out"] if n == 0 else [])
            s.step("act", w, lambda i, n=n, to=to: nc.scalar.activation(to[:, :], PS[:, 5, n * SEQ:(n + 1) * SEQ], ACT.Copy),
                   after=["q_pe", "k_pe"], prev=["qm7", f"s_pe{H - 1}"])
        s.step("pe", "v_pe", lambda i: [nc.tensor.matmul(PS[:, 6, t * P:t * P + P], xnT[:, t * P:t * P + P], wt[:, 2, :], start=True, stop=True)
                                        for t in range(TILES)][-1], after=["xnT"], prev=["o1_1"])
        s.step("dve", "v", lambda i: nc.vector.tensor_copy(
            vaug[:, :, :, 0:HD], PS[:, 6, 0:SEQ].rearrange("p (t h e) -> p t h e", t=TILES, e=HD)), after=["v_pe"], prev=["o_pe"])
        for h in range(H):
            s.step("dve", f"qm{h}", lambda i, h=h: nc.vector.tensor_scalar(qm[:, h, :], qT[:, :], hmask[:, h:h + 1], None, ALU.mult),
                   after=["q"], prev=[f"s_pe{h}"])
        for h in range(H):
            b = h % 4

            def scores(i, h=h, b=b):
                nc.tensor.matmul(PS[:, b, 0:SEQ], kT[:, 0:P], qm[:, h, :], start=True, stop=True)
                return nc.tensor.matmul(PS[:, b, SEQ:SEQ + P], kT[:, P:SEQ], qm[:, h, P:SEQ], start=True, stop=True)
            s.step("pe", f"s_pe{h}", scores, after=["k", f"qm{h}"] + ([f"sd{h - 4}", f"sf{h - 4}"] if h >= 4 else []),
                   prev=[f"sd{h + 4}", f"sf{h + 4}", "pr", "gelu3"] if h < 4 else [])
            s.step("dve", f"sd{h}", lambda i, h=h, b=b: nc.vector.tensor_tensor(
                sT[:, h, 0:NB:2, :], PS[:, b, 0:NB * P].rearrange("p (n q) -> p n q", q=P)[:, 0:NB:2, :],
                keep[:, :].unsqueeze(1).broadcast_to((P, 2, P)), ALU.mult), after=[f"s_pe{h}"], prev=["o_pe"])
            s.step("act", f"sf{h}", lambda i, h=h, b=b: nc.scalar.activation(sT[:, h, 1, :], PS[:, b, P:SEQ], ACT.Copy),
                   after=[f"sd{h}"], prev=["o_pe"])

        def out(i):
            for t in range(TILES):
                for h in range(H):
                    o = PS[:, 6 + t, h * (HD + 1):(h + 1) * (HD + 1)]
                    if t == 0:
                        mm = nc.tensor.matmul(o, sT[:, h, 0, :], vaug[:, 0, h, :], start=True, stop=True)
                    else:
                        nc.tensor.matmul(o, sT[:, h, 1, :], vaug[:, 0, h, :], start=True, stop=False)
                        mm = nc.tensor.matmul(o, sT[:, h, 2, :], vaug[:, 1, h, :], start=False, stop=True)
            return mm
        s.step("pe", "o_pe", out, after=["v"] + [f"{x}{h}" for x in ("sd", "sf") for h in range(H)], prev=["o1_1"])
        s.step("pe", "pr_pe", lambda i: nc.tensor.matmul(PS[0:RANK, 0, 0:SEQ], u1[:, :], xnT[:, :], start=True, stop=True), after=["xnT", "sd4", "sf4"])
        s.step("dve", "pr", lambda i: nc.vector.tensor_copy(pr[:, :], PS[0:RANK, 0, 0:SEQ]), after=["pr_pe"], prev=["h_pe3"])
        for c in range(FC):
            s.step("pe", f"h_pe{c}", lambda i, c=c: nc.tensor.matmul(PS[:, (1, 2, 3, 0)[c], 0:SEQ], v1[:, c * P:c * P + P], pr[:, :], start=True, stop=True),
                   after=["pr", "sd7", "sf7", "sd6", "sf6", "sd5", "sf5"])
        for t in range(TILES):
            o = PS[:, 6 + t, 0:H * (HD + 1)].rearrange("p (h e) -> p h e", e=HD + 1)
            s.step("dve", f"dr{t}", lambda i, t=t, o=o: nc.vector.tensor_copy(dr[:, t, :], o[:, :, HD]), after=["o_pe"], prev=[f"dn{t}"])
            s.step("dve", f"dn{t}", lambda i, t=t: nc.vector.scalar_tensor_tensor(dn[:, t, :], dr[:, t, :], -1.0, dr[:, t, :], ALU.mult, ALU.max),
                   after=[f"dr{t}"], prev=["o1_1"])
        s.step("dve", "dm", lambda i: nc.vector.tensor_scalar(dn[:, :, :], dn[:, :, :], 1.0, None, ALU.max), after=["dn0", "dn1"])
        s.step("dve", "di", lambda i: nc.vector.reciprocal(dn[:, :, :], dn[:, :, :]), after=["dm"])
        for t in range(TILES):
            o = PS[:, 6 + t, 0:H * (HD + 1)].rearrange("p (h e) -> p h e", e=HD + 1)
            s.step("dve", f"o1_{t}", lambda i, t=t, o=o: nc.vector.tensor_tensor(
                o1[:, t, :, :], o[:, :, 0:HD], dn[:, t, :].unsqueeze(2).broadcast_to((P, H, HD)), ALU.mult), after=["di"], prev=["oT_pe"])
        s.step("dve", "sq", lambda i: nc.vector.tensor_tensor(sq[:, :, :, :], o1[:, :, :, :], o1[:, :, :, :], ALU.mult), after=["o1_1"], prev=["ms"])
        s.step("dve", "ms", lambda i: nc.vector.tensor_reduce(ms[:, :, :], sq[:, :, :, :], AX.X, ALU.add), after=["sq"], prev=["o2"])
        s.step("act", "ms_ln", lambda i: nc.scalar.activation(ms[:, :, :], ms[:, :, :], ACT.Ln, bias=self.eps[:, :], scale=1.0 / HD), after=["ms"])
        s.step("act", "ms_rs", lambda i: nc.scalar.activation(ms[:, :, :], ms[:, :, :], ACT.Exp, scale=-0.5), after=["ms_ln"])
        s.step("dve", "o2", lambda i: nc.vector.tensor_tensor(
            o1[:, :, :, :].rearrange("p t h e -> p (t h) e"), o1[:, :, :, :].rearrange("p t h e -> p (t h) e"),
            ms[:, :, :].rearrange("p t h -> p (t h)").unsqueeze(2).broadcast_to((P, TILES * H, HD)), ALU.mult), after=["ms_rs"])
        s.step("dve", "o3", lambda i: nc.vector.tensor_tensor(
            o1[:, :, :, :].rearrange("p t h e -> p (t h) e"), o1[:, :, :, :].rearrange("p t h e -> p (t h) e"),
            nw[:, :].unsqueeze(1).broadcast_to((P, TILES * H, HD)), ALU.mult), after=["o2"])
        s.step("pe", "oT_pe", lambda i: [nc.tensor.transpose(PS[:, 4, t * P:t * P + P], o1[:, t, :, :].rearrange("p h e -> p (h e)"),
                                                             self.ident[:, :]) for t in range(TILES)][-1], after=["o3", "xnT"])
        s.step("act", "oT", lambda i: nc.scalar.activation(oT[:, :], PS[:, 4, 0:SEQ], ACT.Copy), after=["oT_pe"], prev=["p_pe"])
        for c in range(FC):
            s.step("act", f"gelu{c}", lambda i, c=c: nc.scalar.activation(hT[:, c, :], PS[:, (1, 2, 3, 0)[c], 0:SEQ], ACT.Gelu_apprx_tanh, bias=b1[:, c:c + 1]),
                   after=[f"h_pe{c}"], prev=["qr_pe"])
        s.step("pe", "qr_pe", lambda i: [nc.tensor.matmul(PS[0:RANK, 4, SEQ:2 * SEQ], u2[:, c, :], hT[:, c, :], start=(c == 0), stop=(c == FC - 1))
                                         for c in range(FC)][-1], after=["gelu3", "oT"], prev=["qr"])
        s.step("dve", "qr", lambda i: nc.vector.tensor_copy(qr[:, :], PS[0:RANK, 4, SEQ:2 * SEQ]), after=["qr_pe", "oT"], prev=["p_pe"])

        def back(i):
            for t in range(TILES):
                nc.tensor.matmul(PS[:, 5, t * P:t * P + P], oT[:, t * P:t * P + P], wt[:, 3, :], start=True, stop=True)
            for t in range(TILES):
                mm = nc.tensor.matmul(PS[:, 5, SEQ + t * P:SEQ + t * P + P], qr[:, t * P:t * P + P], v2[:, :], start=True, stop=True)
            return mm
        s.step("pe", "p_pe", back, after=["oT", "qr", "q", "k"])
        s.step("dve", "x1", lambda i: nc.vector.tensor_tensor(xs[:, :, :], xs[:, :, :], b2[:, :].unsqueeze(1).broadcast_to((P, TILES, P)), ALU.add), after=["ln_out1"])
        s.step("dve", "x2", lambda i: nc.vector.tensor_tensor(xs[:, :, :], xs[:, :, :], PS[:, 5, 0:SEQ].rearrange("p (t d) -> p t d", t=TILES), ALU.add), after=["x1", "p_pe"])
        s.step("dve", "x_out", lambda i: nc.vector.tensor_tensor(seq_tiles(X, i), xs[:, :, :], PS[:, 5, SEQ:2 * SEQ].rearrange("p (t d) -> p t d", t=TILES), ALU.add), after=["x2"])
        s.run(NSEQ)

    def L2(self):
        nc, d, PS, X = self.nc, self.d, self.PS, self.X
        H, R = 8, 64
        G = 4
        PAIRS = H // 2
        LEAVES, DEPTH = 256, 8
        wq = self.sb("wq", [P, H * R])
        wk = self.sb("wk", [P, H * R])
        wv = self.sb("wv", [P, H * P])
        fq = self.sb("fq", [P, P])
        rt = self.sb("rt", [P, LEAVES - 1])
        lv = self.sb("lv", [P, 2, P])
        wo = self.sb("wo", [P, P])
        bo = self.sb("bo", [P, P])
        qz = self.sb("qz", [P, H, SEQ])
        s = self.stage()
        s.step("sp", "in", lambda i: [nc.sync.dma_start(wq[:, :], d["L2_attn_Wq_T"]), nc.sync.dma_start(wk[:, :], d["L2_attn_Wk_T"]),
                                      nc.sync.dma_start(wv[:, :], d["L2_attn_Wv_T"]), nc.sync.dma_start(fq[:, :], d["L2_ffn_Wq_T"]),
                                      nc.sync.dma_start(rt[:, :], d["L2_ffn_routers_T"]),
                                      nc.sync.dma_start(lv[:, :, :], d["L2_ffn_leaf_values"].rearrange("(c p) d -> p c d", p=P)),
                                      nc.sync.dma_start(wo[:, :], d["L2_ffn_Wout_w_T"]), nc.sync.dma_start(bo[:, :], row(d["L2_ffn_Wout_b"], P))], dmas=8)
        s.step("pool", "zero", lambda i: nc.gpsimd.memset(qz[:, :, :], 0.0))
        s.run()

        xs = self.sb("xs", [P, TILES, P])
        xn = self.sb("xn", [P, TILES, P])
        xnT = self.sb("xnT", [P, SEQ])
        kT = self.sb("kT", [P, PAIRS, SEQ])
        v = self.sb("v", [P, TILES, H * P])
        sm = self.sb("sm", [P, 2, G, SEQ])
        pn = self.sb("pn", [P, 2, G, SEQ])
        pT = self.sb("pT", [P, 2, G * SEQ])
        mx = self.sb("mx", [P, 2, G])
        sl = self.sb("sl", [P, 2, G])
        fqT = self.sb("fqT", [P, SEQ])
        gt = self.sb("gt", [P, TILES, LEAVES])
        gl = self.sb("gl", [P, TILES, LEAVES])
        lp = [self.sb(f"lp{n}", [P, TILES, LEAVES]) for n in range(2)]
        lpT = self.sb("lpT", [P, 2, SEQ])
        rT = self.sb("rT", [P, SEQ])

        s = self.stage()
        s.step("dve", "xs", lambda i: nc.vector.tensor_scalar(xs[:, :, :], seq_tiles(X, i), 1.0, None, ALU.mult), prev=["x_out"])
        self.layernorm(s, xs, xn, "ln", ["xs"], wprev=["xnT_pe"])
        s.step("pe", "xnT_pe", lambda i: [nc.tensor.transpose(PS[:, 4, t * P:t * P + P], xn[:, t, :], self.ident[:, :]) for t in range(TILES)][-1],
               after=["ln_out1"], prev=["lpT"])
        s.step("act", "xnT", lambda i: nc.scalar.activation(xnT[:, :], PS[:, 4, 0:SEQ], ACT.Copy), after=["xnT_pe"], prev=["v_pe1", "fq_pe"])
        for b in range(2):
            s.step("pe", f"q_pe{b}", lambda i, b=b: [nc.tensor.matmul(PS[:, b, c * SEQ:(c + 1) * SEQ], wq[:, (2 * b + c) * P:(2 * b + c + 1) * P], xnT[:, :],
                                                                      start=True, stop=True) for c in range(2)][-1], after=["xnT"], prev=["s_sub2", "s_sub3"])
            for half in range(2):
                r = slice(half * R, half * R + R)
                s.step("act", f"q{b}{half}", lambda i, b=b, half=half, r=r: nc.scalar.activation(
                    qz[r, 4 * b + half:4 * b + half + 3:2, :], PS[r, b, :].rearrange("p (c n) -> p c n", c=2), ACT.Copy),
                    after=[f"q_pe{b}"], prev=["s_pe3"])
        for b in range(2):
            s.step("pe", f"k_pe{b}", lambda i, b=b: [nc.tensor.matmul(PS[:, 2 + b, c * SEQ:(c + 1) * SEQ], wk[:, (2 * b + c) * P:(2 * b + c + 1) * P], xnT[:, :],
                                                                      start=True, stop=True) for c in range(2)][-1], after=["xnT"], prev=["s_sub3"])
            s.step("act", f"k{b}", lambda i, b=b: nc.scalar.activation(
                kT[:, 2 * b:2 * b + 2, :], PS[:, 2 + b, :].rearrange("p (c n) -> p c n", c=2), ACT.Copy), after=[f"k_pe{b}"], prev=["s_pe3"])
        for t in range(TILES):
            s.step("pe", f"v_pe{t}", lambda i, t=t: [nc.tensor.matmul(PS[:, 4 + 2 * t + c, :], xnT[:, t * P:t * P + P], wv[:, c * 512:(c + 1) * 512],
                                                                      start=True, stop=True) for c in range(2)][-1], after=["xnT"],
                   prev=["rT"] if t == 0 else ["x_out"])
            s.step("dve", f"v{t}", lambda i, t=t: nc.vector.tensor_copy(v[:, t, :], PS[:, 4 + 2 * t:6 + 2 * t, :].rearrange("p b n -> p (b n)")),
                   after=[f"v_pe{t}"], prev=["o_pe3"])
        s.step("pe", "fq_pe", lambda i: nc.tensor.matmul(PS[:, 4, 0:SEQ], fq[:, :], xnT[:, :], start=True, stop=True), after=["v0"])
        s.step("act", "fqT", lambda i: nc.scalar.activation(fqT[:, :], PS[:, 4, 0:SEQ], ACT.Copy), after=["fq_pe"], prev=["g_pe"])

        units = [(qt, g) for qt in range(TILES) for g in range(H // G)]

        def bank(u):
            b = 2 * (u % 2)
            return PS[:, b:b + 2, :].rearrange("p b (h k) -> p (b h) k", h=2)

        def scores(u, qt, g):
            def go(i):
                for h in range(G):
                    hh = g * G + h
                    mm = nc.tensor.matmul(bank(u)[:, h, :], qz[:, hh, qt * P:qt * P + P], kT[:, hh // 2, :], start=True, stop=True)
                return mm
            s.step("pe", f"s_pe{u}", go, after=["q11", "q10", "k1"] + ([f"s_sub{u - 2}"] if u >= 2 else []))

        def softmax(u):
            a = u % 2
            old = [f"s_sub{u - 2}"] if u >= 2 else []
            s.step("dve", f"s_max{u}", lambda i: nc.vector.tensor_reduce(mx[:, a, :], bank(u), AX.X, ALU.max),
                   after=[f"s_pe{u}"] + old, prev=[f"s_sub{2 + a}"])
            s.step("dve", f"s_sub{u}", lambda i: nc.vector.tensor_tensor(
                sm[:, a, :, :], bank(u), mx[:, a, :].unsqueeze(2).broadcast_to((P, G, SEQ)), ALU.subtract),
                after=[f"s_max{u}"] + ([f"s_mul{u - 2}"] if u >= 2 else []), prev=[f"s_mul{2 + a}"])
            s.step("act", f"s_exp{u}", lambda i: nc.scalar.activation(sm[:, a, :, :], sm[:, a, :, :], ACT.Exp), after=[f"s_sub{u}"])
            s.step("dve", f"s_sum{u}", lambda i: nc.vector.tensor_reduce(sl[:, a, :], sm[:, a, :, :], AX.X, ALU.add),
                   after=[f"s_exp{u}"] + ([f"s_mul{u - 2}"] if u >= 2 else []), prev=[f"s_mul{2 + a}"])
            s.step("dve", f"s_inv{u}", lambda i: nc.vector.reciprocal(sl[:, a, :], sl[:, a, :]), after=[f"s_sum{u}"])
            s.step("dve", f"s_mul{u}", lambda i: nc.vector.tensor_tensor(
                pn[:, a, :, :], sm[:, a, :, :], sl[:, a, :].unsqueeze(2).broadcast_to((P, G, SEQ)), ALU.mult),
                after=[f"s_inv{u}"] + ([f"t_pe{u - 2}"] if u >= 2 else []), prev=[f"t_pe{2 + a}"])

        def turn(u):
            a = u % 2

            def go(i):
                for c in range(2 * G):
                    mm = nc.tensor.transpose(PS[:, 4 + c // 4, (c % 4) * P:(c % 4 + 1) * P],
                                             pn[:, a, c // 2, (c % 2) * P:(c % 2) * P + P], self.ident[:, :])
                return mm
            s.step("pe", f"t_pe{u}", go, after=[f"s_mul{u}"] + ([f"t{u - 1}"] if u else ["v0", "fqT", "ge"]))
            s.step("act", f"t{u}", lambda i: nc.scalar.activation(pT[:, a, :], PS[:, 4:6, :].rearrange("p b k -> p (b k)"), ACT.Copy),
                   after=[f"t_pe{u}"] + ([f"o_pe{u - 2}"] if u >= 2 else []), prev=[f"o_pe{2 + a}"])

        def output(u, qt, g):
            def go(i):
                for c in range(2 * G):
                    hh, k = g * G + c // 2, c % 2
                    mm = nc.tensor.matmul(PS[:, 6 + qt, 0:P], pT[:, u % 2, c * P:c * P + P], v[:, k, hh * P:(hh + 1) * P],
                                          start=(g == 0 and c == 0), stop=False)
                return mm
            s.step("pe", f"o_pe{u}", go, after=[f"t{u}", "v1"])

        def gate():
            s.step("pe", "g_pe", lambda i: [nc.tensor.matmul(PS[:, 5, t * SEQ:t * SEQ + LEAVES - 1], fqT[:, t * P:t * P + P], rt[:, :], start=True, stop=True)
                                            for t in range(TILES)][-1], after=["fqT", "v0"])
            s.step("act", "ge", lambda i: nc.scalar.activation(gt[:, :, 0:LEAVES - 1], PS[:, 5, :].rearrange("p (t n) -> p t n", t=TILES)[:, :, 0:LEAVES - 1],
                                                               ACT.Exp, scale=-1.0), after=["g_pe"], prev=["lv7"])
            s.step("dve", "g1", lambda i: nc.vector.tensor_scalar(gt[:, :, 0:LEAVES - 1], gt[:, :, 0:LEAVES - 1], 1.0, None, ALU.add), after=["ge"])
            s.step("dve", "g2", lambda i: nc.vector.reciprocal(gt[:, :, 0:LEAVES - 1], gt[:, :, 0:LEAVES - 1]), after=["g1"])
            s.step("pool", "g3", lambda i: nc.gpsimd.tensor_scalar(gl[:, :, 0:LEAVES - 1], gt[:, :, 0:LEAVES - 1], -1.0, 1.0, ALU.mult, ALU.add),
                   after=["g2"], prev=["lv7"], solo=True)
            for lev in range(DEPTH):
                n = 2 ** lev
                src = lp[lev % 2][:, :, 0:n]
                dst = lp[(lev + 1) % 2][:, :, 0:2 * n].rearrange("p t (n two) -> p t n two", two=2)

                def both(i, n=n, src=src, dst=dst):
                    for side, g in ((0, gl), (1, gt)):
                        if n == 1:
                            op = nc.gpsimd.tensor_copy(dst[:, :, :, side], g[:, :, 0:1])
                        else:
                            op = nc.gpsimd.tensor_tensor(dst[:, :, :, side], src, g[:, :, n - 1:2 * n - 1], ALU.mult)
                    return op
                s.step("pool", f"lv{lev}", both, after=["g3"] if lev == 0 else [f"lv{lev - 1}"], prev=["lpT_pe"], solo=True)

        for n in range(len(units) + 2):
            if n < len(units):
                scores(n, *units[n])
                softmax(n)
            if n == 0:
                gate()
            if 1 <= n <= len(units):
                turn(n - 1)
            if n >= 2:
                output(n - 2, *units[n - 2])
        leaf = lp[DEPTH % 2]
        s.step("pe", "lpT_pe", lambda i: [nc.tensor.transpose(PS[:, 4, (c * 2 + t) * P:(c * 2 + t + 1) * P], leaf[:, t, c * P:c * P + P], self.ident[:, :])
                                          for c in range(2) for t in range(TILES)][-1], after=["lv7", "t3"])
        s.step("act", "lpT", lambda i: nc.scalar.activation(lpT[:, :, :].rearrange("p c n -> p (c n)"), PS[:, 4, :], ACT.Copy), after=["lpT_pe"], prev=["rT_pe"])
        s.step("pe", "rT_pe", lambda i: [nc.tensor.matmul(PS[:, 5, 0:SEQ], lv[:, c, :], lpT[:, c, :], start=(c == 0), stop=(c == 1)) for c in range(2)][-1],
               after=["lpT"])
        s.step("act", "rT", lambda i: nc.scalar.activation(rT[:, :], PS[:, 5, 0:SEQ], ACT.Copy), after=["rT_pe"], prev=["w_pe"])
        s.step("pe", "w_pe", lambda i: [nc.tensor.matmul(PS[:, 6 + t, 0:P], rT[:, t * P:t * P + P], wo[:, :], start=False, stop=True) for t in range(TILES)][-1],
               after=["rT"])
        s.step("dve", "x1", lambda i: nc.vector.tensor_tensor(xs[:, :, :], xs[:, :, :], bo[:, :].unsqueeze(1).broadcast_to((P, TILES, P)), ALU.add), after=["ln_out1"])
        s.step("dve", "x_out", lambda i: nc.vector.tensor_tensor(seq_tiles(X, i), xs[:, :, :], PS[:, 6:8, 0:P], ALU.add), after=["x1", "w_pe"])
        s.run(NSEQ)

    def L3a(self):
        nc, d, PS, X, Z = self.nc, self.d, self.PS, self.X, self.Z
        CH, NS, TAPS, DR = 2, 16, 4, 8
        G = 4
        UN = NS // G
        PAD = TAPS - 1
        pre = "L3_attn_"
        lg = self.sb("lg", [P, 2])
        wi = self.sb("wi", [P, 4 * P])
        wx = self.sb("wx", [P, CH, DR + 2 * NS])
        wd = self.sb("wd", [P, CH * P])
        wo = self.sb("wo", [P, CH, P])
        cw = self.sb("cw", [P, CH, TAPS])
        cb, db, dd = (self.sb(n, [P, CH]) for n in ("cb", "db", "dd"))
        al = self.sb("al", [P, CH, NS])
        na = self.sb("na", [P, CH, NS])
        res = self.sb("res", [P, 1])
        xd = self.sb("xd", [P, SEQ])
        xp = self.sb("xp", [P, CH, PAD + SEQ])
        dA = self.sb("dA", [P, CH, G, SEQ])
        s = self.stage()
        s.step("pool", "z0", lambda i: nc.gpsimd.memset(wd[:, :], 0.0))
        s.step("pool", "z1", lambda i: nc.gpsimd.memset(xd[:, :], 0.0))
        s.step("pool", "z2", lambda i: nc.gpsimd.memset(xp[:, :, :], 0.0))
        s.step("pool", "z3", lambda i: nc.gpsimd.memset(dA[:, :, :, :], 0.0))
        s.step("sp", "in", lambda i: [
            nc.sync.dma_start(lg[:, 0:1], d[pre + "ln_g"].rearrange("(p a) -> p a", a=1)),
            nc.sync.dma_start(lg[:, 1:2], d[pre + "ln_b"].rearrange("(p a) -> p a", a=1)),
            nc.sync.dma_start(wi[:, :], d[pre + "in_proj_w_T"]), nc.sync.dma_start(wx[:, :, :], d[pre + "x_proj_w_T"]),
            nc.sync.dma_start(wd[0:DR, :], d[pre + "dt_proj_w_T"]), nc.sync.dma_start(wo[:, :, :], d[pre + "out_proj_w_T"]),
            nc.sync.dma_start(cw[:, :, :], d[pre + "conv_w_T"]), nc.sync.dma_start(cb[:, :], d[pre + "conv_b_T"]),
            nc.sync.dma_start(db[:, :], d[pre + "dt_proj_b_T"]), nc.sync.dma_start(dd[:, :], d[pre + "D_T"]),
            nc.sync.dma_start(al[:, :, :], d[pre + "A_log_T"]), nc.sync.dma_start(res[:, :], row(d[pre + "res_scale"], 1))],
            after=["z0"], dmas=12)
        s.step("act", "ea", lambda i: nc.scalar.activation(na[:, :, :], al[:, :, :], ACT.Exp), after=["in"])
        s.step("dve", "na", lambda i: nc.vector.tensor_scalar(na[:, :, :], na[:, :, :], -1.0, None, ALU.mult), after=["ea"])
        s.run()

        xs = self.sb("xs", [P, TILES, P])
        xn = self.sb("xn", [P, TILES, P])
        xm = self.sb("xm", [P, TILES, P])
        xmT = self.sb("xmT", [P, SEQ])
        zs = self.sb("zs", [P, CH, SEQ])
        zg = self.sb("zg", [P, CH, SEQ])
        xc = self.sb("xc", [P, CH, SEQ])
        xg = self.sb("xg", [P, CH, SEQ])
        dv = self.sb("dv", [P, CH, SEQ])
        de = self.sb("de", [P, CH, SEQ])
        dt = self.sb("dt", [P, CH, SEQ])
        dx = self.sb("dx", [P, CH, SEQ])
        db_x = self.sb("db_x", [P, CH, G, SEQ])
        hs = self.sb("hs", [P, CH, G, SEQ])
        hc = self.sb("hc", [P, CH, G, SEQ])
        yT = self.sb("yT", [P, CH, SEQ])

        def flat(t):
            return t.rearrange("p g n -> p (g n)")

        s = self.stage()
        s.step("dve", "xs", lambda i: nc.vector.tensor_scalar(xs[:, :, :], seq_tiles(X, i), 1.0, None, ALU.mult), prev=["x_out"])
        self.layernorm(s, xs, xn, "ln", ["xs"], wprev=["lm_out1", "zcopy"])
        s.step("dve", "zcopy", lambda i: nc.vector.tensor_scalar(seq_tiles(Z, i), xn[:, :, :], 1.0, None, ALU.mult), after=["ln_out0", "ln_out1"])
        self.layernorm(s, xn, xm, "lm", ["ln_out0", "ln_out1"], wprev=["xmT_pe"])
        s.step("pe", "xmT_pe", lambda i: [nc.tensor.transpose(PS[:, 4, t * P:t * P + P], xm[:, t, :], self.ident[:, :]) for t in range(TILES)][-1],
               after=["lm_out1"], prev=["dv1", "xmT"])
        s.step("act", "xmT", lambda i: nc.scalar.activation(xmT[:, :], PS[:, 4, 0:SEQ], ACT.Identity, bias=lg[:, 1:2], scale=lg[:, 0:1]),
               after=["xmT_pe"], prev=["in_pe1"])
        for b in range(2):
            s.step("pe", f"in_pe{b}", lambda i, b=b: [nc.tensor.matmul(PS[:, b, c * SEQ:(c + 1) * SEQ], wi[:, (2 * b + c) * P:(2 * b + c + 1) * P], xmT[:, :],
                                                                       start=True, stop=True) for c in range(2)][-1], after=["xmT"], prev=[f"dbx{UN - 1}1"])
        s.step("act", "xp", lambda i: nc.scalar.activation(xp[:, :, PAD:PAD + SEQ], PS[:, 0, :].rearrange("p (c n) -> p c n", c=CH), ACT.Copy),
               after=["in_pe0"], prev=[f"cv{PAD}1"])
        s.step("act", "ze", lambda i: nc.scalar.activation(zg[:, :, :], PS[:, 1, :].rearrange("p (c n) -> p c n", c=CH), ACT.Exp, scale=-1.0),
               after=["in_pe1"], prev=["z_s"])
        for c in range(CH):
            s.step("dve", f"cv0{c}", lambda i, c=c: nc.vector.tensor_scalar(xc[:, c, :], xp[:, c, 0:SEQ], cw[:, c, 0:1], cb[:, c:c + 1], ALU.mult, ALU.add),
                   after=["xp"], prev=["y1%d" % c, "xd_pe"])
        for k in range(1, TAPS):
            for c in range(CH):
                s.step("dve", f"cv{k}{c}", lambda i, c=c, k=k: nc.vector.scalar_tensor_tensor(
                    xc[:, c, :], xp[:, c, k:k + SEQ], cw[:, c, k:k + 1], xc[:, c, :], ALU.mult, ALU.add), after=[f"cv{k - 1}{c}"])
        s.step("act", "xe", lambda i: nc.scalar.activation(xg[:, :, :], xc[:, :, :], ACT.Exp, scale=-1.0), after=[f"cv{PAD}0", f"cv{PAD}1"], prev=["x_s"])
        s.step("dve", "z_1", lambda i: nc.vector.tensor_scalar(zg[:, :, :], zg[:, :, :], 1.0, None, ALU.add), after=["ze"])
        s.step("dve", "z_r", lambda i: nc.vector.reciprocal(zg[:, :, :], zg[:, :, :]), after=["z_1"])
        s.step("dve", "z_s", lambda i: nc.vector.tensor_tensor(zs[:, :, :], zg[:, :, :], PS[:, 1, :].rearrange("p (c n) -> p c n", c=CH), ALU.mult),
               after=["z_r"], prev=["y2"])
        s.step("dve", "x_1", lambda i: nc.vector.tensor_scalar(xg[:, :, :], xg[:, :, :], 1.0, None, ALU.add), after=["xe"])
        s.step("dve", "x_r", lambda i: nc.vector.reciprocal(xg[:, :, :], xg[:, :, :]), after=["x_1"])
        s.step("dve", "x_s", lambda i: nc.vector.tensor_tensor(xc[:, :, :], xc[:, :, :], xg[:, :, :], ALU.mult), after=["x_r"])
        s.step("pe", "xd_pe", lambda i: [nc.tensor.matmul(PS[0:DR + 2 * NS, 5, 0:SEQ], wx[:, c, :], xc[:, c, :], start=(c == 0), stop=(c == CH - 1))
                                         for c in range(CH)][-1], after=["x_s"], prev=["x_out"])
        s.step("act", "xd", lambda i: nc.scalar.activation(xd[0:DR + 2 * NS, :], PS[0:DR + 2 * NS, 5, 0:SEQ], ACT.Copy), after=["xd_pe"],
               prev=[f"c_pe{UN - 1}", "dt_pe"])
        s.step("pe", "dt_pe", lambda i: [nc.tensor.matmul(PS[:, 4, c * SEQ:(c + 1) * SEQ], wd[:, c * P:c * P + P], xd[:, :], start=True, stop=True)
                                         for c in range(CH)][-1], after=["xd", "xmT"])
        for c in range(CH):
            s.step("dve", f"dv{c}", lambda i, c=c: nc.vector.tensor_scalar(dv[:, c, :], PS[:, 4, c * SEQ:(c + 1) * SEQ], db[:, c:c + 1], None, ALU.add),
                   after=["dt_pe"], prev=["dt"])
        s.step("dve", "da", lambda i: nc.vector.scalar_tensor_tensor(de[:, :, :], dv[:, :, :], -1.0, dv[:, :, :], ALU.mult, ALU.max),
               after=["dv0", "dv1"], prev=["dt"])
        s.step("act", "de", lambda i: nc.scalar.activation(de[:, :, :], de[:, :, :], ACT.Exp, scale=-1.0), after=["da"])
        s.step("act", "dl", lambda i: nc.scalar.activation(de[:, :, :], de[:, :, :], ACT.Ln, bias=1.0), after=["de"])
        s.step("dve", "dt", lambda i: nc.vector.scalar_tensor_tensor(dt[:, :, :], dv[:, :, :], 0.0, de[:, :, :], ALU.max, ALU.add),
               after=["dl"], prev=["dx", f"dA{UN - 1}"])
        s.step("dve", "dx", lambda i: nc.vector.tensor_tensor(dx[:, :, :], dt[:, :, :], xc[:, :, :], ALU.mult), after=["dt"], prev=[f"dbx{UN - 1}1"])

        def spread(u, first, b0):
            def go(i):
                for g in range(G):
                    r = first + u * G + g
                    mm = nc.tensor.matmul(PS[:, b0 + g // 2, (g % 2) * SEQ:(g % 2 + 1) * SEQ], self.ident[:, r:r + 1].broadcast_to((P, P)), xd[:, :],
                                          start=True, stop=True)
                return mm
            return go

        def sum_states(u):
            def go(i):
                for c in range(CH):
                    for g in range(G):
                        mm = nc.tensor.matmul(PS[:, 6 + c, 0:SEQ], self.ident[:, :], hc[:, c, g, :], start=(u == 0 and g == 0), stop=(u == UN - 1 and g == G - 1))
                return mm
            s.step("pe", f"y_pe{u}", go, after=[f"hc{u}0", f"hc{u}1"], prev=["y10", "y11"] if u == 0 else [])

        for u in range(UN):
            s.step("pe", f"b_pe{u}", spread(u, DR, 0), after=["xd"] + ([f"dbx{u - 1}0", f"dbx{u - 1}1"] if u else ["xp", "z_s"]))
            s.step("pe", f"c_pe{u}", spread(u, DR + NS, 2), after=["xd"] + ([f"hc{u - 1}0", f"hc{u - 1}1"] if u else []), prev=[] if u else [f"hc{UN - 1}1"])
            if u:
                sum_states(u - 1)

            def decay(i, u=u):
                for c in range(CH):
                    for g in range(G):
                        k = u * G + g
                        op = nc.scalar.activation(dA[:, c, g, 1:SEQ], dt[:, c, 1:SEQ], ACT.Exp, scale=na[:, c, k:k + 1])
                return op
            s.step("act", f"dA{u}", decay, after=["dt"] + ([f"h{u - 1}0", f"h{u - 1}1"] if u else []), prev=[] if u else [f"h{UN - 1}1"])
            for c in range(CH):
                s.step("dve", f"dbx{u}{c}", lambda i, c=c: nc.vector.tensor_tensor(
                    db_x[:, c, :, :], dx[:, c, :].unsqueeze(1).broadcast_to((P, G, SEQ)),
                    PS[:, 0:2, :].rearrange("p b (g n) -> p (b g) n", g=2), ALU.mult),
                    after=["dx", f"b_pe{u}"] + ([f"h{u - 1}{c}"] if u else []), prev=[] if u else [f"h{UN - 1}{c}"])
            for c in range(CH):
                s.step("dve", f"h{u}{c}", lambda i, c=c: nc.vector.tensor_tensor_scan(
                    flat(hs[:, c, :, :]), flat(dA[:, c, :, :]), flat(db_x[:, c, :, :]), 0.0, ALU.mult, ALU.add),
                    after=[f"dbx{u}{c}", f"dA{u}"] + ([f"hc{u - 1}{c}"] if u else []), prev=[] if u else [f"hc{UN - 1}{c}"])
            for c in range(CH):
                s.step("dve", f"hc{u}{c}", lambda i, c=c: nc.vector.tensor_tensor(
                    hc[:, c, :, :], hs[:, c, :, :], PS[:, 2:4, :].rearrange("p b (g n) -> p (b g) n", g=2), ALU.mult),
                    after=[f"h{u}{c}", f"c_pe{u}"] + ([f"y_pe{u - 1}"] if u else []), prev=[] if u else [f"y_pe{UN - 1}"])
        sum_states(UN - 1)
        for c in range(CH):
            s.step("dve", f"y1{c}", lambda i, c=c: nc.vector.scalar_tensor_tensor(
                yT[:, c, :], xc[:, c, :], dd[:, c:c + 1], PS[:, 6 + c, 0:SEQ], ALU.mult, ALU.add), after=[f"y_pe{UN - 1}"], prev=["o_pe"])
        s.step("dve", "y2", lambda i: nc.vector.tensor_tensor(yT[:, :, :], yT[:, :, :], zs[:, :, :], ALU.mult), after=["y10", "y11"])
        s.step("pe", "o_pe", lambda i: [nc.tensor.matmul(PS[:, 5, t * P:t * P + P], yT[:, c, t * P:t * P + P], wo[:, c, :], start=(c == 0), stop=(c == CH - 1))
                                        for t in range(TILES) for c in range(CH)][-1], after=["y2", "xd"])
        s.step("dve", "x1", lambda i: nc.vector.tensor_tensor(xs[:, :, :], xs[:, :, :], xn[:, :, :], ALU.add), after=["lm_out1"])
        s.step("dve", "x_out", lambda i: nc.vector.scalar_tensor_tensor(
            seq_tiles(X, i).rearrange("p t d -> p (t d)"), PS[:, 5, 0:SEQ], res[:, :], xs[:, :, :].rearrange("p t d -> p (t d)"), ALU.mult, ALU.add),
            after=["x1", "o_pe"])
        s.run(NSEQ)

    def L3f(self):
        nc, d, PS, X, Z = self.nc, self.d, self.PS, self.X, self.Z
        DEPTH, H, HD, WIN = 6, 16, 64, 32
        INNER = H * HD
        KEYS = 2 * WIN
        PAIRS = H // 2
        NW = P // WIN
        DI = int(P * 4 * 2 / 3)
        CHK = [(0, P), (P, P), (2 * P, DI - 2 * P)]
        QK_SCALE = 8.0
        GRP = 4 * P
        pre = "L3_ffn_"

        wqkv = self.sb("wqkv", [P, 3 * INNER])
        wo = self.sb("wo", [P, PAIRS, P])
        w1 = self.sb("w1", [P, 2 * DI])
        w2 = self.sb("w2", [P, 3, P])
        b1 = self.sb("b1", [P, 2, 3])
        b2 = self.sb("b2", [P, P])
        gb = self.sb("gb", [P, 2])
        qks = self.sb("qks", [P, 4, HD])
        rotc = self.sb("rotc", [P, TILES, 4, HD])
        rot = self.sb("rot", [P, TILES, 4, HD])
        lmask = self.sb("lmask", [P, TILES, KEYS])
        mean = self.sb("mean", [P, P])
        fn = self.sb("fn", [P, NT * P])
        zT = self.sb("zT", [P, SEQ + 1])
        sT = self.sb("sT", [P, SEQ + 1])
        qz = self.sb("qz", [P, TILES, PAIRS, 2, P])
        kT = self.sb("kT", [P, PAIRS, WIN + SEQ])
        vw = self.sb("vw", [P, TILES * NW + 1, PAIRS * HD])
        s = self.stage()
        s.step("sp", "in", lambda i: [nc.sync.dma_start(rotc[:, :, :, :], d["c_rot"]), nc.sync.dma_start(lmask[:, :, :], d["c_local"])], dmas=2)
        s.step("pool", "m0", lambda i: nc.gpsimd.memset(mean[:, :], 1.0 / P))
        s.step("pool", "m1", lambda i: nc.gpsimd.memset(zT[:, :], 0.0))
        s.step("pool", "m2", lambda i: nc.gpsimd.memset(sT[:, :], 0.0))
        s.step("pool", "m3", lambda i: nc.gpsimd.memset(qz[:, :, :, :, :], 0.0))
        s.step("pool", "m4", lambda i: nc.gpsimd.memset(kT[:, :, :], 0.0))
        s.step("pool", "m5", lambda i: nc.gpsimd.memset(vw[:, :, :], 0.0))
        s.run()

        zs = self.sb("zs", [P, TILES, P])
        raw = self.sb("raw", [P, 2, 2 * INNER])
        sqr = self.sb("sqr", [P, 2 * INNER])
        ss = self.sb("ss", [P, 2, 2 * H])
        t1 = self.sb("t1", [P, 2 * INNER])
        t2 = self.sb("t2", [P, 2 * INNER])
        v2 = self.sb("v2", [P, TILES, 2, PAIRS * HD])
        sm = self.sb("sm", [P, PAIRS, 2, KEYS])
        mx = self.sb("mx", [P, PAIRS, 2])
        sl = self.sb("sl", [P, PAIRS, 2])
        pT = self.sb("pT", [P, PAIRS, P])
        oT = self.sb("oT", [P, PAIRS, P])
        zn = self.sb("zn", [P, TILES, P])
        xc = self.sb("xc", [P, SEQ])
        xq = self.sb("xq", [P, SEQ])
        rs = self.sb("rs", [P, SEQ])
        gg = self.sb("gg", [P, 3, GRP])
        hh = self.sb("hh", [P, 3, GRP])
        zb = self.sb("zb", [P, GRP // P, P])

        def at(name, l):
            a = d[pre + name][bass.ds(l, 1)]
            return a

        with nc.Fori(0, DEPTH) as l:
            s = self.stage()

            def loads(i):
                out = [nc.sync.dma_start(wqkv[:, :], at("Wqkv", l).rearrange("a p n -> (a p) n")),
                       nc.sync.dma_start(wo[:, :, :], at("Wo", l).rearrange("a (c p) n -> p (a c) n", p=P)),
                       nc.sync.dma_start(w1[:, :], at("W1", l).rearrange("a p n -> (a p) n")),
                       nc.sync.dma_start(b2[:, :], at("b2", l).broadcast_to((P, P))),
                       nc.sync.dma_start(gb[:, 0:1], at("ln_g", l).rearrange("a (p b) -> (a p) b", b=1)),
                       nc.sync.dma_start(gb[:, 1:2], at("ln_b", l).rearrange("a (p b) -> (a p) b", b=1))]
                for c, (o, m) in enumerate(CHK):
                    out.append(nc.sync.dma_start(w2[0:m, c, :], at("W2", l)[:, o:o + m, :].rearrange("a p n -> (a p) n")))
                    for half in range(2):
                        out.append(nc.sync.dma_start(b1[0:m, half, c:c + 1], at("b1", l)[:, half * DI + o:half * DI + o + m].rearrange("a (p b) -> (a p) b", b=1)))
                for n, w in enumerate(("q_scale", "k_scale")):
                    out.append(nc.sync.dma_start(qks[:, 2 * n, :], at(w, l).broadcast_to((P, HD))))
                    for half in range(2):
                        to, fr = half * HD // 2, (1 - half) * HD // 2
                        out.append(nc.sync.dma_start(qks[:, 2 * n + 1, to:to + HD // 2], at(w, l)[:, fr:fr + HD // 2].broadcast_to((P, HD // 2))))
                return out
            s.step("sp", "w", loads, dmas=6 + 9 + 6)
            for t in range(TILES):
                s.step("dve", f"rot{t}", lambda i, t=t: nc.vector.tensor_tensor(rot[:, t, :, :], rotc[:, t, :, :], qks[:, :, :], ALU.mult), after=["w"])
            s.run()

            s = self.stage()
            s.step("dve", "zs", lambda i: nc.vector.tensor_scalar(zs[:, :, :], seq_tiles(Z, i), 1.0, None, ALU.mult), prev=["zn1"])
            s.step("pe", "zT_pe", lambda i: [nc.tensor.transpose(PS[:, 7, t * P:t * P + P], zs[:, t, :], self.ident[:, :]) for t in range(TILES)][-1],
                   after=["zs"], prev=["var"])
            s.step("act", "zTa", lambda i: nc.scalar.activation(zT[0:HD, 0:SEQ], PS[0:HD, 7, 0:SEQ], ACT.Copy), after=["zT_pe"], prev=["p_pe1_5"])
            s.step("act", "zTb", lambda i: nc.scalar.activation(zT[HD:P, 1:SEQ + 1], PS[HD:P, 7, 0:SEQ], ACT.Copy), after=["zT_pe"], prev=["p_pe1_5"])

            def front(t):
                for j in range(6):
                    n = 6 * t + j
                    b = n % 3
                    freed = f"raw{(n - 3) // 6}_{(n - 3) % 6}"
                    if j < 4:
                        w = wqkv[:, j * 512:(j + 1) * 512]
                    else:
                        w = wqkv[:, 2 * INNER:].rearrange("p (a h e) -> p h a e", h=2, e=HD)[:, j - 4, :, :]
                    s.step("pe", f"p_pe{t}_{j}", lambda i, b=b, w=w, t=t: nc.tensor.matmul(PS[:, b, :], zT[:, t * P:t * P + P], w, start=True, stop=True),
                           after=["zTa", "zTb"] + ([freed] if n >= 3 else []) + (["oT0"] if 0 else []),
                           prev=["oT0", "oT1", f"raw1_{n + 3}"] if n < 3 else [])
                    if j < 4:
                        s.step("act", f"raw{t}_{j}", lambda i, b=b, j=j, t=t: nc.scalar.activation(raw[:, t, j * 512:(j + 1) * 512], PS[:, b, :], ACT.Copy),
                               after=[f"p_pe{t}_{j}"], prev=[f"rq{t}", f"sqr{t}"])
                    else:
                        s.step("act", f"raw{t}_{j}", lambda i, b=b, j=j, t=t: nc.scalar.activation(v2[:, t, j - 4, :], PS[:, b, :], ACT.Copy),
                               after=[f"p_pe{t}_{j}"], prev=["vlow", "vhigh"])
                s.step("pool", f"sqr{t}", lambda i, t=t: nc.gpsimd.tensor_tensor(sqr[:, :], raw[:, t, :], raw[:, t, :], ALU.mult),
                       after=[f"raw{t}_3"] + (["ss0"] if t else []), prev=[] if t else ["ss1"])
                s.step("dve", f"ss{t}", lambda i, t=t: nc.vector.tensor_reduce(ss[:, t, :], sqr[:, :].rearrange("p (h e) -> p h e", e=HD), AX.X, ALU.add),
                       after=[f"sqr{t}"], prev=[f"rq{t}"])
                s.step("dve", f"sc{t}", lambda i, t=t: nc.vector.tensor_scalar(ss[:, t, :], ss[:, t, :], 1e-24, None, ALU.max), after=[f"ss{t}"])
                s.step("act", f"sl{t}", lambda i, t=t: nc.scalar.activation(ss[:, t, :], ss[:, t, :], ACT.Ln), after=[f"sc{t}"])
                s.step("act", f"sr{t}", lambda i, t=t: nc.scalar.activation(ss[:, t, :], ss[:, t, :], ACT.Exp, scale=-0.5), after=[f"sl{t}"])

                def heads(a):
                    return a.rearrange("p (h e) -> p h e", e=HD)
                s.step("dve", f"rq{t}", lambda i, t=t: nc.vector.tensor_tensor(
                    heads(raw[:, t, :]), heads(raw[:, t, :]), ss[:, t, :].unsqueeze(2).broadcast_to((P, 2 * H, HD)), ALU.mult), after=[f"sr{t}"])

                def cosine(i, t=t):
                    for n in range(2):
                        op = nc.vector.tensor_tensor(heads(t1[:, n * INNER:(n + 1) * INNER]), heads(raw[:, t, n * INNER:(n + 1) * INNER]),
                                                     rot[:, t, 2 * n, :].unsqueeze(1).broadcast_to((P, H, HD)), ALU.mult)
                    return op

                def sine(i, t=t):
                    for n in range(2):
                        for half in range(2):
                            to = slice(half * HD // 2, (half + 1) * HD // 2)
                            fr = slice((1 - half) * HD // 2, (2 - half) * HD // 2)
                            op = nc.gpsimd.tensor_tensor(heads(t2[:, n * INNER:(n + 1) * INNER])[:, :, to], heads(raw[:, t, n * INNER:(n + 1) * INNER])[:, :, fr],
                                                         rot[:, t, 2 * n + 1, to].unsqueeze(1).broadcast_to((P, H, HD // 2)), ALU.mult)
                    return op
                s.step("dve", f"rc{t}", cosine, after=[f"rq{t}"] + (["qk_pe0_3"] if t else []), prev=[] if t else ["qk_pe1_3"])
                s.step("pool", f"rn{t}", sine, after=[f"rq{t}"] + (["ra0"] if t else []), prev=[] if t else ["ra1"])
                s.step("dve", f"ra{t}", lambda i: nc.vector.tensor_tensor(t1[:, :], t1[:, :], t2[:, :], ALU.add), after=[f"rc{t}", f"rn{t}"])
                for g in range(4):
                    b = 3 + g % 2
                    before = [f"qk{t}_{g - 2}"] if g >= 2 else []
                    s.step("pe", f"qk_pe{t}_{g}", lambda i, g=g, b=b: [nc.tensor.transpose(
                        PS[:, b, c * P:c * P + P], t1[:, (4 * g + c) * P:(4 * g + c + 1) * P], self.ident[:, :]) for c in range(4)][-1],
                        after=[f"ra{t}"] + before + ([f"qk0_{g + 2}"] if t and g < 2 else []), prev=["pT1"] if not t and g < 2 else [])
                    src = PS[:, b, :].rearrange("p (c n) -> p c n", n=P)
                    if g < 2:
                        def put(i, g=g, src=src, t=t):
                            for half in range(2):
                                r = slice(half * HD, half * HD + HD)
                                op = nc.scalar.activation(qz[r, t, 4 * g:4 * g + 4, half, :], src[r, :, :], ACT.Copy)
                            return op
                        s.step("act", f"qk{t}_{g}", put, after=[f"qk_pe{t}_{g}"], prev=[f"s_pe{t}"])
                    else:
                        s.step("act", f"qk{t}_{g}", lambda i, g=g, t=t, src=src: nc.scalar.activation(
                            kT[:, 4 * (g - 2):4 * (g - 1), WIN + t * P:WIN + (t + 1) * P], src, ACT.Copy), after=[f"qk_pe{t}_{g}"], prev=["s_pe1"])

            def scores(t):
                def go(i):
                    for w in range(NW):
                        for h in range(H):
                            mm = nc.tensor.matmul(PS[w * WIN:(w + 1) * WIN, 5 + h % 2, (h // 2) * KEYS:(h // 2 + 1) * KEYS],
                                                  qz[:, t, h // 2, h % 2, w * WIN:(w + 1) * WIN], kT[:, h // 2, t * P + w * WIN:t * P + w * WIN + KEYS],
                                                  start=True, stop=True)
                    return mm
                s.step("pe", f"s_pe{t}", go, after=[f"qk{t}_3"] + (["s_in0"] if t else []), prev=[] if t else ["s_in1"])

            def softmax(t):
                p3 = sm[:, :, :, :].rearrange("p a b k -> p (a b) k")

                def masked(i):
                    for half in range(2):
                        op = nc.vector.scalar_tensor_tensor(sm[:, :, half, :], PS[:, 5 + half, :].rearrange("p (a k) -> p a k", k=KEYS), QK_SCALE,
                                                            lmask[:, t, :].unsqueeze(1).broadcast_to((P, PAIRS, KEYS)), ALU.mult, ALU.add)
                    return op
                s.step("dve", f"s_in{t}", masked, after=[f"s_pe{t}"] + (["pT_pe0"] if t else []), prev=[] if t else ["pT_pe1"])
                s.step("dve", f"s_max{t}", lambda i: nc.vector.tensor_reduce(mx[:, :, :], sm[:, :, :, :], AX.X, ALU.max), after=[f"s_in{t}"])
                s.step("dve", f"s_sub{t}", lambda i: nc.vector.tensor_tensor(
                    p3, p3, mx[:, :, :].rearrange("p a b -> p (a b)").unsqueeze(2).broadcast_to((P, H, KEYS)), ALU.subtract), after=[f"s_max{t}"])
                s.step("act", f"s_exp{t}", lambda i: nc.scalar.activation(sm[:, :, :, :], sm[:, :, :, :], ACT.Exp), after=[f"s_sub{t}"])
                s.step("dve", f"s_sum{t}", lambda i: nc.vector.tensor_reduce(sl[:, :, :], sm[:, :, :, :], AX.X, ALU.add), after=[f"s_exp{t}"])
                s.step("dve", f"s_inv{t}", lambda i: nc.vector.reciprocal(sl[:, :, :], sl[:, :, :]), after=[f"s_sum{t}"])
                s.step("dve", f"s_mul{t}", lambda i: nc.vector.tensor_tensor(
                    p3, p3, sl[:, :, :].rearrange("p a b -> p (a b)").unsqueeze(2).broadcast_to((P, H, KEYS)), ALU.mult), after=[f"s_inv{t}"])

            def windows():
                for nm, part, shift in (("vhigh", WIN, 0), ("vlow", 0, 1)):
                    def go(i, part=part, shift=shift):
                        out = []
                        for half in range(2):
                            for k in range(NW):
                                dst = vw[half * HD + part:half * HD + part + WIN, k + shift:k + shift + NW * (TILES - 1) + 1:NW, :]
                                out.append(nc.sync.dma_start(dst, v2[k * WIN:(k + 1) * WIN, :, half, :]))
                        return out
                    s.step("sp", nm, go, after=["raw0_5", "raw1_5"], prev=["o_pe1"], dmas=2 * NW, dma=nm)

            def back(t):
                def turn(i):
                    for a in range(PAIRS):
                        mm = nc.tensor.transpose(PS[:, 3 + a // 4, (a % 4) * P:(a % 4 + 1) * P], sm[:, a, :, :].rearrange("p b k -> p (b k)"), self.ident[:, :])
                    return mm
                s.step("pe", f"pT_pe{t}", turn, after=[f"s_mul{t}", f"qk1_3"])
                s.step("act", f"pT{t}", lambda i: nc.scalar.activation(pT[:, :, :].rearrange("p a n -> p (a n)"), PS[:, 3:5, :].rearrange("p b n -> p (b n)"), ACT.Copy),
                       after=[f"pT_pe{t}"] + (["o_pe0"] if t else []), prev=[] if t else ["o_pe1"])

                def values(i):
                    for a in range(PAIRS):
                        for w in range(NW):
                            for half in range(2):
                                r = slice(half * HD, half * HD + HD)
                                mm = nc.tensor.matmul(PS[r, a // 4, (a % 4) * P + w * WIN:(a % 4) * P + (w + 1) * WIN], vw[r, t * NW + w, a * HD:(a + 1) * HD],
                                                      pT[r, a, w * WIN:(w + 1) * WIN], start=True, stop=True)
                    return mm
                s.step("pe", f"o_pe{t}", values, after=[f"pT{t}", "vlow", "vhigh", "raw1_3", "raw1_4", "raw1_5"] + (["oT0"] if t else []), solo=True)
                s.step("act", f"oT{t}", lambda i: nc.scalar.activation(oT[:, :, :].rearrange("p a n -> p (a n)"), PS[:, 0:2, :].rearrange("p b n -> p (b n)"), ACT.Copy),
                       after=[f"o_pe{t}"] + (["w_pe0"] if t else []), prev=[] if t else ["w_pe1"])
                s.step("pe", f"w_pe{t}", lambda i: [nc.tensor.matmul(PS[:, 2, t * P:t * P + P], oT[:, a, :], wo[:, a, :], start=(a == 0), stop=(a == PAIRS - 1))
                                                    for a in range(PAIRS)][-1], after=[f"oT{t}", "raw1_5"] + (["zn0"] if t else []), prev=[] if t else ["zn1"])
                s.step("dve", f"zn{t}", lambda i: nc.vector.tensor_tensor(zn[:, t, :], zs[:, t, :], PS[:, 2, t * P:t * P + P], ALU.add),
                       after=[f"w_pe{t}"], prev=["zput", "n_pe"])

            front(0)
            front(1)
            windows()
            scores(0)
            softmax(0)
            back_t0 = len(s.steps)
            scores(1)
            back(0)
            softmax(1)
            back(1)
            s.step("dve", "zput", lambda i: nc.vector.tensor_scalar(seq_tiles(Z, i), zn[:, :, :], 1.0, None, ALU.mult), after=["zn0", "zn1"])
            s.step("pe", "n_pe", lambda i: [nc.tensor.transpose(PS[:, 7, t * P:t * P + P], zn[:, t, :], self.ident[:, :]) for t in range(TILES)][-1],
                   after=["zn0", "zn1", "zTb"])
            s.step("act", "sTa", lambda i: nc.scalar.activation(sT[0:HD, 0:SEQ], PS[0:HD, 7, 0:SEQ], ACT.Copy), after=["n_pe"], prev=["cent"])
            s.step("act", "sTb", lambda i: nc.scalar.activation(sT[HD:P, 1:SEQ + 1], PS[HD:P, 7, 0:SEQ], ACT.Copy), after=["n_pe"], prev=["cent"])
            s.step("pe", "m_pe", lambda i: nc.tensor.matmul(PS[:, 7, 0:SEQ], mean[:, :], sT[:, 0:SEQ], start=True, stop=True), after=["sTa", "sTb"])
            s.step("dve", "cent", lambda i: nc.vector.tensor_tensor(xc[:, :], sT[:, 0:SEQ], PS[:, 7, 0:SEQ], ALU.subtract), after=["m_pe"], prev=["fn1"])
            s.step("dve", "xq", lambda i: nc.vector.tensor_tensor(xq[:, :], xc[:, :], xc[:, :], ALU.mult), after=["cent"], prev=["v_pe"])
            s.step("pe", "v_pe", lambda i: nc.tensor.matmul(PS[:, 7, 0:SEQ], mean[:, :], xq[:, :], start=True, stop=True), after=["xq"])
            s.step("act", "var", lambda i: nc.scalar.activation(rs[:, :], PS[:, 7, 0:SEQ], ACT.Ln, bias=self.eps[:, :]), after=["v_pe"], prev=["fn1"])
            s.step("act", "rstd", lambda i: nc.scalar.activation(rs[:, :], rs[:, :], ACT.Exp, scale=-0.5), after=["var"])
            s.step("dve", "fn1", lambda i: nc.vector.tensor_tensor(xc[:, :], xc[:, :], rs[:, :], ALU.mult), after=["rstd"])
            s.step("dve", "fn2", lambda i: nc.vector.tensor_scalar(fn[:, bass.ds(i * SEQ, SEQ)], xc[:, :], gb[:, 0:1], gb[:, 1:2], ALU.mult, ALU.add), after=["fn1"])
            s.run(NSEQ)

            s = self.stage()
            for c, (o, m) in enumerate(CHK):
                s.step("pe", f"g_pe{c}", lambda i, c=c, o=o, m=m: nc.tensor.matmul(PS[0:m, 3 + c, :], w1[:, DI + o:DI + o + m], fn[:, bass.ds(i * GRP, GRP)],
                                                                                   start=True, stop=True), prev=[f"gg{c}"])
                s.step("pe", f"a_pe{c}", lambda i, c=c, o=o, m=m: nc.tensor.matmul(PS[0:m, c, :], w1[:, o:o + m], fn[:, bass.ds(i * GRP, GRP)],
                                                                                   start=True, stop=True), prev=[f"hh{c}"])
                s.step("act", f"gg{c}", lambda i, c=c, m=m: nc.scalar.activation(gg[0:m, c, :], PS[0:m, 3 + c, :], ACT.Gelu, bias=b1[0:m, 1, c:c + 1]),
                       after=[f"g_pe{c}"], prev=[f"hh{c}"])
                s.step("dve", f"hh{c}", lambda i, c=c, m=m: nc.vector.scalar_tensor_tensor(hh[0:m, c, :], PS[0:m, c, :], b1[0:m, 0, c:c + 1], gg[0:m, c, :], ALU.add, ALU.mult),
                       after=[f"a_pe{c}", f"gg{c}"], prev=["o_pe"])
            s.step("pe", "o_pe", lambda i: [nc.tensor.matmul(PS[:, 6, t * P:t * P + P], hh[0:m, c, t * P:t * P + P], w2[0:m, c, :], start=(c == 0), stop=(c == 2))
                                            for t in range(GRP // P) for c, (o, m) in enumerate(CHK)][-1], after=["hh0", "hh1", "hh2"], prev=["z_out"])
            s.step("dve", "zb", lambda i: nc.vector.tensor_tensor(zb[:, :, :], Z[:, bass.ds(i * (GRP // P), GRP // P), :],
                                                                  b2[:, :].unsqueeze(1).broadcast_to((P, GRP // P, P)), ALU.add), prev=["z_out"])
            s.step("dve", "z_out", lambda i: nc.vector.tensor_tensor(Z[:, bass.ds(i * (GRP // P), GRP // P), :], zb[:, :, :],
                                                                     PS[:, 6, :].rearrange("p (t d) -> p t d", d=P), ALU.add), after=["zb", "o_pe"])
            s.run(NT * P // GRP)
        s = self.stage()
        s.step("dve", "sum", lambda i: nc.vector.tensor_tensor(Z[:, :, :], Z[:, :, :], X[:, :, :], ALU.add))
        s.run()


def constants():
    p = np.arange(P)
    c = {"c_ident": np.eye(P, dtype=np.float32)}
    c["c_causal"] = np.where(p[None, :] <= p[:, None], 0.0, NEG).astype(np.float32)
    c["c_causal01"] = (p[:, None] <= p[None, :]).astype(np.float32)
    c["c_head16"] = (p[:, None] // 8 == np.arange(16)[None, :]).astype(np.float32)
    c["c_head8"] = (p[:, None] // 16 == np.arange(8)[None, :]).astype(np.float32)
    q, k = p[:, None] % 32, np.arange(64)[None, :]
    seen = (k >= q) & (k <= q + 32)
    first = seen & ((p[:, None] >= 32) | (k >= 32))
    c["c_local"] = np.where(np.stack([first, seen], 1), 0.0, NEG).astype(np.float32)
    hd, win = 64, 32
    half = np.arange(0, hd, 2, dtype=np.float32)
    pos = np.arange(SEQ, dtype=np.float32)
    freqs = np.tile(pos[:, None] * (1.0 / 10000.0 ** (half / hd)).astype(np.float32)[None, :], (1, 2))
    power = ((pos - SEQ // 2) / (win // 2)).astype(np.float32)
    scale = np.tile(((half + 0.4 * hd) / (1.4 * hd)).astype(np.float32)[None, :] ** power[:, None], (1, 2))
    sign = np.where(np.arange(hd) < hd // 2, -1.0, 1.0).astype(np.float32)
    rot = np.stack([np.cos(freqs) * scale, np.sin(freqs) * scale * sign, np.cos(freqs) / scale, np.sin(freqs) / scale * sign], 1)
    c["c_rot"] = rot.reshape(TILES, P, 4, hd).swapaxes(0, 1).astype(np.float32)
    return c


def laid_out(x):
    def turn(a):
        return a.T

    def cols(n):
        return lambda a: a.reshape(n, -1, *a.shape[1:]).swapaxes(0, 1)

    def cols_t(n):
        return lambda a: a.T.reshape(n, -1, a.shape[0]).swapaxes(0, 1)

    how = {f"L{n}_attn_{w}": turn for n, ws in ((0, ("Wq", "Wk", "Wv", "Wp")), (1, ("Wq", "Wk", "Wv", "Wo")),
                                                  (2, ("Wq", "Wk", "Wv"))) for w in ws}
    how.update(L1_ffn_b1=cols(4), L2_ffn_Wq=turn, L2_ffn_routers=turn, L2_ffn_Wout_w=turn,
               L3_attn_in_proj_w=turn, L3_attn_x_proj_w=cols_t(2), L3_attn_dt_proj_w=turn,
               L3_attn_out_proj_w=cols_t(2), L3_attn_conv_w=cols(2), L3_attn_conv_b=cols(2), L3_attn_dt_proj_b=cols(2),
               L3_attn_A_log=cols(2), L3_attn_D=cols(2))
    return {(k + "_T" if k in how else k): how.get(k, lambda a: a)(np.asarray(v)) for k, v in x.items()
            if k != "L2_ffn_leaf_keys"}


def kernel(**inputs):
    import concourse.bacc as _bacc
    from concourse.bass_utils import run_bass_kernel_spmd as _run

    nc = _bacc.Bacc("TRN2", target_bir_lowering=False, num_devices=1)
    arrays, aps = {}, {}
    given = {k: np.ascontiguousarray(v) for k, v in laid_out(inputs).items()}
    for name, a in list(given.items()) + list(constants().items()):
        a = a.reshape(a.shape or (1,))
        arrays[f"in_{name}"] = a
        aps[name] = nc.dram_tensor(f"in_{name}", a.shape, mybir.dt.from_np(a.dtype), kind="ExternalInput").ap()
    out = nc.dram_tensor("out", (NSEQ, SEQ, P), F32, kind="ExternalOutput").ap()
    Kernel(nc, aps, out, ('L0', 'L1', 'L2', 'L3a', 'L3f')).build()
    r = _run(nc, [arrays], core_ids=[0])
    return r.results[0]["out"]
```

```python
import numpy as np
import concourse.bass as bass
from concourse import mybir
from contextlib import ExitStack

F32 = mybir.dt.float32
BF16 = mybir.dt.bfloat16
I32 = mybir.dt.int32
ALU = mybir.AluOpType
ACT = mybir.ActivationFunctionType
AX = mybir.AxisListType

P = 128
NSEQ, SEQ = 16, 256
TILES = SEQ // P
NT = NSEQ * TILES
EPS = 1e-5
NEG = -1e30
EXP_LN = "natural_log_exp_and_others"


class Stage:

    def __init__(self, nc, sems, dma_sems):
        self.nc, self.sems, self.dma_sems = nc, sems, dma_sems
        self.engines = {"pe": nc.tensor, "dve": nc.vector, "act": nc.scalar, "pool": nc.gpsimd, "sp": nc.sync}
        self.steps, self.names = [], set()

    def step(self, eng, name, fn, after=(), prev=(), dmas=0, dma="load", solo=False):
        assert name not in self.names, name
        self.names.add(name)
        self.steps.append((eng, name, fn, tuple(after), tuple(prev), dmas, dma, solo))

    def order(self, eng, names):
        place = {n: k for k, n in enumerate(names)}
        mine = sorted((s for s in self.steps if s[0] == eng), key=lambda s: place[s[1]])
        self.steps = mine + [s for s in self.steps if s[0] != eng]

    def sem(self, key):
        return self.sems[key] if key in self.sems else self.dma_sems[key]

    def run(self, turns=1, part=None, at=0, table=None):
        nc = self.nc
        steps = [s for s in self.steps if part is None or s[1] in part]
        mark, count = {}, {}
        for eng, name, _, _, _, dmas, dma, _ in steps:
            key, inc = (dma, 16 * dmas) if dmas else (eng, 1)
            count[key] = count.get(key, 0) + inc
            mark[name] = (key, count[key])
        if table:
            nc.scalar.preload_act_table_set(table)
        if turns == 1:
            self._write(steps, mark, count, None, at)
        else:
            for key, n in count.items():
                self.engines.get(key, nc.sync).sem_inc(self.sem(key), n)
            with nc.Fori(0, turns) as turn:
                self._write(steps, mark, count, turn, turn)
        for key, n in count.items():
            if key not in self.engines:
                nc.sync.wait_ge(self.sem(key), n * (turns + (turns > 1)))
        nc.all_engine_barrier()
        for key in count:
            nc.sync.sem_clear(self.sem(key))
        nc.all_engine_barrier()

    def _write(self, steps, mark, count, turn, at):
        seen = {}
        for eng, name, fn, after, prev, dmas, dma, solo in steps:
            e = self.engines[eng]
            need = {}
            for n in after:
                if n in mark:
                    key, v = mark[n]
                    need[key] = max(need.get(key, -1 << 30), v)
            if turn is not None:
                for n in prev:
                    key, v = mark[n]
                    need[key] = max(need.get(key, -1 << 30), v - count[key])
            waited = False
            for key, v in need.items():
                if seen.get((eng, key), -1 << 30) >= v:
                    continue
                seen[(eng, key)] = v
                n = count[key]
                e.wait_ge(self.sem(key), v if turn is None else turn * n + (v + n))
                waited = True
            if waited and solo and turn is not None:
                e.sem_inc(self.sems["spare_" + eng], 1)
            out = fn(at)
            if dmas:
                for d in out:
                    d.then_inc(self.sem(dma), 16)
            else:
                out.then_inc(self.sems[eng], 1)


def seq_tiles(ap, i):
    return ap[:, bass.ds(i * TILES, TILES), :]


def row(ap, n):
    return ap.rearrange("(a n) -> a n", a=1).broadcast_to((P, n))


class Kernel:
    def __init__(self, nc, d, out, stages):
        self.nc, self.d, self.out, self.stages = nc, d, out, stages

    def sb(self, name, shape, dt=F32):
        return self.ctx.enter_context(self.nc.sbuf_tensor(f"{self.tag}_{name}", shape, dt))

    def stage(self):
        return Stage(self.nc, self.sems, self.dma_sems)

    def build(self):
        nc, d = self.nc, self.d
        with ExitStack() as ctx:
            self.ctx, self.tag = ctx, "all"
            self.sems = {k: ctx.enter_context(nc.semaphore(f"done_{k}")) for k in ("pe", "dve", "act", "pool")}
            for k in ("pe", "dve", "act", "pool"):
                self.sems["spare_" + k] = ctx.enter_context(nc.semaphore(f"spare_{k}"))
            self.dma_sems = {k: ctx.enter_context(nc.semaphore(f"dma_{k}"))
                             for k in ("load", "vlow", "vhigh", "store", "w_attn", "w_ffn")}
            self.X = self.sb("x", [P, NT, P])
            self.Z = self.sb("z", [P, NSEQ, SEQ + 1])
            self.ident = self.sb("ident", [P, P])
            self.identb = self.sb("identb", [P, P], BF16)
            self.PS = ctx.enter_context(nc.psum_tensor("ps", [P, 8, 512], F32))
            self.eps = self.sb("eps", [P, 1])
            s = self.stage()
            s.step("sp", "x", lambda i: [nc.sync.dma_start(self.X[:, :, :], d["L0_attn_x"].rearrange("b (t p) d -> p (b t) d", p=P))], dmas=1)
            s.step("sp", "ident", lambda i: [nc.sync.dma_start(self.ident[:, :], d["c_ident"])], dmas=1, dma="store")
            s.step("dve", "identb", lambda i: nc.vector.tensor_copy(self.identb[:, :], self.ident[:, :]), after=["ident"])
            s.step("pool", "zero", lambda i: nc.gpsimd.memset(self.Z[:, :, :], 0.0))
            s.step("dve", "eps", lambda i: nc.vector.memset(self.eps[:, :], EPS))
            s.run()
            for k in self.stages:
                with ExitStack() as self.ctx:
                    self.tag = k
                    {"L0": self.L0, "L1": self.L1, "L2": self.L2, "L3a": self.L3a, "L3f": self.L3f}[k]()
            s = self.stage()
            s.step("sp", "out", lambda i: [nc.sync.dma_start(self.out.rearrange("b (t p) d -> p (b t) d", p=P), self.X[:, :, :])], dmas=1, dma="store")
            s.run()

    def layernorm(self, s, src, dst, name, after, prev=(), wprev=()):
        nc = self.nc
        st, mv, ls, rs = (self.sb(f"{name}_{n}", [P, TILES, w]) for n, w in (("st", 6), ("mv", 2), ("ls", 1), ("rs", 1)))
        for t in range(TILES):
            s.step("dve", f"{name}_st{t}", lambda i, t=t: nc.vector.bn_stats(st[:, t, :], src[:, t, :]),
                   after=after, prev=[f"{name}_mv{t}"])
            s.step("dve", f"{name}_mv{t}", lambda i, t=t: nc.vector.bn_aggr(mv[:, t, :], st[:, t, :]),
                   after=[f"{name}_st{t}"], prev=[f"{name}_out{t}"], solo=True)
        s.step("act", f"{name}_ln", lambda i: nc.scalar.activation(ls[:, :, 0], mv[:, :, 1], ACT.Ln, bias=self.eps[:, :]),
               after=[f"{name}_mv1"], prev=[f"{name}_rs"])
        s.step("act", f"{name}_rs", lambda i: nc.scalar.activation(rs[:, :, 0], ls[:, :, 0], ACT.Exp, scale=-0.5),
               after=[f"{name}_ln"], prev=["%s_out%d" % (name, TILES - 1)])
        for t in range(TILES):
            s.step("dve", f"{name}_out{t}", lambda i, t=t: nc.vector.tensor_scalar(
                dst[:, t, :], src[:, t, :], mv[:, t, 0:1], rs[:, t, :], ALU.subtract, ALU.mult),
                after=[f"{name}_rs"], prev=wprev)

    def L0(self):
        nc, d, PS, X = self.nc, self.d, self.PS, self.X
        H, HD = 16, 8
        G = 4
        wt = self.sb("wt", [P, 4, P])
        bqk = self.sb("bqk", [P, 2])
        bvp = self.sb("bvp", [P, 2, P])
        hmask = self.sb("hmask", [P, H])
        cmask = self.sb("cmask", [P, P])
        cmaskb = self.sb("cmaskb", [P, P], BF16)
        kb = self.sb("kb", [P, P], BF16)
        kf = self.sb("kf", [P, P])
        sc = self.sb("sc", [P, 2])
        rsc = self.sb("rsc", [P, 2])
        ssc = self.sb("ssc", [P, 1])
        fbias = self.sb("fbias", [P, P], BF16)
        kq = self.sb("kq", [P, P], BF16)
        vaug = self.sb("vaug", [P, TILES, H, HD + 1])
        qz = [self.sb(f"qz_{n}", [P, SEQ]) for n in ("p", "m", "r", "w")]

        def quantise(s, name, src, dst, w, scal, after, prev=(), first=None):
            xs, mg, r, t2 = (q[:, 0:w] for q in qz)
            s.step("dve", name + "0", lambda i: nc.vector.tensor_scalar(xs, src, scal, None, ALU.mult), after=after, prev=prev)
            s.step("dve", name + "1", lambda i: nc.vector.tensor_scalar(
                mg.bitcast(I32), xs.bitcast(I32), 0x7F800000, None, ALU.bitwise_and), after=[name + "0"])
            s.step("dve", name + "2", lambda i: nc.vector.tensor_scalar(
                mg, mg, 2.0 ** -6, 1.5 * 2.0 ** 20, ALU.max, ALU.mult), after=[name + "1"])
            s.step("dve", name + "3", lambda i: nc.vector.tensor_tensor(r, xs, mg, ALU.add), after=[name + "2"])
            s.step("dve", name + "4", lambda i: nc.vector.tensor_tensor(r, r, mg, ALU.subtract), after=[name + "3"])
            s.step("dve", name + "5", lambda i: nc.vector.tensor_tensor(t2, r, r, ALU.mult), after=[name + "4"])
            s.step("dve", name + "6", lambda i: nc.vector.tensor_scalar(
                t2, t2, 448.0 ** 2, -(448.0 ** 2), ALU.max, ALU.add), after=[name + "5"])
            s.step("dve", name + "7", lambda i: nc.vector.tensor_scalar(t2, t2, 2.0 ** 127, None, ALU.mult), after=[name + "6"])
            s.step("dve", name + "8", lambda i: nc.vector.tensor_tensor(t2, t2, t2, ALU.subtract), after=[name + "7"])
            s.step("dve", name + "9", lambda i: nc.vector.tensor_tensor(dst, r, t2, ALU.add), after=[name + "8"])

        s = self.stage()
        s.step("sp", "in", lambda i: [nc.sync.dma_start(wt[:, n, :], d["L0_attn_" + w + "_T"]) for n, w in enumerate(("Wq", "Wk", "Wv", "Wp"))]
               + [nc.sync.dma_start(bqk[:, n:n + 1], d["L0_attn_" + w].rearrange("(p a) -> p a", a=1)) for n, w in enumerate(("bq", "bk"))]
               + [nc.sync.dma_start(bvp[:, n, :], row(d["L0_attn_" + w], P)) for n, w in enumerate(("bv", "bp"))]
               + [nc.sync.dma_start(hmask[:, :], d["c_head16"]), nc.sync.dma_start(cmask[:, :], d["c_causal"]),
                  nc.sync.dma_start(kb[:, :], d["L0_ffn_kernel"]), nc.sync.dma_start(fbias[:, :], row(d["L0_ffn_bias"], P)),
                  nc.sync.dma_start(sc[:, 0:1], row(d["L0_ffn_input_scale"], 1)),
                  nc.sync.dma_start(sc[:, 1:2], row(d["L0_ffn_kernel_scale"], 1))], dmas=14)
        s.step("dve", "cmaskb", lambda i: nc.vector.tensor_copy(cmaskb[:, :], cmask[:, :]), after=["in"])
        s.step("dve", "kf", lambda i: nc.vector.tensor_copy(kf[:, :], kb[:, :]), after=["in"])
        s.step("dve", "rsc", lambda i: nc.vector.reciprocal(rsc[:, :], sc[:, :]), after=["in"])
        s.step("dve", "ssc", lambda i: nc.vector.tensor_tensor(ssc[:, :], sc[:, 0:1], sc[:, 1:2], ALU.mult), after=["in"])
        quantise(s, "kq", kf[:, :], kq[:, :], P, rsc[:, 1:2], ["kf", "rsc"])
        s.step("pool", "ones", lambda i: nc.gpsimd.memset(vaug[:, :, :, HD], 1.0))
        s.run()

        xs = self.sb("xs", [P, TILES, P])
        xn = self.sb("xn", [P, TILES, P])
        xnT = self.sb("xnT", [P, SEQ])
        xb = self.sb("xb", [P, SEQ], BF16)
        xq = self.sb("xq", [P, SEQ], BF16)
        yb = self.sb("yb", [P, TILES, P], BF16)
        qT = self.sb("qT", [P, SEQ])
        kT = self.sb("kT", [P, SEQ])
        qm = self.sb("qm", [P, H, SEQ])
        sm = self.sb("sm", [P, 2, G * SEQ])
        pT = self.sb("pT", [P, 2, G * SEQ])
        mx = self.sb("mx", [P, 2, G])
        ob = self.sb("ob", [P, TILES, H, HD])
        rl = self.sb("rl", [P, TILES, H])
        oT = self.sb("oT", [P, SEQ])

        s = self.stage()
        s.step("dve", "xs", lambda i: nc.vector.tensor_scalar(xs[:, :, :], seq_tiles(X, i), 1.0, None, ALU.mult), prev=["x_out"])
        self.layernorm(s, xs, xn, "ln", ["xs"], wprev=["xnT_pe"])
        s.step("pe", "xnT_pe", lambda i: [nc.tensor.transpose(PS[:, 4, t * P:t * P + P], xn[:, t, :], self.ident[:, :]) for t in range(TILES)][-1],
               after=["ln_out1"], prev=["oT"])
        s.step("act", "xnT", lambda i: nc.scalar.activation(xnT[:, :], PS[:, 4, 0:SEQ], ACT.Copy), after=["xnT_pe"], prev=["v_pe", "xb"])
        for n, (w, to, b) in enumerate((("q", qT, 0), ("k", kT, 1))):
            s.step("pe", w + "_pe", lambda i, n=n, b=b: nc.tensor.matmul(PS[:, b, 0:SEQ], wt[:, n, :], xnT[:, :], start=True, stop=True),
                   after=["xnT"], prev=["s_sub%d" % (2 * H // G - 2)])
            s.step("act", w, lambda i, n=n, to=to, b=b: nc.scalar.activation(to[:, :], PS[:, b, 0:SEQ], ACT.Identity, bias=bqk[:, n:n + 1]),
                   after=[w + "_pe"], prev=["qm15", "s_pe%d" % (2 * H // G - 1)])
        s.step("pe", "v_pe", lambda i: [nc.tensor.matmul(PS[:, 5, t * P:t * P + P], xnT[:, t * P:t * P + P], wt[:, 2, :], start=True, stop=True)
                                        for t in range(TILES)][-1], after=["xnT"], prev=["x_out"])
        for t in range(TILES):
            s.step("dve", f"v{t}", lambda i, t=t: nc.vector.tensor_tensor(
                vaug[:, t, :, 0:HD], PS[:, 5, t * P:t * P + P].rearrange("p (h e) -> p h e", e=HD),
                bvp[:, 0, :].rearrange("p (h e) -> p h e", e=HD), ALU.add), after=["v_pe"], prev=["o_pe%d" % (2 * H // G - 1)])
        for h in range(H):
            s.step("dve", f"qm{h}", lambda i, h=h: nc.vector.tensor_scalar(qm[:, h, :], qT[:, :], hmask[:, h:h + 1], None, ALU.mult),
                   after=["q"], prev=["s_pe%d" % (2 * H // G - 1)])

        units = [(qt, g) for g in range(H // G) for qt in range(TILES)]

        def view(t, qt):
            return t[:, 0:G * P * (qt + 1)].rearrange("p (h k) -> p h k", h=G)

        def bank(u, qt):
            b = 2 * (u % 2)
            return PS[:, b:b + 2, :].rearrange("p b k -> p (b k)") if qt else PS[:, b, :]

        def scores(u, qt, g):
            n = P * (qt + 1)

            def go(i):
                for h in range(G):
                    o = bank(u, qt)[:, h * n:h * n + n]
                    nc.tensor.matmul(o, qm[:, g * G + h, qt * P:qt * P + P], kT[:, 0:n], start=True, stop=False)
                    mm = nc.tensor.matmul(o[:, n - P:n], self.identb[:, :], cmaskb[:, :], start=False, stop=True)
                return mm
            s.step("pe", f"s_pe{u}", go, after=["k", f"qm{g * G + G - 1}"] + ([f"s_sub{u - 2}"] if u >= 2 else []) + ["q", "k"])

        def softmax(u, qt):
            n = P * (qt + 1)
            a = u % 2
            src = view(bank(u, qt), qt)
            sv = view(sm[:, a, :], qt)
            s.step("dve", f"s_max{u}", lambda i: nc.vector.tensor_reduce(mx[:, a, :], src, AX.X, ALU.max),
                   after=[f"s_pe{u}"] + ([f"s_sub{u - 2}"] if u >= 2 else []), prev=[f"s_sub{len(units) - 2 + a}"])
            s.step("dve", f"s_sub{u}", lambda i: nc.vector.tensor_tensor(
                sv, src, mx[:, a, :].unsqueeze(2).broadcast_to((P, G, n)), ALU.subtract),
                after=[f"s_max{u}"] + ([f"t_pe{u - 2}"] if u >= 2 else []), prev=[f"t_pe{len(units) - 2 + a}"])
            s.step("act", f"s_exp{u}", lambda i: nc.scalar.activation(
                sm[:, a, 0:G * n], sm[:, a, 0:G * n], ACT.Exp, scale=float(HD) ** -0.5), after=[f"s_sub{u}"])

        def turn(u, qt):
            n = P * (qt + 1)
            a = u % 2

            def go(i):
                for h in range(G):
                    for k in range(qt + 1):
                        c = h * (qt + 1) + k
                        mm = nc.tensor.transpose(PS[:, 4 + c // 4, (c % 4) * P:(c % 4 + 1) * P],
                                                 sm[:, a, h * n + k * P:h * n + k * P + P], self.ident[:, :])
                return mm
            s.step("pe", f"t_pe{u}", go, after=[f"s_exp{u}"] + ([f"t{u - 1}"] if u else ["v1", "xnT"]))
            s.step("act", f"t{u}", lambda i: nc.scalar.activation(
                pT[:, a, 0:G * n], PS[:, 4:6, :].rearrange("p b k -> p (b k)")[:, 0:G * n], ACT.Copy),
                after=[f"t_pe{u}"] + ([f"o_pe{u - 2}"] if u >= 2 else []), prev=[f"o_pe{len(units) - 2 + a}"])

        def output(u, qt, g):
            def go(i):
                for h in range(G):
                    hh = g * G + h
                    for k in range(qt + 1):
                        c = h * (qt + 1) + k
                        mm = nc.tensor.matmul(PS[:, 6 + qt, hh * (HD + 1):(hh + 1) * (HD + 1)], pT[:, u % 2, c * P:c * P + P],
                                              vaug[:, k, hh, :], start=(k == 0), stop=(k == qt))
                return mm
            s.step("pe", f"o_pe{u}", go, after=[f"t{u}", "v1"], prev=["ob1"])

        for n in range(len(units) + 2):
            if n < len(units):
                scores(n, *units[n])
                softmax(n, units[n][0])
            if 1 <= n <= len(units):
                turn(n - 1, units[n - 1][0])
            if n >= 2:
                output(n - 2, *units[n - 2])
        last = len(units) - 1
        s.step("dve", "xb", lambda i: nc.vector.tensor_copy(xb[:, :], xnT[:, :]), after=["xnT"], prev=["xq0"])
        quantise(s, "xq", xb[:, :], xq[:, :], SEQ, rsc[:, 0:1], ["xb"], prev=["y_pe"])
        for t in range(TILES):
            o = PS[:, 6 + t, 0:H * (HD + 1)].rearrange("p (h e) -> p h e", e=HD + 1)
            s.step("dve", f"rl{t}", lambda i, t=t, o=o: nc.vector.reciprocal(rl[:, t, :], o[:, :, HD]),
                   after=[f"o_pe{last}"], prev=[f"ob{t}"])
            s.step("dve", f"ob{t}", lambda i, t=t, o=o: nc.vector.tensor_tensor(
                ob[:, t, :, :], o[:, :, 0:HD], rl[:, t, :].unsqueeze(2).broadcast_to((P, H, HD)), ALU.mult),
                after=[f"rl{t}"], prev=["oT_pe"])
        s.step("pe", "oT_pe", lambda i: [nc.tensor.transpose(PS[:, 4, t * P:t * P + P], ob[:, t, :, :].rearrange("p h e -> p (h e)"),
                                                             self.ident[:, :]) for t in range(TILES)][-1], after=["ob1", f"t{last}"])
        s.step("act", "oT", lambda i: nc.scalar.activation(oT[:, :], PS[:, 4, 0:SEQ], ACT.Copy), after=["oT_pe"], prev=["p_pe"])
        s.step("pe", "p_pe", lambda i: [nc.tensor.matmul(PS[:, 5, t * P:t * P + P], oT[:, t * P:t * P + P], wt[:, 3, :], start=True, stop=True)
                                        for t in range(TILES)][-1], after=["oT", f"t{last}"])
        s.step("pe", "y_pe", lambda i: [nc.tensor.matmul(PS[:, 2, t * P:t * P + P], xq[:, t * P:t * P + P], kq[:, :], start=True, stop=True)
                                        for t in range(TILES)][-1], after=["xq9", f"s_sub{last}"])
        s.step("dve", "y0", lambda i: nc.vector.tensor_scalar(yb[:, :, :].rearrange("p t d -> p (t d)"), PS[:, 2, 0:SEQ], ssc[:, :], None, ALU.mult), after=["y_pe"])
        s.step("dve", "y1", lambda i: nc.vector.tensor_tensor(yb[:, :, :], yb[:, :, :], fbias[:, :].unsqueeze(1).broadcast_to((P, TILES, P)), ALU.add), after=["y0"])
        s.step("dve", "x1", lambda i: nc.vector.tensor_tensor(xs[:, :, :], xs[:, :, :], yb[:, :, :], ALU.add), after=["y1"])
        s.step("dve", "x2", lambda i: nc.vector.tensor_tensor(xs[:, :, :], xs[:, :, :], bvp[:, 1, :].unsqueeze(1).broadcast_to((P, TILES, P)), ALU.add), after=["x1"])
        s.step("dve", "x_out", lambda i: nc.vector.tensor_tensor(seq_tiles(X, i), xs[:, :, :], PS[:, 5, 0:SEQ].rearrange("p (t d) -> p t d", t=TILES), ALU.add),
               after=["x2", "p_pe"])
        s.run(NSEQ, table=EXP_LN)

    def L1(self):
        nc, d, PS, X = self.nc, self.d, self.PS, self.X
        H, HD = 8, 16
        FF, RANK = 512, 32
        FC = FF // P
        NB = 3
        wt = self.sb("wt", [P, 4, P])
        hmask = self.sb("hmask", [P, H])
        keep = self.sb("keep", [P, P])
        nw = self.sb("nw", [P, HD])
        u1 = self.sb("u1", [P, RANK])
        v1 = self.sb("v1", [RANK, FF])
        b1 = self.sb("b1", [P, FC])
        u2 = self.sb("u2", [P, FC, RANK])
        v2 = self.sb("v2", [RANK, P])
        b2 = self.sb("b2", [P, P])
        vaug = self.sb("vaug", [P, TILES, H, HD + 1])
        s = self.stage()
        s.step("sp", "in", lambda i: [nc.sync.dma_start(wt[:, n, :], d["L1_attn_" + w + "_T"]) for n, w in enumerate(("Wq", "Wk", "Wv", "Wo"))]
               + [nc.sync.dma_start(hmask[:, :], d["c_head8"]), nc.sync.dma_start(keep[:, :], d["c_causal01"]),
                  nc.sync.dma_start(nw[:, :], row(d["L1_attn_norm_w"], HD)), nc.sync.dma_start(u1[:, :], d["L1_ffn_U1"]),
                  nc.sync.dma_start(v1[:, :], d["L1_ffn_V1"]), nc.sync.dma_start(b1[:, :], d["L1_ffn_b1_T"]),
                  nc.sync.dma_start(u2[:, :, :], d["L1_ffn_U2"].rearrange("(c p) r -> p c r", p=P)),
                  nc.sync.dma_start(v2[:, :], d["L1_ffn_V2"]), nc.sync.dma_start(b2[:, :], row(d["L1_ffn_b2"], P))], dmas=13)
        s.step("pool", "ones", lambda i: nc.gpsimd.memset(vaug[:, :, :, HD], 1.0))
        s.run()

        xs = self.sb("xs", [P, TILES, P])
        xn = self.sb("xn", [P, TILES, P])
        xnT = self.sb("xnT", [P, SEQ])
        qT = self.sb("qT", [P, SEQ])
        kT = self.sb("kT", [P, SEQ])
        qm = self.sb("qm", [P, H, SEQ])
        sT = self.sb("sT", [P, H, NB, P])
        dn = self.sb("dn", [P, TILES, H])
        dr = self.sb("dr", [P, TILES, H])
        o1 = self.sb("o1", [P, TILES, H, HD])
        sq = self.sb("sq", [P, TILES, H, HD])
        ms = self.sb("ms", [P, TILES, H])
        oT = self.sb("oT", [P, SEQ])
        pr = self.sb("pr", [RANK, SEQ])
        hT = self.sb("hT", [P, FC, SEQ])
        qr = self.sb("qr", [RANK, SEQ])

        s = self.stage()
        s.step("dve", "xs", lambda i: nc.vector.tensor_scalar(xs[:, :, :], seq_tiles(X, i), 1.0, None, ALU.mult), prev=["x_out"])
        self.layernorm(s, xs, xn, "ln", ["xs"], wprev=["xnT_pe"])
        s.step("pe", "xnT_pe", lambda i: [nc.tensor.transpose(PS[:, 4, t * P:t * P + P], xn[:, t, :], self.ident[:, :]) for t in range(TILES)][-1],
               after=["ln_out1"], prev=["oT"])
        s.step("act", "xnT", lambda i: nc.scalar.activation(xnT[:, :], PS[:, 4, 0:SEQ], ACT.Copy), after=["xnT_pe"], prev=["v_pe", "pr_pe"])
        for n, (w, to) in enumerate((("q", qT), ("k", kT))):
            s.step("pe", w + "_pe", lambda i, n=n: nc.tensor.matmul(PS[:, 5, n * SEQ:(n + 1) * SEQ], wt[:, n, :], xnT[:, :], start=True, stop=True),
                   after=["xnT"], prev=["x_out"] if n == 0 else [])
            s.step("act", w, lambda i, n=n, to=to: nc.scalar.activation(to[:, :], PS[:, 5, n * SEQ:(n + 1) * SEQ], ACT.Copy),
                   after=["q_pe", "k_pe"], prev=["qm7", f"s_pe{H - 1}"])
        s.step("pe", "v_pe", lambda i: [nc.tensor.matmul(PS[:, 6, t * P:t * P + P], xnT[:, t * P:t * P + P], wt[:, 2, :], start=True, stop=True)
                                        for t in range(TILES)][-1], after=["xnT"], prev=["o1_1"])
        s.step("dve", "v", lambda i: nc.vector.tensor_copy(
            vaug[:, :, :, 0:HD], PS[:, 6, 0:SEQ].rearrange("p (t h e) -> p t h e", t=TILES, e=HD)), after=["v_pe"], prev=["o_pe"])
        for h in range(H):
            s.step("dve", f"qm{h}", lambda i, h=h: nc.vector.tensor_scalar(qm[:, h, :], qT[:, :], hmask[:, h:h + 1], None, ALU.mult),
                   after=["q"], prev=[f"s_pe{h}"])
        for h in range(H):
            b = h % 4

            def scores(i, h=h, b=b):
                nc.tensor.matmul(PS[:, b, 0:SEQ], kT[:, 0:P], qm[:, h, :], start=True, stop=True)
                return nc.tensor.matmul(PS[:, b, SEQ:SEQ + P], kT[:, P:SEQ], qm[:, h, P:SEQ], start=True, stop=True)
            s.step("pe", f"s_pe{h}", scores, after=["k", f"qm{h}"] + ([f"sd{h - 4}", f"sf{h - 4}"] if h >= 4 else []),
                   prev=[f"sd{h + 4}", f"sf{h + 4}", "pr", "gelu3"] if h < 4 else [])
            s.step("dve", f"sd{h}", lambda i, h=h, b=b: nc.vector.tensor_tensor(
                sT[:, h, 0:NB:2, :], PS[:, b, 0:NB * P].rearrange("p (n q) -> p n q", q=P)[:, 0:NB:2, :],
                keep[:, :].unsqueeze(1).broadcast_to((P, 2, P)), ALU.mult), after=[f"s_pe{h}"], prev=["o_pe"])
            s.step("act", f"sf{h}", lambda i, h=h, b=b: nc.scalar.activation(sT[:, h, 1, :], PS[:, b, P:SEQ], ACT.Copy),
                   after=[f"sd{h}"], prev=["o_pe"])

        def out(i):
            for t in range(TILES):
                for h in range(H):
                    o = PS[:, 6 + t, h * (HD + 1):(h + 1) * (HD + 1)]
                    if t == 0:
                        mm = nc.tensor.matmul(o, sT[:, h, 0, :], vaug[:, 0, h, :], start=True, stop=True)
                    else:
                        nc.tensor.matmul(o, sT[:, h, 1, :], vaug[:, 0, h, :], start=True, stop=False)
                        mm = nc.tensor.matmul(o, sT[:, h, 2, :], vaug[:, 1, h, :], start=False, stop=True)
            return mm
        s.step("pe", "o_pe", out, after=["v"] + [f"{x}{h}" for x in ("sd", "sf") for h in range(H)], prev=["o1_1"])
        s.step("pe", "pr_pe", lambda i: nc.tensor.matmul(PS[0:RANK, 0, 0:SEQ], u1[:, :], xnT[:, :], start=True, stop=True), after=["xnT", "sd4", "sf4"])
        s.step("dve", "pr", lambda i: nc.vector.tensor_copy(pr[:, :], PS[0:RANK, 0, 0:SEQ]), after=["pr_pe"], prev=["h_pe3"])
        for c in range(FC):
            s.step("pe", f"h_pe{c}", lambda i, c=c: nc.tensor.matmul(PS[:, (1, 2, 3, 0)[c], 0:SEQ], v1[:, c * P:c * P + P], pr[:, :], start=True, stop=True),
                   after=["pr", "sd7", "sf7", "sd6", "sf6", "sd5", "sf5"])
        for t in range(TILES):
            o = PS[:, 6 + t, 0:H * (HD + 1)].rearrange("p (h e) -> p h e", e=HD + 1)
            s.step("dve", f"dr{t}", lambda i, t=t, o=o: nc.vector.tensor_copy(dr[:, t, :], o[:, :, HD]), after=["o_pe"], prev=[f"dn{t}"])
            s.step("dve", f"dn{t}", lambda i, t=t: nc.vector.scalar_tensor_tensor(dn[:, t, :], dr[:, t, :], -1.0, dr[:, t, :], ALU.mult, ALU.max),
                   after=[f"dr{t}"], prev=["o1_1"])
        s.step("dve", "dm", lambda i: nc.vector.tensor_scalar(dn[:, :, :], dn[:, :, :], 1.0, None, ALU.max), after=["dn0", "dn1"])
        s.step("dve", "di", lambda i: nc.vector.reciprocal(dn[:, :, :], dn[:, :, :]), after=["dm"])
        for t in range(TILES):
            o = PS[:, 6 + t, 0:H * (HD + 1)].rearrange("p (h e) -> p h e", e=HD + 1)
            s.step("dve", f"o1_{t}", lambda i, t=t, o=o: nc.vector.tensor_tensor(
                o1[:, t, :, :], o[:, :, 0:HD], dn[:, t, :].unsqueeze(2).broadcast_to((P, H, HD)), ALU.mult), after=["di"], prev=["oT_pe"])
        s.step("dve", "sq", lambda i: nc.vector.tensor_tensor(sq[:, :, :, :], o1[:, :, :, :], o1[:, :, :, :], ALU.mult), after=["o1_1"], prev=["ms"])
        s.step("dve", "ms", lambda i: nc.vector.tensor_reduce(ms[:, :, :], sq[:, :, :, :], AX.X, ALU.add), after=["sq"], prev=["o2"])
        s.step("act", "ms_ln", lambda i: nc.scalar.activation(ms[:, :, :], ms[:, :, :], ACT.Ln, bias=self.eps[:, :], scale=1.0 / HD), after=["ms"])
        s.step("act", "ms_rs", lambda i: nc.scalar.activation(ms[:, :, :], ms[:, :, :], ACT.Exp, scale=-0.5), after=["ms_ln"])
        s.step("dve", "o2", lambda i: nc.vector.tensor_tensor(
            o1[:, :, :, :].rearrange("p t h e -> p (t h) e"), o1[:, :, :, :].rearrange("p t h e -> p (t h) e"),
            ms[:, :, :].rearrange("p t h -> p (t h)").unsqueeze(2).broadcast_to((P, TILES * H, HD)), ALU.mult), after=["ms_rs"])
        s.step("dve", "o3", lambda i: nc.vector.tensor_tensor(
            o1[:, :, :, :].rearrange("p t h e -> p (t h) e"), o1[:, :, :, :].rearrange("p t h e -> p (t h) e"),
            nw[:, :].unsqueeze(1).broadcast_to((P, TILES * H, HD)), ALU.mult), after=["o2"])
        s.step("pe", "oT_pe", lambda i: [nc.tensor.transpose(PS[:, 4, t * P:t * P + P], o1[:, t, :, :].rearrange("p h e -> p (h e)"),
                                                             self.ident[:, :]) for t in range(TILES)][-1], after=["o3", "xnT"])
        s.step("act", "oT", lambda i: nc.scalar.activation(oT[:, :], PS[:, 4, 0:SEQ], ACT.Copy), after=["oT_pe"], prev=["p_pe"])
        def gelu(i, c):
            op = nc.scalar.activation(hT[:, c, :], PS[:, (1, 2, 3, 0)[c], 0:SEQ], ACT.Gelu_apprx_tanh, bias=b1[:, c:c + 1])
            if c == FC - 1:
                nc.scalar.preload_act_table_set(EXP_LN)
            return op
        for c in range(FC):
            s.step("act", f"gelu{c}", lambda i, c=c: gelu(i, c),
                   after=[f"h_pe{c}"], prev=["qr_pe"])
        s.step("pe", "qr_pe", lambda i: [nc.tensor.matmul(PS[0:RANK, 4, SEQ:2 * SEQ], u2[:, c, :], hT[:, c, :], start=(c == 0), stop=(c == FC - 1))
                                         for c in range(FC)][-1], after=["gelu3", "oT"], prev=["qr"])
        s.step("dve", "qr", lambda i: nc.vector.tensor_copy(qr[:, :], PS[0:RANK, 4, SEQ:2 * SEQ]), after=["qr_pe", "oT"], prev=["p_pe"])

        def back(i):
            for t in range(TILES):
                nc.tensor.matmul(PS[:, 5, t * P:t * P + P], oT[:, t * P:t * P + P], wt[:, 3, :], start=True, stop=True)
            for t in range(TILES):
                mm = nc.tensor.matmul(PS[:, 5, SEQ + t * P:SEQ + t * P + P], qr[:, t * P:t * P + P], v2[:, :], start=True, stop=True)
            return mm
        s.step("pe", "p_pe", back, after=["oT", "qr", "q", "k"])
        s.step("dve", "x1", lambda i: nc.vector.tensor_tensor(xs[:, :, :], xs[:, :, :], b2[:, :].unsqueeze(1).broadcast_to((P, TILES, P)), ALU.add), after=["ln_out1"])
        s.step("dve", "x2", lambda i: nc.vector.tensor_tensor(xs[:, :, :], xs[:, :, :], PS[:, 5, 0:SEQ].rearrange("p (t d) -> p t d", t=TILES), ALU.add), after=["x1", "p_pe"])
        s.step("dve", "x_out", lambda i: nc.vector.tensor_tensor(seq_tiles(X, i), xs[:, :, :], PS[:, 5, SEQ:2 * SEQ].rearrange("p (t d) -> p t d", t=TILES), ALU.add), after=["x2"])
        s.run(NSEQ, table=EXP_LN)

    def L2(self):
        nc, d, PS, X = self.nc, self.d, self.PS, self.X
        H, R = 8, 64
        G = 4
        PAIRS = H // 2
        LEAVES, DEPTH = 256, 8
        wq = self.sb("wq", [P, H * R])
        wk = self.sb("wk", [P, H * R])
        wv = self.sb("wv", [P, H * P])
        fq = self.sb("fq", [P, P])
        rt = self.sb("rt", [P, LEAVES - 1])
        lv = self.sb("lv", [P, 2, P])
        wo = self.sb("wo", [P, P])
        bo = self.sb("bo", [P, P])
        qz = self.sb("qz", [P, H, SEQ])
        s = self.stage()
        s.step("sp", "in", lambda i: [nc.sync.dma_start(wq[:, :], d["L2_attn_Wq_T"]), nc.sync.dma_start(wk[:, :], d["L2_attn_Wk_T"]),
                                      nc.sync.dma_start(wv[:, :], d["L2_attn_Wv_T"]), nc.sync.dma_start(fq[:, :], d["L2_ffn_Wq_T"]),
                                      nc.sync.dma_start(rt[:, :], d["L2_ffn_routers_T"]),
                                      nc.sync.dma_start(lv[:, :, :], d["L2_ffn_leaf_values"].rearrange("(c p) d -> p c d", p=P)),
                                      nc.sync.dma_start(wo[:, :], d["L2_ffn_Wout_w_T"]), nc.sync.dma_start(bo[:, :], row(d["L2_ffn_Wout_b"], P))], dmas=8)
        s.step("pool", "zero", lambda i: nc.gpsimd.memset(qz[:, :, :], 0.0))
        s.run()

        xs = self.sb("xs", [P, TILES, P])
        xn = self.sb("xn", [P, TILES, P])
        xnT = self.sb("xnT", [P, SEQ])
        kT = self.sb("kT", [P, PAIRS, SEQ])
        v = self.sb("v", [P, TILES, H * P])
        sm = self.sb("sm", [P, 2, G, SEQ])
        pn = self.sb("pn", [P, 2, G, SEQ])
        pT = self.sb("pT", [P, 2, G * SEQ])
        mx = self.sb("mx", [P, 2, G])
        sl = self.sb("sl", [P, 2, G])
        fqT = self.sb("fqT", [P, SEQ])
        gt = self.sb("gt", [P, TILES, LEAVES])
        gl = self.sb("gl", [P, TILES, LEAVES])
        lp = [self.sb(f"lp{n}", [P, TILES, LEAVES]) for n in range(2)]
        lpT = self.sb("lpT", [P, 2, SEQ])
        rT = self.sb("rT", [P, SEQ])

        s = self.stage()
        s.step("dve", "xs", lambda i: nc.vector.tensor_scalar(xs[:, :, :], seq_tiles(X, i), 1.0, None, ALU.mult), prev=["x_out"])
        self.layernorm(s, xs, xn, "ln", ["xs"], wprev=["xnT_pe"])
        s.step("pe", "xnT_pe", lambda i: [nc.tensor.transpose(PS[:, 4, t * P:t * P + P], xn[:, t, :], self.ident[:, :]) for t in range(TILES)][-1],
               after=["ln_out1"], prev=["lpT"])
        s.step("act", "xnT", lambda i: nc.scalar.activation(xnT[:, :], PS[:, 4, 0:SEQ], ACT.Copy), after=["xnT_pe"], prev=["v_pe1", "fq_pe"])
        for b in range(2):
            s.step("pe", f"q_pe{b}", lambda i, b=b: [nc.tensor.matmul(PS[:, b, c * SEQ:(c + 1) * SEQ], wq[:, (2 * b + c) * P:(2 * b + c + 1) * P], xnT[:, :],
                                                                      start=True, stop=True) for c in range(2)][-1], after=["xnT"], prev=["s_sub2", "s_sub3"])
            for half in range(2):
                r = slice(half * R, half * R + R)
                s.step("act", f"q{b}{half}", lambda i, b=b, half=half, r=r: nc.scalar.activation(
                    qz[r, 4 * b + half:4 * b + half + 3:2, :], PS[r, b, :].rearrange("p (c n) -> p c n", c=2), ACT.Copy),
                    after=[f"q_pe{b}"], prev=["s_pe3"])
        for b in range(2):
            s.step("pe", f"k_pe{b}", lambda i, b=b: [nc.tensor.matmul(PS[:, 2 + b, c * SEQ:(c + 1) * SEQ], wk[:, (2 * b + c) * P:(2 * b + c + 1) * P], xnT[:, :],
                                                                      start=True, stop=True) for c in range(2)][-1], after=["xnT"], prev=["s_sub3"])
            s.step("act", f"k{b}", lambda i, b=b: nc.scalar.activation(
                kT[:, 2 * b:2 * b + 2, :], PS[:, 2 + b, :].rearrange("p (c n) -> p c n", c=2), ACT.Copy), after=[f"k_pe{b}"], prev=["s_pe3"])
        for t in range(TILES):
            s.step("pe", f"v_pe{t}", lambda i, t=t: [nc.tensor.matmul(PS[:, 4 + 2 * t + c, :], xnT[:, t * P:t * P + P], wv[:, c * 512:(c + 1) * 512],
                                                                      start=True, stop=True) for c in range(2)][-1], after=["xnT"],
                   prev=["rT"] if t == 0 else ["x_out"])
            s.step("dve", f"v{t}", lambda i, t=t: nc.vector.tensor_copy(v[:, t, :], PS[:, 4 + 2 * t:6 + 2 * t, :].rearrange("p b n -> p (b n)")),
                   after=[f"v_pe{t}"], prev=["o_pe3"])
        s.step("pe", "fq_pe", lambda i: nc.tensor.matmul(PS[:, 4, 0:SEQ], fq[:, :], xnT[:, :], start=True, stop=True), after=["v0"])
        s.step("act", "fqT", lambda i: nc.scalar.activation(fqT[:, :], PS[:, 4, 0:SEQ], ACT.Copy), after=["fq_pe"], prev=["g_pe"])

        units = [(qt, g) for qt in range(TILES) for g in range(H // G)]

        def bank(u):
            b = 2 * (u % 2)
            return PS[:, b:b + 2, :].rearrange("p b (h k) -> p (b h) k", h=2)

        def scores(u, qt, g):
            def go(i):
                for h in range(G):
                    hh = g * G + h
                    mm = nc.tensor.matmul(bank(u)[:, h, :], qz[:, hh, qt * P:qt * P + P], kT[:, hh // 2, :], start=True, stop=True)
                return mm
            s.step("pe", f"s_pe{u}", go, after=["q11", "q10", "k1"] + ([f"s_sub{u - 2}"] if u >= 2 else []))

        def softmax(u):
            a = u % 2
            old = [f"s_sub{u - 2}"] if u >= 2 else []
            s.step("dve", f"s_max{u}", lambda i: nc.vector.tensor_reduce(mx[:, a, :], bank(u), AX.X, ALU.max),
                   after=[f"s_pe{u}"] + old, prev=[f"s_sub{2 + a}"])
            s.step("dve", f"s_sub{u}", lambda i: nc.vector.tensor_tensor(
                sm[:, a, :, :], bank(u), mx[:, a, :].unsqueeze(2).broadcast_to((P, G, SEQ)), ALU.subtract),
                after=[f"s_max{u}"] + ([f"s_mul{u - 2}"] if u >= 2 else []), prev=[f"s_mul{2 + a}"])
            s.step("act", f"s_exp{u}", lambda i: nc.scalar.activation(sm[:, a, :, :], sm[:, a, :, :], ACT.Exp), after=[f"s_sub{u}"])
            s.step("dve", f"s_sum{u}", lambda i: nc.vector.tensor_reduce(sl[:, a, :], sm[:, a, :, :], AX.X, ALU.add),
                   after=[f"s_exp{u}"] + ([f"s_mul{u - 2}"] if u >= 2 else []), prev=[f"s_mul{2 + a}"])
            s.step("dve", f"s_inv{u}", lambda i: nc.vector.reciprocal(sl[:, a, :], sl[:, a, :]), after=[f"s_sum{u}"])
            s.step("dve", f"s_mul{u}", lambda i: nc.vector.tensor_tensor(
                pn[:, a, :, :], sm[:, a, :, :], sl[:, a, :].unsqueeze(2).broadcast_to((P, G, SEQ)), ALU.mult),
                after=[f"s_inv{u}"] + ([f"t_pe{u - 2}"] if u >= 2 else []), prev=[f"t_pe{2 + a}"])

        def turn(u):
            a = u % 2

            def go(i):
                for c in range(2 * G):
                    mm = nc.tensor.transpose(PS[:, 4 + c // 4, (c % 4) * P:(c % 4 + 1) * P],
                                             pn[:, a, c // 2, (c % 2) * P:(c % 2) * P + P], self.ident[:, :])
                return mm
            s.step("pe", f"t_pe{u}", go, after=[f"s_mul{u}"] + ([f"t{u - 1}"] if u else ["v0", "fqT", "ge"]))
            s.step("act", f"t{u}", lambda i: nc.scalar.activation(pT[:, a, :], PS[:, 4:6, :].rearrange("p b k -> p (b k)"), ACT.Copy),
                   after=[f"t_pe{u}"] + ([f"o_pe{u - 2}"] if u >= 2 else []), prev=[f"o_pe{2 + a}"])

        def output(u, qt, g):
            def go(i):
                for c in range(2 * G):
                    hh, k = g * G + c // 2, c % 2
                    mm = nc.tensor.matmul(PS[:, 6 + qt, 0:P], pT[:, u % 2, c * P:c * P + P], v[:, k, hh * P:(hh + 1) * P],
                                          start=(g == 0 and c == 0), stop=False)
                return mm
            s.step("pe", f"o_pe{u}", go, after=[f"t{u}", "v1"])

        def gate():
            s.step("pe", "g_pe", lambda i: [nc.tensor.matmul(PS[:, 5, t * SEQ:t * SEQ + LEAVES - 1], fqT[:, t * P:t * P + P], rt[:, :], start=True, stop=True)
                                            for t in range(TILES)][-1], after=["fqT", "v0"])
            s.step("act", "ge", lambda i: nc.scalar.activation(gt[:, :, 0:LEAVES - 1], PS[:, 5, :].rearrange("p (t n) -> p t n", t=TILES)[:, :, 0:LEAVES - 1],
                                                               ACT.Exp, scale=-1.0), after=["g_pe"], prev=["lv7"])
            s.step("dve", "g1", lambda i: nc.vector.tensor_scalar(gt[:, :, 0:LEAVES - 1], gt[:, :, 0:LEAVES - 1], 1.0, None, ALU.add), after=["ge"])
            s.step("dve", "g2", lambda i: nc.vector.reciprocal(gt[:, :, 0:LEAVES - 1], gt[:, :, 0:LEAVES - 1]), after=["g1"])
            s.step("pool", "g3", lambda i: nc.gpsimd.tensor_scalar(gl[:, :, 0:LEAVES - 1], gt[:, :, 0:LEAVES - 1], -1.0, 1.0, ALU.mult, ALU.add),
                   after=["g2"], prev=["lv7"], solo=True)
            for lev in range(DEPTH):
                n = 2 ** lev
                src = lp[lev % 2][:, :, 0:n]
                dst = lp[(lev + 1) % 2][:, :, 0:2 * n].rearrange("p t (n two) -> p t n two", two=2)

                def both(i, n=n, src=src, dst=dst):
                    for side, g in ((0, gl), (1, gt)):
                        if n == 1:
                            op = nc.gpsimd.tensor_copy(dst[:, :, :, side], g[:, :, 0:1])
                        else:
                            op = nc.gpsimd.tensor_tensor(dst[:, :, :, side], src, g[:, :, n - 1:2 * n - 1], ALU.mult)
                    return op
                s.step("pool", f"lv{lev}", both, after=["g3"] if lev == 0 else [f"lv{lev - 1}"], prev=["lpT_pe"], solo=True)

        for n in range(len(units) + 2):
            if n < len(units):
                scores(n, *units[n])
                softmax(n)
            if n == 0:
                gate()
            if 1 <= n <= len(units):
                turn(n - 1)
            if n >= 2:
                output(n - 2, *units[n - 2])
        leaf = lp[DEPTH % 2]
        s.step("pe", "lpT_pe", lambda i: [nc.tensor.transpose(PS[:, 4, (c * 2 + t) * P:(c * 2 + t + 1) * P], leaf[:, t, c * P:c * P + P], self.ident[:, :])
                                          for c in range(2) for t in range(TILES)][-1], after=["lv7", "t3"])
        s.step("act", "lpT", lambda i: nc.scalar.activation(lpT[:, :, :].rearrange("p c n -> p (c n)"), PS[:, 4, :], ACT.Copy), after=["lpT_pe"], prev=["rT_pe"])
        s.step("pe", "rT_pe", lambda i: [nc.tensor.matmul(PS[:, 5, 0:SEQ], lv[:, c, :], lpT[:, c, :], start=(c == 0), stop=(c == 1)) for c in range(2)][-1],
               after=["lpT"])
        s.step("act", "rT", lambda i: nc.scalar.activation(rT[:, :], PS[:, 5, 0:SEQ], ACT.Copy), after=["rT_pe"], prev=["w_pe"])
        s.step("pe", "w_pe", lambda i: [nc.tensor.matmul(PS[:, 6 + t, 0:P], rT[:, t * P:t * P + P], wo[:, :], start=False, stop=True) for t in range(TILES)][-1],
               after=["rT"])
        s.step("dve", "x1", lambda i: nc.vector.tensor_tensor(xs[:, :, :], xs[:, :, :], bo[:, :].unsqueeze(1).broadcast_to((P, TILES, P)), ALU.add), after=["ln_out1"])
        s.step("dve", "x_out", lambda i: nc.vector.tensor_tensor(seq_tiles(X, i), xs[:, :, :], PS[:, 6:8, 0:P], ALU.add), after=["x1", "w_pe"])
        s.run(NSEQ, table=EXP_LN)

    def L3a(self):
        nc, d, PS, X, Z = self.nc, self.d, self.PS, self.X, self.Z
        CH, NS, TAPS, DR = 2, 16, 4, 8
        G = 4
        UN = NS // G
        PAD = TAPS - 1
        pre = "L3_attn_"
        lg = self.sb("lg", [P, 2])
        wi = self.sb("wi", [P, 4 * P])
        wx = self.sb("wx", [P, CH, DR + 2 * NS])
        wd = self.sb("wd", [P, CH * P])
        wo = self.sb("wo", [P, CH, P])
        cw = self.sb("cw", [P, CH, TAPS])
        cb, db, dd = (self.sb(n, [P, CH]) for n in ("cb", "db", "dd"))
        al = self.sb("al", [P, CH, NS])
        na = self.sb("na", [P, CH, NS])
        res = self.sb("res", [P, 1])
        xd = self.sb("xd", [P, SEQ])
        xp = self.sb("xp", [P, CH, PAD + SEQ])
        dA = self.sb("dA", [P, CH, G, SEQ])
        s = self.stage()
        s.step("pool", "z0", lambda i: nc.gpsimd.memset(wd[:, :], 0.0))
        s.step("pool", "z1", lambda i: nc.gpsimd.memset(xd[:, :], 0.0))
        s.step("pool", "z2", lambda i: nc.gpsimd.memset(xp[:, :, :], 0.0))
        s.step("pool", "z3", lambda i: nc.gpsimd.memset(dA[:, :, :, :], 0.0))
        s.step("sp", "in", lambda i: [
            nc.sync.dma_start(lg[:, 0:1], d[pre + "ln_g"].rearrange("(p a) -> p a", a=1)),
            nc.sync.dma_start(lg[:, 1:2], d[pre + "ln_b"].rearrange("(p a) -> p a", a=1)),
            nc.sync.dma_start(wi[:, :], d[pre + "in_proj_w_T"]), nc.sync.dma_start(wx[:, :, :], d[pre + "x_proj_w_T"]),
            nc.sync.dma_start(wd[0:DR, :], d[pre + "dt_proj_w_T"]), nc.sync.dma_start(wo[:, :, :], d[pre + "out_proj_w_T"]),
            nc.sync.dma_start(cw[:, :, :], d[pre + "conv_w_T"]), nc.sync.dma_start(cb[:, :], d[pre + "conv_b_T"]),
            nc.sync.dma_start(db[:, :], d[pre + "dt_proj_b_T"]), nc.sync.dma_start(dd[:, :], d[pre + "D_T"]),
            nc.sync.dma_start(al[:, :, :], d[pre + "A_log_T"]), nc.sync.dma_start(res[:, :], row(d[pre + "res_scale"], 1))],
            after=["z0"], dmas=12)
        s.step("act", "ea", lambda i: nc.scalar.activation(na[:, :, :], al[:, :, :], ACT.Exp), after=["in"])
        s.step("dve", "na", lambda i: nc.vector.tensor_scalar(na[:, :, :], na[:, :, :], -1.0, None, ALU.mult), after=["ea"])
        s.run()

        xs = self.sb("xs", [P, TILES, P])
        xn = self.sb("xn", [P, TILES, P])
        xm = self.sb("xm", [P, TILES, P])
        xmT = self.sb("xmT", [P, SEQ])
        zs = self.sb("zs", [P, CH, SEQ])
        zg = self.sb("zg", [P, CH, SEQ])
        xc = self.sb("xc", [P, CH, SEQ])
        xg = self.sb("xg", [P, CH, SEQ])
        dv = self.sb("dv", [P, CH, SEQ])
        de = self.sb("de", [P, CH, SEQ])
        dt = self.sb("dt", [P, CH, SEQ])
        dx = self.sb("dx", [P, CH, SEQ])
        db_x = self.sb("db_x", [P, CH, G, SEQ])
        hs = self.sb("hs", [P, CH, G, SEQ])
        hc = self.sb("hc", [P, CH, G, SEQ])
        yT = self.sb("yT", [P, CH, SEQ])

        def flat(t):
            return t.rearrange("p g n -> p (g n)")

        s = self.stage()
        s.step("dve", "xs", lambda i: nc.vector.tensor_scalar(xs[:, :, :], seq_tiles(X, i), 1.0, None, ALU.mult), prev=["x_out"])
        self.layernorm(s, xs, xn, "ln", ["xs"], wprev=["lm_out1", "z_pe", "x1"])
        s.step("pe", "z_pe", lambda i: [nc.tensor.transpose(PS[:, 5, SEQ + t * P:SEQ + t * P + P], xn[:, t, :], self.ident[:, :]) for t in range(TILES)][-1],
               after=["ln_out1"], prev=["x_out"])

        def z_put(i):
            for r, c in ((slice(0, P // 2), 0), (slice(P // 2, P), 1)):
                op = nc.vector.tensor_scalar(Z[r, bass.ds(i, 1), c:c + SEQ], PS[r, 5, SEQ:2 * SEQ].unsqueeze(1), 1.0, None, ALU.mult)
            return op
        s.step("dve", "z_put", z_put, after=["z_pe"])
        self.layernorm(s, xn, xm, "lm", ["ln_out0", "ln_out1"], wprev=["xmT_pe"])
        s.step("pe", "xmT_pe", lambda i: [nc.tensor.transpose(PS[:, 4, t * P:t * P + P], xm[:, t, :], self.ident[:, :]) for t in range(TILES)][-1],
               after=["lm_out1"], prev=["dv1", "xmT"])
        s.step("act", "xmT", lambda i: nc.scalar.activation(xmT[:, :], PS[:, 4, 0:SEQ], ACT.Identity, bias=lg[:, 1:2], scale=lg[:, 0:1]),
               after=["xmT_pe"], prev=["in_pe1"])
        for b in range(2):
            s.step("pe", f"in_pe{b}", lambda i, b=b: [nc.tensor.matmul(PS[:, b, c * SEQ:(c + 1) * SEQ], wi[:, (2 * b + c) * P:(2 * b + c + 1) * P], xmT[:, :],
                                                                       start=True, stop=True) for c in range(2)][-1], after=["xmT"], prev=[f"dbx{UN - 1}1"])
        s.step("act", "xp", lambda i: nc.scalar.activation(xp[:, :, PAD:PAD + SEQ], PS[:, 0, :].rearrange("p (c n) -> p c n", c=CH), ACT.Copy),
               after=["in_pe0"], prev=[f"cv{PAD}1"])
        s.step("act", "ze", lambda i: nc.scalar.activation(zg[:, :, :], PS[:, 1, :].rearrange("p (c n) -> p c n", c=CH), ACT.Exp, scale=-1.0),
               after=["in_pe1"], prev=["z_s"])
        for c in range(CH):
            s.step("dve", f"cv0{c}", lambda i, c=c: nc.vector.tensor_scalar(xc[:, c, :], xp[:, c, 0:SEQ], cw[:, c, 0:1], cb[:, c:c + 1], ALU.mult, ALU.add),
                   after=["xp"], prev=["y1%d" % c, "xd_pe"])
        for k in range(1, TAPS):
            for c in range(CH):
                s.step("dve", f"cv{k}{c}", lambda i, c=c, k=k: nc.vector.scalar_tensor_tensor(
                    xc[:, c, :], xp[:, c, k:k + SEQ], cw[:, c, k:k + 1], xc[:, c, :], ALU.mult, ALU.add), after=[f"cv{k - 1}{c}"])
        s.step("act", "xe", lambda i: nc.scalar.activation(xg[:, :, :], xc[:, :, :], ACT.Exp, scale=-1.0), after=[f"cv{PAD}0", f"cv{PAD}1"], prev=["x_s"])
        s.step("dve", "z_1", lambda i: nc.vector.tensor_scalar(zg[:, :, :], zg[:, :, :], 1.0, None, ALU.add), after=["ze"])
        s.step("dve", "z_r", lambda i: nc.vector.reciprocal(zg[:, :, :], zg[:, :, :]), after=["z_1"])
        s.step("dve", "z_s", lambda i: nc.vector.tensor_tensor(zs[:, :, :], zg[:, :, :], PS[:, 1, :].rearrange("p (c n) -> p c n", c=CH), ALU.mult),
               after=["z_r"], prev=["y2"])
        s.step("dve", "x_1", lambda i: nc.vector.tensor_scalar(xg[:, :, :], xg[:, :, :], 1.0, None, ALU.add), after=["xe"])
        s.step("dve", "x_r", lambda i: nc.vector.reciprocal(xg[:, :, :], xg[:, :, :]), after=["x_1"])
        s.step("dve", "x_s", lambda i: nc.vector.tensor_tensor(xc[:, :, :], xc[:, :, :], xg[:, :, :], ALU.mult), after=["x_r"])
        s.step("pe", "xd_pe", lambda i: [nc.tensor.matmul(PS[0:DR + 2 * NS, 5, 0:SEQ], wx[:, c, :], xc[:, c, :], start=(c == 0), stop=(c == CH - 1))
                                         for c in range(CH)][-1], after=["x_s", "z_put"], prev=["x_out"])
        s.step("act", "xd", lambda i: nc.scalar.activation(xd[0:DR + 2 * NS, :], PS[0:DR + 2 * NS, 5, 0:SEQ], ACT.Copy), after=["xd_pe"],
               prev=[f"c_pe{UN - 1}", "dt_pe"])
        s.step("pe", "dt_pe", lambda i: [nc.tensor.matmul(PS[:, 4, c * SEQ:(c + 1) * SEQ], wd[:, c * P:c * P + P], xd[:, :], start=True, stop=True)
                                         for c in range(CH)][-1], after=["xd", "xmT"])
        for c in range(CH):
            s.step("dve", f"dv{c}", lambda i, c=c: nc.vector.tensor_scalar(dv[:, c, :], PS[:, 4, c * SEQ:(c + 1) * SEQ], db[:, c:c + 1], None, ALU.add),
                   after=["dt_pe"], prev=["dt"])
        s.step("dve", "da", lambda i: nc.vector.scalar_tensor_tensor(de[:, :, :], dv[:, :, :], -1.0, dv[:, :, :], ALU.mult, ALU.max),
               after=["dv0", "dv1"], prev=["dt"])
        s.step("act", "de", lambda i: nc.scalar.activation(de[:, :, :], de[:, :, :], ACT.Exp, scale=-1.0), after=["da"])
        s.step("act", "dl", lambda i: nc.scalar.activation(de[:, :, :], de[:, :, :], ACT.Ln, bias=1.0), after=["de"])
        s.step("dve", "dt", lambda i: nc.vector.scalar_tensor_tensor(dt[:, :, :], dv[:, :, :], 0.0, de[:, :, :], ALU.max, ALU.add),
               after=["dl"], prev=["dx", f"dA{UN - 1}"])
        s.step("dve", "dx", lambda i: nc.vector.tensor_tensor(dx[:, :, :], dt[:, :, :], xc[:, :, :], ALU.mult), after=["dt"], prev=[f"dbx{UN - 1}1"])

        def spread(u, first, b0):
            def go(i):
                for g in range(G):
                    r = first + u * G + g
                    mm = nc.tensor.matmul(PS[:, b0 + g // 2, (g % 2) * SEQ:(g % 2 + 1) * SEQ], self.ident[:, r:r + 1].broadcast_to((P, P)), xd[:, :],
                                          start=True, stop=True)
                return mm
            return go

        def sum_states(u):
            def go(i):
                for c in range(CH):
                    for g in range(G):
                        mm = nc.tensor.matmul(PS[:, 6 + c, 0:SEQ], self.ident[:, :], hc[:, c, g, :], start=(u == 0 and g == 0), stop=(u == UN - 1 and g == G - 1))
                return mm
            s.step("pe", f"y_pe{u}", go, after=[f"hc{u}0", f"hc{u}1"], prev=["y10", "y11"] if u == 0 else [])

        for u in range(UN):
            s.step("pe", f"b_pe{u}", spread(u, DR, 0), after=["xd"] + ([f"dbx{u - 1}0", f"dbx{u - 1}1"] if u else ["xp", "z_s"]))
            s.step("pe", f"c_pe{u}", spread(u, DR + NS, 2), after=["xd"] + ([f"hc{u - 1}0", f"hc{u - 1}1"] if u else []), prev=[] if u else [f"hc{UN - 1}1"])
            if u:
                sum_states(u - 1)

            def decay(i, u=u):
                for c in range(CH):
                    for g in range(G):
                        k = u * G + g
                        op = nc.scalar.activation(dA[:, c, g, 1:SEQ], dt[:, c, 1:SEQ], ACT.Exp, scale=na[:, c, k:k + 1])
                return op
            s.step("act", f"dA{u}", decay, after=["dt"] + ([f"h{u - 1}0", f"h{u - 1}1"] if u else []), prev=[] if u else [f"h{UN - 1}1"])
            for c in range(CH):
                s.step("dve", f"dbx{u}{c}", lambda i, c=c: nc.vector.tensor_tensor(
                    db_x[:, c, :, :], dx[:, c, :].unsqueeze(1).broadcast_to((P, G, SEQ)),
                    PS[:, 0:2, :].rearrange("p b (g n) -> p (b g) n", g=2), ALU.mult),
                    after=["dx", f"b_pe{u}"] + ([f"h{u - 1}{c}"] if u else []), prev=[] if u else [f"h{UN - 1}{c}"])
            for c in range(CH):
                s.step("dve", f"h{u}{c}", lambda i, c=c: nc.vector.tensor_tensor_scan(
                    flat(hs[:, c, :, :]), flat(dA[:, c, :, :]), flat(db_x[:, c, :, :]), 0.0, ALU.mult, ALU.add),
                    after=[f"dbx{u}{c}", f"dA{u}"] + ([f"hc{u - 1}{c}"] if u else []), prev=[] if u else [f"hc{UN - 1}{c}"])
            for c in range(CH):
                s.step("dve", f"hc{u}{c}", lambda i, c=c: nc.vector.tensor_tensor(
                    hc[:, c, :, :], hs[:, c, :, :], PS[:, 2:4, :].rearrange("p b (g n) -> p (b g) n", g=2), ALU.mult),
                    after=[f"h{u}{c}", f"c_pe{u}"] + ([f"y_pe{u - 1}"] if u else []), prev=[] if u else [f"y_pe{UN - 1}"])
        sum_states(UN - 1)
        for c in range(CH):
            s.step("dve", f"y1{c}", lambda i, c=c: nc.vector.scalar_tensor_tensor(
                yT[:, c, :], xc[:, c, :], dd[:, c:c + 1], PS[:, 6 + c, 0:SEQ], ALU.mult, ALU.add), after=[f"y_pe{UN - 1}"], prev=["o_pe"])
        s.step("dve", "y2", lambda i: nc.vector.tensor_tensor(yT[:, :, :], yT[:, :, :], zs[:, :, :], ALU.mult), after=["y10", "y11"])
        s.step("pe", "o_pe", lambda i: [nc.tensor.matmul(PS[:, 5, t * P:t * P + P], yT[:, c, t * P:t * P + P], wo[:, c, :], start=(c == 0), stop=(c == CH - 1))
                                        for t in range(TILES) for c in range(CH)][-1], after=["y2", "xd"])
        s.step("dve", "x1", lambda i: nc.vector.tensor_tensor(xs[:, :, :], xs[:, :, :], xn[:, :, :], ALU.add), after=["lm_out1"])
        s.step("dve", "x_out", lambda i: nc.vector.scalar_tensor_tensor(
            seq_tiles(X, i).rearrange("p t d -> p (t d)"), PS[:, 5, 0:SEQ], res[:, :], xs[:, :, :].rearrange("p t d -> p (t d)"), ALU.mult, ALU.add),
            after=["x1", "o_pe"])
        s.run(NSEQ, table=EXP_LN)

    def L3f(self):
        nc, d, PS, X, Z = self.nc, self.d, self.PS, self.X, self.Z
        DEPTH, H, HD, WIN = 6, 16, 64, 32
        INNER = H * HD
        KEYS = 2 * WIN
        PAIRS = H // 2
        NW = P // WIN
        DI = int(P * 4 * 2 / 3)
        CHK = [(0, P), (P, P), (2 * P, DI - 2 * P)]
        QK_SCALE = 8.0
        GRP = 4 * P
        pre = "L3_ffn_"

        wqkv = self.sb("wqkv", [P, 3 * INNER])
        wo = self.sb("wo", [P, PAIRS, P])
        w1 = self.sb("w1", [P, 2 * DI])
        w2 = self.sb("w2", [P, 3, P])
        b1 = self.sb("b1", [P, 2, 3])
        b2 = self.sb("b2", [P, 1])
        gb = self.sb("gb", [P, 2])
        qks = self.sb("qks", [P, 4, HD])
        rotc = self.sb("rotc", [P, TILES, 4, HD])
        rot = self.sb("rot", [P, TILES, 4, HD])
        lmask = self.sb("lmask", [P, TILES, KEYS])
        lmaskb = self.sb("lmaskb", [P, TILES, PAIRS, KEYS], BF16)
        mean = self.sb("mean", [P, P])
        fn = self.sb("fn", [P, NT * P])
        sT = self.sb("sT", [P, SEQ + 1])
        qz = self.sb("qz", [P, TILES, PAIRS, 2, P])
        kT = self.sb("kT", [P, PAIRS, WIN + SEQ])
        vw = self.sb("vw", [P, TILES * NW + 1, PAIRS * HD])
        s = self.stage()
        s.step("sp", "in", lambda i: [nc.sync.dma_start(rotc[:, :, :, :], d["c_rot"]), nc.sync.dma_start(lmask[:, :, :], d["c_local"])], dmas=2)
        s.step("pool", "m0", lambda i: nc.gpsimd.memset(mean[:, :], 1.0 / P))
        s.step("pool", "m2", lambda i: nc.gpsimd.memset(sT[:, :], 0.0))
        s.step("pool", "m3", lambda i: nc.gpsimd.memset(qz[:, :, :, :, :], 0.0))
        s.step("pool", "m4", lambda i: nc.gpsimd.memset(kT[:, :, :], 0.0))
        s.step("pool", "m5", lambda i: nc.gpsimd.memset(vw[:, :, :], 0.0))
        for t in range(TILES):
            s.step("dve", f"lmaskb{t}", lambda i, t=t: nc.vector.tensor_copy(lmaskb[:, t, :, :], lmask[:, t, :].unsqueeze(1).broadcast_to((P, PAIRS, KEYS))), after=["in"])
        s.run()

        zc = self.sb("zc", [P, SEQ])
        raw = self.sb("raw", [P, 2, 2 * INNER])
        sqr = self.sb("sqr", [P, 2 * INNER])
        ss = self.sb("ss", [P, 2, 2 * H])
        t1 = self.sb("t1", [P, 2 * INNER])
        t2 = self.sb("t2", [P, 2 * INNER])
        v2 = self.sb("v2", [P, TILES, 2, PAIRS * HD])
        sm = self.sb("sm", [P, PAIRS, 2, KEYS])
        mx = self.sb("mx", [P, PAIRS, 2])
        sl = self.sb("sl", [P, PAIRS, 2])
        pT = self.sb("pT", [P, PAIRS, P])
        ob = self.sb("ob", [P, PAIRS, 2, HD])
        oT = self.sb("oT", [P, PAIRS, SEQ])
        xc = self.sb("xc", [P, SEQ])
        xq = self.sb("xq", [P, SEQ])
        rs = self.sb("rs", [P, SEQ])
        gg = self.sb("gg", [P, 3, GRP])
        hh = self.sb("hh", [P, 3, GRP])

        def at(name, l):
            a = d[pre + name][bass.ds(l, 1)]
            return a

        with nc.Fori(0, DEPTH) as l:
            s = self.stage()

            def loads(i):
                out = [nc.sync.dma_start(wqkv[:, :], at("Wqkv", l).rearrange("a p n -> (a p) n")),
                       nc.sync.dma_start(wo[:, :, :], at("Wo", l).rearrange("a (c p) n -> p (a c) n", p=P)),
                       nc.sync.dma_start(w1[:, :], at("W1", l).rearrange("a p n -> (a p) n")),
                       nc.sync.dma_start(b2[:, :], at("b2", l).rearrange("a (p b) -> (a p) b", b=1)),
                       nc.sync.dma_start(gb[:, 0:1], at("ln_g", l).rearrange("a (p b) -> (a p) b", b=1)),
                       nc.sync.dma_start(gb[:, 1:2], at("ln_b", l).rearrange("a (p b) -> (a p) b", b=1))]
                for c, (o, m) in enumerate(CHK):
                    out.append(nc.sync.dma_start(w2[0:m, c, :], at("W2", l)[:, o:o + m, :].rearrange("a p n -> (a p) n")))
                    for half in range(2):
                        out.append(nc.sync.dma_start(b1[0:m, half, c:c + 1], at("b1", l)[:, half * DI + o:half * DI + o + m].rearrange("a (p b) -> (a p) b", b=1)))
                for n, w in enumerate(("q_scale", "k_scale")):
                    out.append(nc.sync.dma_start(qks[:, 2 * n, :], at(w, l).broadcast_to((P, HD))))
                    for half in range(2):
                        to, fr = half * HD // 2, (1 - half) * HD // 2
                        out.append(nc.sync.dma_start(qks[:, 2 * n + 1, to:to + HD // 2], at(w, l)[:, fr:fr + HD // 2].broadcast_to((P, HD // 2))))
                return out
            s.step("sp", "w", loads, dmas=6 + 9 + 6)
            for t in range(TILES):
                s.step("dve", f"rot{t}", lambda i, t=t: nc.vector.tensor_tensor(rot[:, t, :, :], rotc[:, t, :, :], qks[:, :, :], ALU.mult), after=["w"])
            s.run()

            s = self.stage()
            s.step("dve", "zc", lambda i: nc.vector.tensor_scalar(zc[:, :].unsqueeze(1), Z[:, bass.ds(i + 1, 1), 0:SEQ], 1.0, None, ALU.mult), prev=["p_pe1_5"])

            def front(t):
                for j in range(6):
                    n = 6 * t + j
                    b = n % 3
                    last = (n - 3) % 12
                    freed = [f"raw{last // 6}_{last % 6}"]
                    if j < 4:
                        w = wqkv[:, j * 512:(j + 1) * 512]
                    else:
                        w = wqkv[:, 2 * INNER:].rearrange("p (a h e) -> p h a e", h=2, e=HD)[:, j - 4, :, :]
                    s.step("pe", f"p_pe{t}_{j}", lambda i, b=b, w=w, t=t: nc.tensor.matmul(PS[:, b, :], zc[:, t * P:t * P + P], w, start=True, stop=True),
                           after=["zc"] + (freed if n >= 3 else []), prev=freed if n < 3 else [])
                    if j < 4:
                        s.step("act", f"raw{t}_{j}", lambda i, b=b, j=j, t=t: nc.scalar.activation(raw[:, t, j * 512:(j + 1) * 512], PS[:, b, :], ACT.Copy),
                               after=[f"p_pe{t}_{j}"], prev=[f"rc{t}", f"rn{t}", f"sqr{t}"])
                    else:
                        s.step("act", f"raw{t}_{j}", lambda i, b=b, j=j, t=t: nc.scalar.activation(v2[:, t, j - 4, :], PS[:, b, :], ACT.Copy),
                               after=[f"p_pe{t}_{j}"], prev=["vlow", "vhigh"])
                s.step("pool", f"sqr{t}", lambda i, t=t: nc.gpsimd.tensor_tensor(sqr[:, :], raw[:, t, :], raw[:, t, :], ALU.mult),
                       after=[f"raw{t}_3"] + (["ss0"] if t else []), prev=[] if t else ["ss1"])
                s.step("dve", f"ss{t}", lambda i, t=t: nc.vector.tensor_reduce(ss[:, t, :], sqr[:, :].rearrange("p (h e) -> p h e", e=HD), AX.X, ALU.add),
                       after=[f"sqr{t}", f"s_in{t}"], prev=[f"rq{t}"])
                s.step("dve", f"sc{t}", lambda i, t=t: nc.vector.tensor_scalar(ss[:, t, :], ss[:, t, :], 1e-24, None, ALU.max), after=[f"ss{t}"])
                s.step("act", f"sl{t}", lambda i, t=t: nc.scalar.activation(ss[:, t, :], ss[:, t, :], ACT.Ln), after=[f"sc{t}"])
                s.step("act", f"sr{t}", lambda i, t=t: nc.scalar.activation(ss[:, t, :], ss[:, t, :], ACT.Exp, scale=-0.5), after=[f"sl{t}"])

                def heads(a):
                    return a.rearrange("p (h e) -> p h e", e=HD)
                s.step("dve", f"rq{t}", lambda i, t=t: nc.vector.tensor_tensor(
                    heads(raw[:, t, INNER:]), heads(raw[:, t, INNER:]), ss[:, t, H:].unsqueeze(2).broadcast_to((P, H, HD)), ALU.mult), after=[f"sr{t}"])

                def cosine(i, t=t):
                    for n in range(2):
                        op = nc.vector.tensor_tensor(heads(t1[:, n * INNER:(n + 1) * INNER]), heads(raw[:, t, n * INNER:(n + 1) * INNER]),
                                                     rot[:, t, 2 * n, :].unsqueeze(1).broadcast_to((P, H, HD)), ALU.mult)
                    return op

                def sine(i, t=t):
                    for n in range(2):
                        for half in range(2):
                            to = slice(half * HD // 2, (half + 1) * HD // 2)
                            fr = slice((1 - half) * HD // 2, (2 - half) * HD // 2)
                            op = nc.gpsimd.tensor_tensor(heads(t2[:, n * INNER:(n + 1) * INNER])[:, :, to], heads(raw[:, t, n * INNER:(n + 1) * INNER])[:, :, fr],
                                                         rot[:, t, 2 * n + 1, to].unsqueeze(1).broadcast_to((P, H, HD // 2)), ALU.mult)
                    return op
                s.step("dve", f"rc{t}", cosine, after=[f"rq{t}"] + (["qk_pe0_3"] if t else ["qk_pe1_3"]))
                s.step("pool", f"rn{t}", sine, after=[f"rq{t}"] + (["ra0"] if t else []), prev=[] if t else ["ra1"])
                s.step("dve", f"ra{t}", lambda i: nc.vector.tensor_tensor(t1[:, :], t1[:, :], t2[:, :], ALU.add), after=[f"rc{t}", f"rn{t}"])

            def turned(t):
                for g in range(4):
                    b = 3 + g % 2
                    s.step("pe", f"qk_pe{t}_{g}", lambda i, g=g, b=b: [nc.tensor.transpose(
                        PS[:, b, c * P:c * P + P], t1[:, (4 * g + c) * P:(4 * g + c + 1) * P], self.ident[:, :]) for c in range(4)][-1],
                        after=([f"qk{t}_{g - 2}"] if g >= 2 else ["oT0"] if t == 0 else []) + (["ra0"] if t == 0 else []),
                        prev=["ra1", "oT1"] if t else [])
                    src = PS[:, b, :].rearrange("p (c n) -> p c n", n=P)
                    last = ["s_pe0", "s_pe1"] if t == 0 else []
                    if g < 2:
                        def put(i, g=g, src=src, t=t):
                            for half in range(2):
                                r = slice(half * HD, half * HD + HD)
                                op = nc.scalar.activation(qz[r, t, 4 * g:4 * g + 4, half, :], src[r, :, :], ACT.Copy)
                            return op
                        s.step("act", f"qk{t}_{g}", put, after=[f"qk_pe{t}_{g}"] + last, prev=["s_pe1"] if t else [])
                    else:
                        s.step("act", f"qk{t}_{g}", lambda i, g=g, t=t, src=src: nc.scalar.activation(
                            kT[:, 4 * (g - 2):4 * (g - 1), WIN + t * P:WIN + (t + 1) * P], src, ACT.Copy), after=[f"qk_pe{t}_{g}"] + last, prev=["s_pe1"] if t else [])

            def scores(t):
                def go(i):
                    for half in range(2):
                        nc.tensor.matmul(PS[:, 5 + half, :], self.identb[:, :], lmaskb[:, t, :, :].rearrange("p a k -> p (a k)"), start=True, stop=False,
                                         skip_group_check=True)
                    for w in range(NW):
                        for h in range(H):
                            mm = nc.tensor.matmul(PS[w * WIN:(w + 1) * WIN, 5 + h % 2, (h // 2) * KEYS:(h // 2 + 1) * KEYS],
                                                  qz[:, t, h // 2, h % 2, w * WIN:(w + 1) * WIN], kT[:, h // 2, t * P + w * WIN:t * P + w * WIN + KEYS],
                                                  start=False, stop=True, skip_group_check=True)
                    return mm
                s.step("pe", f"s_pe{t}", go, after=["s_in0", "qk1_1", "qk1_3"] if t else [], prev=[] if t else ["qk0_1", "qk0_3", "on1"])

            def softmax(t):
                p3 = sm[:, :, :, :].rearrange("p a b k -> p (a b) k")

                s.step("dve", f"s_in{t}", lambda i: nc.vector.tensor_tensor(
                    sm[:, :, :, :].rearrange("p a b k -> p b a k"), PS[:, 5:7, :].rearrange("p b (a k) -> p b a k", k=KEYS),
                    ss[:, t, 0:H].rearrange("p (a b) -> p b a", b=2).unsqueeze(3).broadcast_to((P, 2, PAIRS, KEYS)), ALU.mult),
                    after=[f"s_pe{t}"] + (["pT_pe0"] if t else []), prev=[f"sr{t}"] + ([] if t else ["pT_pe1"]))
                s.step("dve", f"s_max{t}", lambda i: nc.vector.tensor_reduce(mx[:, :, :], sm[:, :, :, :], AX.X, ALU.max), after=[f"s_in{t}"])
                s.step("dve", f"s_sub{t}", lambda i: nc.vector.tensor_tensor(
                    p3, p3, mx[:, :, :].rearrange("p a b -> p (a b)").unsqueeze(2).broadcast_to((P, H, KEYS)), ALU.subtract), after=[f"s_max{t}"])
                s.step("act", f"s_exp{t}", lambda i: nc.scalar.activation(sm[:, :, :, :], sm[:, :, :, :], ACT.Exp, scale=QK_SCALE), after=[f"s_sub{t}"])
                s.step("dve", f"s_sum{t}", lambda i: nc.vector.tensor_reduce(sl[:, :, :], sm[:, :, :, :], AX.X, ALU.add), after=[f"s_exp{t}"] + (["on0"] if t else []), prev=[] if t else ["on1"])
                s.step("dve", f"s_inv{t}", lambda i: nc.vector.reciprocal(sl[:, :, :], sl[:, :, :]), after=[f"s_sum{t}"])

            def windows():
                for nm, part, shift in (("vhigh", WIN, 0), ("vlow", 0, 1)):
                    def go(i, part=part, shift=shift):
                        out = []
                        for half in range(2):
                            for k in range(NW):
                                dst = vw[half * HD + part:half * HD + part + WIN, k + shift:k + shift + NW * (TILES - 1) + 1:NW, :]
                                out.append(nc.sync.dma_start(dst, v2[k * WIN:(k + 1) * WIN, :, half, :]))
                        return out
                    s.step("sp", nm, go, after=["raw0_5", "raw1_5", "o_pe1"], dmas=2 * NW, dma=nm)

            def back(t):
                def turn(i):
                    for a in range(PAIRS):
                        mm = nc.tensor.transpose(PS[:, 3 + a // 4, (a % 4) * P:(a % 4 + 1) * P], sm[:, a, :, :].rearrange("p b k -> p (b k)"), self.ident[:, :])
                    return mm
                s.step("pe", f"pT_pe{t}", turn, after=[f"s_exp{t}"] + (["qk0_2", "qk0_3", "oT0"] if t else ["qk1_2", "qk1_3"]))
                s.step("act", f"pT{t}", lambda i: nc.scalar.activation(pT[:, :, :].rearrange("p a n -> p (a n)"), PS[:, 3:5, :].rearrange("p b n -> p (b n)"), ACT.Copy),
                       after=[f"pT_pe{t}"] + (["o_pe0"] if t else []), prev=[] if t else ["o_pe1"])

                def values(i):
                    for a in range(PAIRS):
                        for w in range(NW):
                            for half in range(2):
                                r = slice(half * HD, half * HD + HD)
                                mm = nc.tensor.matmul(PS[w * WIN:(w + 1) * WIN, 5 + half, a * HD:(a + 1) * HD], pT[r, a, w * WIN:(w + 1) * WIN],
                                                      vw[r, t * NW + w, a * HD:(a + 1) * HD], start=True, stop=True)
                    return mm
                s.step("pe", f"o_pe{t}", values, after=[f"pT{t}", "s_in1"] + (["on0"] if t else []), prev=["vlow", "vhigh"], solo=True)
                s.step("dve", f"on{t}", lambda i: nc.vector.tensor_tensor(
                    ob[:, :, :, :].rearrange("p a b e -> p b a e"), PS[:, 5:7, :].rearrange("p b (a e) -> p b a e", e=HD),
                    sl[:, :, :].rearrange("p a b -> p b a").unsqueeze(3).broadcast_to((P, 2, PAIRS, HD)), ALU.mult),
                    after=[f"o_pe{t}", f"s_inv{t}"] + (["oT_pe0"] if t else []), prev=[] if t else ["oT_pe1"])
                s.step("pe", f"oT_pe{t}", lambda i: [nc.tensor.transpose(PS[:, 3 + a // 4, (a % 4) * P:(a % 4 + 1) * P],
                                                                         ob[:, a, :, :].rearrange("p b e -> p (b e)"), self.ident[:, :]) for a in range(PAIRS)][-1],
                       after=[f"on{t}", f"pT{t}"])
                s.step("act", f"oT{t}", lambda i: nc.scalar.activation(oT[:, :, t * P:(t + 1) * P], PS[:, 3:5, :].rearrange("p b (a n) -> p (b a) n", n=P), ACT.Copy),
                       after=[f"oT_pe{t}"], prev=["w_pe"])

            for t in range(TILES):
                front(t)
            turned(0)
            windows()
            begins = set(s.names)
            turned(1)
            for t in range(TILES):
                scores(t)
                softmax(t)
                back(t)
            s.step("pe", "w_pe", lambda i: [nc.tensor.matmul(PS[:, 7, 0:SEQ], wo[:, a, :], oT[:, a, :], start=(a == 0), stop=(a == PAIRS - 1))
                                            for a in range(PAIRS)][-1], after=["oT0", "oT1"], prev=["var"])

            def residual(i):
                for r, c in ((slice(0, HD), slice(0, SEQ)), (slice(HD, P), slice(1, SEQ + 1))):
                    op = nc.vector.tensor_tensor(sT[r, c].unsqueeze(1), Z[r, bass.ds(i, 1), c], PS[r, 7, 0:SEQ].unsqueeze(1), ALU.add)
                return op
            s.step("dve", "zn", residual, after=["w_pe"], prev=["zput", "cent", "m_pe"])
            s.step("dve", "zput", lambda i: nc.vector.tensor_scalar(Z[:, bass.ds(i, 1), :], sT[:, :].unsqueeze(1), 1.0, None, ALU.mult), after=["zn"])
            s.step("pe", "m_pe", lambda i: nc.tensor.matmul(PS[:, 7, SEQ:2 * SEQ], mean[:, :], sT[:, 0:SEQ], start=True, stop=True), after=["zn"])
            s.step("dve", "cent", lambda i: nc.vector.tensor_tensor(xc[:, :], sT[:, 0:SEQ], PS[:, 7, SEQ:2 * SEQ], ALU.subtract), after=["m_pe"], prev=["fn2"])
            s.step("dve", "xq", lambda i: nc.vector.tensor_tensor(xq[:, :], xc[:, :], xc[:, :], ALU.mult), after=["cent"], prev=["v_pe"])
            s.step("pe", "v_pe", lambda i: nc.tensor.matmul(PS[:, 7, SEQ:2 * SEQ], mean[:, :], xq[:, :], start=True, stop=True), after=["xq"])
            s.step("act", "var", lambda i: nc.scalar.activation(rs[:, :], PS[:, 7, SEQ:2 * SEQ], ACT.Ln, bias=self.eps[:, :]), after=["v_pe"], prev=["fn1"])
            s.step("act", "rstd", lambda i: nc.scalar.activation(rs[:, :], rs[:, :], ACT.Exp, scale=-0.5), after=["var"])
            s.step("dve", "fn1", lambda i: nc.vector.tensor_tensor(xc[:, :], xc[:, :], rs[:, :], ALU.mult), after=["rstd"])
            s.step("dve", "fn2", lambda i: nc.vector.tensor_scalar(fn[:, bass.ds(i * SEQ, SEQ)], xc[:, :], gb[:, 0:1], gb[:, 1:2], ALU.mult, ALU.add), after=["fn1"])
            each = range(6)
            s.order("pe", ["s_pe0"] + [f"p_pe0_{j}" for j in each] + [f"qk_pe1_{g}" for g in range(4)] + ["s_pe1", "pT_pe0", "o_pe0"] + [f"p_pe1_{j}" for j in each]
                    + ["oT_pe0"] + [f"qk_pe0_{g}" for g in range(4)] + ["pT_pe1", "o_pe1", "oT_pe1", "w_pe", "m_pe", "v_pe"])
            s.order("act", ["raw0_0", "raw0_1", "raw0_2", "s_exp0", "raw0_3", "raw0_4", "raw0_5"] + [f"qk1_{g}" for g in range(4)] + ["pT0", "sl0", "sr0", "s_exp1"]
                    + [f"raw1_{j}" for j in each] + ["oT0"] + [f"qk0_{g}" for g in range(4)] + ["sl1", "sr1", "pT1", "oT1", "var", "rstd"])
            s.order("dve", ["zc", "s_in0", "s_max0", "s_sub0", "s_sum0", "s_inv0", "ss0", "sc0", "s_in1", "s_max1", "s_sub1", "rq0", "rc0", "on0", "s_sum1", "s_inv1",
                            "ra0", "ss1", "sc1", "rq1", "rc1", "on1", "ra1", "zn", "zput", "cent", "xq", "fn1", "fn2"])
            s.run(part=begins, at=-1, table=EXP_LN)
            s.run(NSEQ - 1, table=EXP_LN)
            s.run(part=s.names - begins, at=NSEQ - 1, table=EXP_LN)

            s = self.stage()
            for c, (o, m) in enumerate(CHK):
                s.step("pe", f"g_pe{c}", lambda i, c=c, o=o, m=m: nc.tensor.matmul(PS[0:m, 3 + c, :], w1[:, DI + o:DI + o + m], fn[:, bass.ds(i * GRP, GRP)],
                                                                                   start=True, stop=True), prev=[f"gg{c}"])
                s.step("pe", f"a_pe{c}", lambda i, c=c, o=o, m=m: nc.tensor.matmul(PS[0:m, c, :], w1[:, o:o + m], fn[:, bass.ds(i * GRP, GRP)],
                                                                                   start=True, stop=True), prev=[f"hh{c}"])
                s.step("act", f"gg{c}", lambda i, c=c, m=m: nc.scalar.activation(gg[0:m, c, :], PS[0:m, 3 + c, :], ACT.Gelu, bias=b1[0:m, 1, c:c + 1]),
                       after=[f"g_pe{c}"], prev=[f"hh{c}"])
                s.step("dve", f"hh{c}", lambda i, c=c, m=m: nc.vector.scalar_tensor_tensor(hh[0:m, c, :], PS[0:m, c, :], b1[0:m, 0, c:c + 1], gg[0:m, c, :], ALU.add, ALU.mult),
                       after=[f"a_pe{c}", f"gg{c}"], prev=["o_pe"])
            s.step("pe", "o_pe", lambda i: [nc.tensor.matmul(PS[:, 6, :], w2[0:m, c, :], hh[0:m, c, :], start=(c == 0), stop=(c == 2))
                                            for c, (o, m) in enumerate(CHK)][-1], after=["hh0", "hh1", "hh2"], prev=["z_out"])

            def add(i):
                for r, c in ((slice(0, HD), 0), (slice(HD, P), 1)):
                    for q in range(GRP // SEQ):
                        z = Z[r, bass.ds(i * (GRP // SEQ) + q, 1), c:c + SEQ].rearrange("p a n -> p (a n)")
                        op = nc.vector.scalar_tensor_tensor(z, PS[r, 6, q * SEQ:(q + 1) * SEQ], b2[r, :], z, ALU.add, ALU.add)
                return op
            s.step("dve", "z_out", add, after=["o_pe"])
            s.run(NT * P // GRP, table="gelu_and_others")
        zu = self.sb("zu", [P, SEQ])
        s = self.stage()

        def unshift(i):
            for r, c in ((slice(0, HD), 0), (slice(HD, P), 1)):
                op = nc.vector.tensor_scalar(zu[r, :].unsqueeze(1), Z[r, bass.ds(i, 1), c:c + SEQ], 1.0, None, ALU.mult)
            return op
        s.step("dve", "zu", unshift, prev=["pe"])
        s.step("pe", "pe", lambda i: [nc.tensor.transpose(PS[:, 0, t * P:t * P + P], zu[:, t * P:t * P + P], self.ident[:, :]) for t in range(TILES)][-1],
               after=["zu"], prev=["x_out"])
        s.step("dve", "x_out", lambda i: nc.vector.tensor_tensor(seq_tiles(X, i), seq_tiles(X, i), PS[:, 0, 0:SEQ].rearrange("p (t d) -> p t d", t=TILES), ALU.add),
               after=["pe"])
        s.run(NSEQ)


def constants():
    p = np.arange(P)
    c = {"c_ident": np.eye(P, dtype=np.float32)}
    c["c_causal"] = np.where(p[None, :] <= p[:, None], 0.0, NEG).astype(np.float32)
    c["c_causal01"] = (p[:, None] <= p[None, :]).astype(np.float32)
    c["c_head16"] = (p[:, None] // 8 == np.arange(16)[None, :]).astype(np.float32)
    c["c_head8"] = (p[:, None] // 16 == np.arange(8)[None, :]).astype(np.float32)
    q, k = p[:, None] % 32, np.arange(64)[None, :]
    seen = (k >= q) & (k <= q + 32)
    first = seen & ((p[:, None] >= 32) | (k >= 32))
    c["c_local"] = np.where(np.stack([first, seen], 1), 0.0, NEG).astype(np.float32)
    hd, win = 64, 32
    half = np.arange(0, hd, 2, dtype=np.float32)
    pos = np.arange(SEQ, dtype=np.float32)
    freqs = np.tile(pos[:, None] * (1.0 / 10000.0 ** (half / hd)).astype(np.float32)[None, :], (1, 2))
    power = ((pos - SEQ // 2) / (win // 2)).astype(np.float32)
    scale = np.tile(((half + 0.4 * hd) / (1.4 * hd)).astype(np.float32)[None, :] ** power[:, None], (1, 2))
    sign = np.where(np.arange(hd) < hd // 2, -1.0, 1.0).astype(np.float32)
    rot = np.stack([np.cos(freqs) * scale, np.sin(freqs) * scale * sign, np.cos(freqs) / scale, np.sin(freqs) / scale * sign], 1)
    c["c_rot"] = rot.reshape(TILES, P, 4, hd).swapaxes(0, 1).astype(np.float32)
    return c


def laid_out(x):
    def turn(a):
        return a.T

    def cols(n):
        return lambda a: a.reshape(n, -1, *a.shape[1:]).swapaxes(0, 1)

    def cols_t(n):
        return lambda a: a.T.reshape(n, -1, a.shape[0]).swapaxes(0, 1)

    how = {f"L{n}_attn_{w}": turn for n, ws in ((0, ("Wq", "Wk", "Wv", "Wp")), (1, ("Wq", "Wk", "Wv", "Wo")),
                                                  (2, ("Wq", "Wk", "Wv"))) for w in ws}
    how.update(L1_ffn_b1=cols(4), L2_ffn_Wq=turn, L2_ffn_routers=turn, L2_ffn_Wout_w=turn,
               L3_attn_in_proj_w=turn, L3_attn_x_proj_w=cols_t(2), L3_attn_dt_proj_w=turn,
               L3_attn_out_proj_w=cols_t(2), L3_attn_conv_w=cols(2), L3_attn_conv_b=cols(2), L3_attn_dt_proj_b=cols(2),
               L3_attn_A_log=cols(2), L3_attn_D=cols(2))
    return {(k + "_T" if k in how else k): how.get(k, lambda a: a)(np.asarray(v)) for k, v in x.items()
            if k != "L2_ffn_leaf_keys"}


def kernel(**inputs):
    import concourse.bacc as _bacc
    from concourse.bass_utils import run_bass_kernel_spmd as _run

    nc = _bacc.Bacc("TRN2", target_bir_lowering=False, num_devices=1)
    arrays, aps = {}, {}
    given = {k: np.ascontiguousarray(v) for k, v in laid_out(inputs).items()}
    for name, a in list(given.items()) + list(constants().items()):
        a = a.reshape(a.shape or (1,))
        arrays[f"in_{name}"] = a
        aps[name] = nc.dram_tensor(f"in_{name}", a.shape, mybir.dt.from_np(a.dtype), kind="ExternalInput").ap()
    out = nc.dram_tensor("out", (NSEQ, SEQ, P), F32, kind="ExternalOutput").ap()
    Kernel(nc, aps, out, ('L0', 'L1', 'L2', 'L3a', 'L3f')).build()
    r = _run(nc, [arrays], core_ids=[0])
    return r.results[0]["out"]
```

```python
import numpy as np
import concourse.bass as bass
from concourse import mybir
from contextlib import ExitStack

F32 = mybir.dt.float32
BF16 = mybir.dt.bfloat16
I32 = mybir.dt.int32
ALU = mybir.AluOpType
ACT = mybir.ActivationFunctionType
AX = mybir.AxisListType

P = 128
NSEQ, SEQ = 16, 256
TILES = SEQ // P
NT = NSEQ * TILES
EPS = 1e-5
NEG = -1e30
EXP_LN = "natural_log_exp_and_others"


class Stage:

    def __init__(self, nc, sems, dma_sems):
        self.nc, self.sems, self.dma_sems = nc, sems, dma_sems
        self.engines = {"pe": nc.tensor, "dve": nc.vector, "act": nc.scalar, "pool": nc.gpsimd, "sp": nc.sync}
        self.steps, self.names = [], set()

    def step(self, eng, name, fn, after=(), prev=(), dmas=0, dma="load", solo=False):
        assert name not in self.names, name
        self.names.add(name)
        self.steps.append((eng, name, fn, tuple(after), tuple(prev), dmas, dma, solo))

    def order(self, eng, names):
        place = {n: k for k, n in enumerate(names)}
        mine = sorted((s for s in self.steps if s[0] == eng), key=lambda s: place[s[1]])
        self.steps = mine + [s for s in self.steps if s[0] != eng]

    def sem(self, key):
        return self.sems[key] if key in self.sems else self.dma_sems[key]

    def run(self, turns=1, part=None, at=0, table=None):
        nc = self.nc
        steps = [s for s in self.steps if part is None or s[1] in part]
        mark, count = {}, {}
        for eng, name, _, _, _, dmas, dma, _ in steps:
            key, inc = (dma, 16 * dmas) if dmas else (eng, 1)
            count[key] = count.get(key, 0) + inc
            mark[name] = (key, count[key])
        if table:
            nc.scalar.preload_act_table_set(table)
        if turns == 1:
            self._write(steps, mark, count, None, at)
        else:
            for key, n in count.items():
                self.engines.get(key, nc.sync).sem_inc(self.sem(key), n)
            with nc.Fori(0, turns) as turn:
                self._write(steps, mark, count, turn, turn)
        for key, n in count.items():
            if key not in self.engines:
                nc.sync.wait_ge(self.sem(key), n * (turns + (turns > 1)))
        nc.all_engine_barrier()
        for key in count:
            nc.sync.sem_clear(self.sem(key))
        nc.all_engine_barrier()

    def _write(self, steps, mark, count, turn, at):
        seen = {}
        for eng, name, fn, after, prev, dmas, dma, solo in steps:
            e = self.engines[eng]
            need = {}
            for n in after:
                if n in mark:
                    key, v = mark[n]
                    need[key] = max(need.get(key, -1 << 30), v)
            if turn is not None:
                for n in prev:
                    key, v = mark[n]
                    need[key] = max(need.get(key, -1 << 30), v - count[key])
            waited = False
            for key, v in need.items():
                if seen.get((eng, key), -1 << 30) >= v:
                    continue
                seen[(eng, key)] = v
                n = count[key]
                e.wait_ge(self.sem(key), v if turn is None else turn * n + (v + n))
                waited = True
            if waited and solo and turn is not None:
                e.sem_inc(self.sems["spare_" + eng], 1)
            out = fn(at)
            if dmas:
                for d in out:
                    d.then_inc(self.sem(dma), 16)
            else:
                out.then_inc(self.sems[eng], 1)


def seq_tiles(ap, i):
    return ap[:, bass.ds(i * TILES, TILES), :]


def row(ap, n):
    return ap.rearrange("(a n) -> a n", a=1).broadcast_to((P, n))


class Kernel:
    def __init__(self, nc, d, out, stages):
        self.nc, self.d, self.out, self.stages = nc, d, out, stages

    def sb(self, name, shape, dt=F32):
        return self.ctx.enter_context(self.nc.sbuf_tensor(f"{self.tag}_{name}", shape, dt))

    def stage(self):
        return Stage(self.nc, self.sems, self.dma_sems)

    def build(self):
        nc, d = self.nc, self.d
        with ExitStack() as ctx:
            self.ctx, self.tag = ctx, "all"
            self.sems = {k: ctx.enter_context(nc.semaphore(f"done_{k}")) for k in ("pe", "dve", "act", "pool")}
            for k in ("pe", "dve", "act", "pool"):
                self.sems["spare_" + k] = ctx.enter_context(nc.semaphore(f"spare_{k}"))
            self.dma_sems = {k: ctx.enter_context(nc.semaphore(f"dma_{k}"))
                             for k in ("load", "vlow", "vhigh", "store")}
            self.X = self.sb("x", [P, NT, P])
            self.Z = self.sb("z", [P, NSEQ, SEQ + 1])
            self.ident = self.sb("ident", [P, P])
            self.identb = self.sb("identb", [P, P], BF16)
            self.PS = ctx.enter_context(nc.psum_tensor("ps", [P, 8, 512], F32))
            self.eps = self.sb("eps", [P, 1])
            s = self.stage()
            s.step("sp", "x", lambda i: [nc.sync.dma_start(self.X[:, :, :], d["L0_attn_x"].rearrange("b (t p) d -> p (b t) d", p=P))], dmas=1)
            s.step("sp", "ident", lambda i: [nc.sync.dma_start(self.ident[:, :], d["c_ident"])], dmas=1, dma="store")
            s.step("dve", "identb", lambda i: nc.vector.tensor_copy(self.identb[:, :], self.ident[:, :]), after=["ident"])
            s.step("pool", "zero", lambda i: nc.gpsimd.memset(self.Z[:, :, :], 0.0))
            s.step("dve", "eps", lambda i: nc.vector.memset(self.eps[:, :], EPS))
            s.run()
            for k in self.stages:
                with ExitStack() as self.ctx:
                    self.tag = k
                    {"L0": self.L0, "L1": self.L1, "L2": self.L2, "L3a": self.L3a, "L3f": self.L3f}[k]()
            s = self.stage()
            s.step("sp", "out", lambda i: [nc.sync.dma_start(self.out.rearrange("b (t p) d -> p (b t) d", p=P), self.X[:, :, :])], dmas=1, dma="store")
            s.run()

    def layernorm(self, s, src, dst, name, after, prev=(), wprev=()):
        nc = self.nc
        st, mv, ls, rs = (self.sb(f"{name}_{n}", [P, TILES, w]) for n, w in (("st", 6), ("mv", 2), ("ls", 1), ("rs", 1)))
        for t in range(TILES):
            s.step("dve", f"{name}_st{t}", lambda i, t=t: nc.vector.bn_stats(st[:, t, :], src[:, t, :]),
                   after=after, prev=[f"{name}_mv{t}"])
            s.step("dve", f"{name}_mv{t}", lambda i, t=t: nc.vector.bn_aggr(mv[:, t, :], st[:, t, :]),
                   after=[f"{name}_st{t}"], prev=[f"{name}_out{t}"], solo=True)
        s.step("act", f"{name}_ln", lambda i: nc.scalar.activation(ls[:, :, 0], mv[:, :, 1], ACT.Ln, bias=self.eps[:, :]),
               after=[f"{name}_mv0", f"{name}_mv1"], prev=[f"{name}_rs"])
        s.step("act", f"{name}_rs", lambda i: nc.scalar.activation(rs[:, :, 0], ls[:, :, 0], ACT.Exp, scale=-0.5),
               after=[f"{name}_ln"], prev=[f"{name}_out{t}" for t in range(TILES)])
        for t in range(TILES):
            s.step("dve", f"{name}_out{t}", lambda i, t=t: nc.vector.tensor_scalar(
                dst[:, t, :], src[:, t, :], mv[:, t, 0:1], rs[:, t, :], ALU.subtract, ALU.mult),
                after=[f"{name}_rs"], prev=wprev)

    def L0(self):
        nc, d, PS, X = self.nc, self.d, self.PS, self.X
        H, HD = 16, 8
        G = 4
        wt = self.sb("wt", [P, 4, P])
        bqk = self.sb("bqk", [P, 2])
        bvp = self.sb("bvp", [P, 2, P])
        hmask = self.sb("hmask", [P, H])
        cmask = self.sb("cmask", [P, P])
        cmaskb = self.sb("cmaskb", [P, P], BF16)
        kb = self.sb("kb", [P, P], BF16)
        kf = self.sb("kf", [P, P])
        sc = self.sb("sc", [P, 2])
        rsc = self.sb("rsc", [P, 2])
        ssc = self.sb("ssc", [P, 1])
        fbias = self.sb("fbias", [P, P], BF16)
        kq = self.sb("kq", [P, P], BF16)
        vaug = self.sb("vaug", [P, TILES, H, HD + 1])
        qz = [self.sb(f"qz_{n}", [P, SEQ]) for n in ("p", "m", "r", "w")]

        def quantise(s, name, src, dst, w, scal, after, prev=()):
            xs, mg, r, t2 = (q[:, 0:w] for q in qz)
            s.step("dve", name + "0", lambda i: nc.vector.tensor_scalar(xs, src, scal, None, ALU.mult), after=after, prev=prev)
            s.step("dve", name + "1", lambda i: nc.vector.tensor_scalar(
                mg.bitcast(I32), xs.bitcast(I32), 0x7F800000, None, ALU.bitwise_and), after=[name + "0"])
            s.step("dve", name + "2", lambda i: nc.vector.tensor_scalar(
                mg, mg, 2.0 ** -6, 1.5 * 2.0 ** 20, ALU.max, ALU.mult), after=[name + "1"])
            s.step("dve", name + "3", lambda i: nc.vector.tensor_tensor(r, xs, mg, ALU.add), after=[name + "2"])
            s.step("dve", name + "4", lambda i: nc.vector.tensor_tensor(r, r, mg, ALU.subtract), after=[name + "3"])
            s.step("dve", name + "5", lambda i: nc.vector.tensor_tensor(t2, r, r, ALU.mult), after=[name + "4"])
            s.step("dve", name + "6", lambda i: nc.vector.tensor_scalar(
                t2, t2, 448.0 ** 2, -(448.0 ** 2), ALU.max, ALU.add), after=[name + "5"])
            s.step("dve", name + "7", lambda i: nc.vector.tensor_scalar(t2, t2, 2.0 ** 127, None, ALU.mult), after=[name + "6"])
            s.step("dve", name + "8", lambda i: nc.vector.tensor_tensor(t2, t2, t2, ALU.subtract), after=[name + "7"])
            s.step("dve", name + "9", lambda i: nc.vector.tensor_tensor(dst, r, t2, ALU.add), after=[name + "8"])

        s = self.stage()
        s.step("sp", "in", lambda i: [nc.sync.dma_start(wt[:, n, :], d["L0_attn_" + w + "_T"]) for n, w in enumerate(("Wq", "Wk", "Wv", "Wp"))]
               + [nc.sync.dma_start(bqk[:, n:n + 1], d["L0_attn_" + w].rearrange("(p a) -> p a", a=1)) for n, w in enumerate(("bq", "bk"))]
               + [nc.sync.dma_start(bvp[:, n, :], row(d["L0_attn_" + w], P)) for n, w in enumerate(("bv", "bp"))]
               + [nc.sync.dma_start(hmask[:, :], d["c_head16"]), nc.sync.dma_start(cmask[:, :], d["c_causal"]),
                  nc.sync.dma_start(kb[:, :], d["L0_ffn_kernel"]), nc.sync.dma_start(fbias[:, :], row(d["L0_ffn_bias"], P)),
                  nc.sync.dma_start(sc[:, 0:1], row(d["L0_ffn_input_scale"], 1)),
                  nc.sync.dma_start(sc[:, 1:2], row(d["L0_ffn_kernel_scale"], 1))], dmas=14)
        s.step("dve", "cmaskb", lambda i: nc.vector.tensor_copy(cmaskb[:, :], cmask[:, :]), after=["in"])
        s.step("dve", "kf", lambda i: nc.vector.tensor_copy(kf[:, :], kb[:, :]), after=["in"])
        s.step("dve", "rsc", lambda i: nc.vector.reciprocal(rsc[:, :], sc[:, :]), after=["in"])
        s.step("dve", "ssc", lambda i: nc.vector.tensor_tensor(ssc[:, :], sc[:, 0:1], sc[:, 1:2], ALU.mult), after=["in"])
        quantise(s, "kq", kf[:, :], kq[:, :], P, rsc[:, 1:2], ["kf", "rsc"])
        s.step("pool", "ones", lambda i: nc.gpsimd.memset(vaug[:, :, :, HD], 1.0))
        s.run()

        xs = self.sb("xs", [P, TILES, P])
        xn = self.sb("xn", [P, TILES, P])
        xnT = self.sb("xnT", [P, SEQ])
        xb = self.sb("xb", [P, SEQ], BF16)
        xq = self.sb("xq", [P, SEQ], BF16)
        yb = self.sb("yb", [P, TILES, P], BF16)
        qT = self.sb("qT", [P, SEQ])
        kT = self.sb("kT", [P, SEQ])
        qm = self.sb("qm", [P, H, SEQ])
        sm = self.sb("sm", [P, 2, G * SEQ])
        pT = self.sb("pT", [P, 2, G * SEQ])
        mx = self.sb("mx", [P, 2, G])
        ob = self.sb("ob", [P, TILES, H, HD])
        rl = self.sb("rl", [P, TILES, H])
        oT = self.sb("oT", [P, SEQ])

        s = self.stage()
        s.step("dve", "xs", lambda i: nc.vector.tensor_scalar(xs[:, :, :], seq_tiles(X, i + 1), 1.0, None, ALU.mult), prev=["x2"])
        self.layernorm(s, xs, xn, "ln", ["xs"], wprev=["xnT_pe"])
        s.step("pe", "xnT_pe", lambda i: [nc.tensor.transpose(PS[:, 0, t * P:t * P + P], xn[:, t, :], self.ident[:, :]) for t in range(TILES)][-1],
               after=["ln_out0", "ln_out1", "s_sub6"], prev=["xnT"])
        s.step("act", "xnT", lambda i: nc.scalar.activation(xnT[:, :], PS[:, 0, 0:SEQ], ACT.Copy), after=["xnT_pe", "q_pe", "k_pe", "v_pe"], prev=["xb"])
        for n, (w, to, b) in enumerate((("q", qT, 0), ("k", kT, 1))):
            s.step("pe", w + "_pe", lambda i, n=n, b=b: nc.tensor.matmul(PS[:, b, 0:SEQ], wt[:, n, :], xnT[:, :], start=True, stop=True),
                   prev=["xnT", "s_sub%d" % (2 * H // G - 2)])
            s.step("act", w, lambda i, n=n, to=to, b=b: nc.scalar.activation(to[:, :], PS[:, b, 0:SEQ], ACT.Identity, bias=bqk[:, n:n + 1]),
                   after=[w + "_pe"], prev=[f"qm{h}" for h in range(H)] + ["s_pe%d" % (2 * H // G - 1)])
        s.step("pe", "v_pe", lambda i: [nc.tensor.matmul(PS[:, 5, t * P:t * P + P], xnT[:, t * P:t * P + P], wt[:, 2, :], start=True, stop=True)
                                        for t in range(TILES)][-1], prev=["xnT", "x_out", "oT"])
        for t in range(TILES):
            s.step("dve", f"v{t}", lambda i, t=t: nc.vector.tensor_tensor(
                vaug[:, t, :, 0:HD], PS[:, 5, t * P:t * P + P].rearrange("p (h e) -> p h e", e=HD),
                bvp[:, 0, :].rearrange("p (h e) -> p h e", e=HD), ALU.add), after=["v_pe"], prev=["o_pe%d" % (2 * H // G - 1)])
        for h in range(H):
            s.step("dve", f"qm{h}", lambda i, h=h: nc.vector.tensor_scalar(qm[:, h, :], qT[:, :], hmask[:, h:h + 1], None, ALU.mult),
                   after=["q"], prev=["s_pe%d" % (2 * H // G - 1)])

        units = [(qt, g) for g in range(H // G) for qt in range(TILES)]

        def view(t, qt):
            return t[:, 0:G * P * (qt + 1)].rearrange("p (h k) -> p h k", h=G)

        def bank(u, qt):
            b = 2 * (u % 2)
            return PS[:, b:b + 2, :].rearrange("p b k -> p (b k)") if qt else PS[:, b, :]

        def scores(u, qt, g):
            n = P * (qt + 1)

            def go(i):
                for h in range(G):
                    o = bank(u, qt)[:, h * n:h * n + n]
                    nc.tensor.matmul(o, qm[:, g * G + h, qt * P:qt * P + P], kT[:, 0:n], start=True, stop=False)
                    mm = nc.tensor.matmul(o[:, n - P:n], self.identb[:, :], cmaskb[:, :], start=False, stop=True)
                return mm
            s.step("pe", f"s_pe{u}", go, after=["k"] + [f"qm{g * G + h}" for h in range(G)] + ([f"s_sub{u - 2}"] if u >= 2 else []) + ["q", "k"], prev=["y0"] if u == 1 else [])

        def softmax(u, qt):
            n = P * (qt + 1)
            a = u % 2
            src = view(bank(u, qt), qt)
            sv = view(sm[:, a, :], qt)
            s.step("dve", f"s_max{u}", lambda i: nc.vector.tensor_reduce(mx[:, a, :], src, AX.X, ALU.max),
                   after=[f"s_pe{u}"] + ([f"s_sub{u - 2}"] if u >= 2 else []), prev=[f"s_sub{len(units) - 2 + a}"])
            s.step("dve", f"s_sub{u}", lambda i: nc.vector.tensor_tensor(
                sv, src, mx[:, a, :].unsqueeze(2).broadcast_to((P, G, n)), ALU.subtract),
                after=[f"s_max{u}"] + ([f"t_pe{u - 2}"] if u >= 2 else []), prev=[f"t_pe{len(units) - 2 + a}"])
            s.step("act", f"s_exp{u}", lambda i: nc.scalar.activation(
                sm[:, a, 0:G * n], sm[:, a, 0:G * n], ACT.Exp, scale=float(HD) ** -0.5), after=[f"s_sub{u}"])

        def turn(u, qt):
            n = P * (qt + 1)
            a = u % 2

            def go(i):
                for h in range(G):
                    for k in range(qt + 1):
                        c = h * (qt + 1) + k
                        mm = nc.tensor.transpose(PS[:, 4 + c // 4, (c % 4) * P:(c % 4 + 1) * P],
                                                 sm[:, a, h * n + k * P:h * n + k * P + P], self.ident[:, :])
                return mm
            s.step("pe", f"t_pe{u}", go, after=[f"s_exp{u}"] + ([f"t{u - 1}"] if u else ["v0", "v1"]))
            s.step("act", f"t{u}", lambda i: nc.scalar.activation(
                pT[:, a, 0:G * n], PS[:, 4:6, :].rearrange("p b k -> p (b k)")[:, 0:G * n], ACT.Copy),
                after=[f"t_pe{u}"] + ([f"o_pe{u - 2}"] if u >= 2 else []), prev=[f"o_pe{len(units) - 2 + a}"])

        def output(u, qt, g):
            def go(i):
                for h in range(G):
                    hh = g * G + h
                    for k in range(qt + 1):
                        c = h * (qt + 1) + k
                        mm = nc.tensor.matmul(PS[:, 6 + qt, hh * (HD + 1):(hh + 1) * (HD + 1)], pT[:, u % 2, c * P:c * P + P],
                                              vaug[:, k, hh, :], start=(k == 0), stop=(k == qt))
                return mm
            s.step("pe", f"o_pe{u}", go, after=[f"t{u}", "v0", "v1"], prev=["ob0", "ob1"])

        for n in range(len(units) + 2):
            if n < len(units):
                scores(n, *units[n])
                softmax(n, units[n][0])
            if 1 <= n <= len(units):
                turn(n - 1, units[n - 1][0])
            if n >= 2:
                output(n - 2, *units[n - 2])
        last = len(units) - 1
        s.step("dve", "xb", lambda i: nc.vector.tensor_copy(xb[:, :], xnT[:, :]), after=["xnT"], prev=["xq0"])
        quantise(s, "xq", xb[:, :], xq[:, :], SEQ, rsc[:, 0:1], ["xb"], prev=["y_pe"])
        for t in range(TILES):
            o = PS[:, 6 + t, 0:H * (HD + 1)].rearrange("p (h e) -> p h e", e=HD + 1)
            s.step("dve", f"rl{t}", lambda i, t=t, o=o: nc.vector.reciprocal(rl[:, t, :], o[:, :, HD]),
                   after=[f"o_pe{u}" for u in range(len(units))], prev=[f"ob{t}"])
            s.step("dve", f"ob{t}", lambda i, t=t, o=o: nc.vector.tensor_tensor(
                ob[:, t, :, :], o[:, :, 0:HD], rl[:, t, :].unsqueeze(2).broadcast_to((P, H, HD)), ALU.mult),
                after=[f"rl{t}"], prev=["oT_pe"])
        s.step("pe", "oT_pe", lambda i: [nc.tensor.transpose(PS[:, 4, t * P:t * P + P], ob[:, t, :, :].rearrange("p h e -> p (h e)"),
                                                             self.ident[:, :]) for t in range(TILES)][-1], after=["ob0", "ob1", f"t{last}"])
        s.step("act", "oT", lambda i: nc.scalar.activation(oT[:, :], PS[:, 4, 0:SEQ], ACT.Copy), after=["oT_pe"], prev=["p_pe"])
        s.step("pe", "p_pe", lambda i: [nc.tensor.matmul(PS[:, 5, t * P:t * P + P], oT[:, t * P:t * P + P], wt[:, 3, :], start=True, stop=True)
                                        for t in range(TILES)][-1], after=["oT", f"t{last}"])
        s.step("pe", "y_pe", lambda i: [nc.tensor.matmul(PS[:, 2, t * P:t * P + P], xq[:, t * P:t * P + P], kq[:, :], start=True, stop=True)
                                        for t in range(TILES)][-1], after=["xq9", f"s_sub{last}"])
        s.step("dve", "y0", lambda i: nc.vector.tensor_scalar(yb[:, :, :].rearrange("p t d -> p (t d)"), PS[:, 2, 0:SEQ], ssc[:, :], None, ALU.mult), after=["y_pe"])
        s.step("dve", "y1", lambda i: nc.vector.tensor_tensor(yb[:, :, :], yb[:, :, :], fbias[:, :].unsqueeze(1).broadcast_to((P, TILES, P)), ALU.add), after=["y0"])
        s.step("dve", "x1", lambda i: nc.vector.tensor_tensor(xs[:, :, :], xs[:, :, :], yb[:, :, :], ALU.add), after=["y1"])
        s.step("dve", "x2", lambda i: nc.vector.tensor_tensor(seq_tiles(X, i + 1), xs[:, :, :], bvp[:, 1, :].unsqueeze(1).broadcast_to((P, TILES, P)), ALU.add), after=["x1"])
        s.step("dve", "x_out", lambda i: nc.vector.tensor_tensor(seq_tiles(X, i), seq_tiles(X, i), PS[:, 5, 0:SEQ].rearrange("p (t d) -> p t d", t=TILES), ALU.add),
               after=["p_pe"], prev=["x2"])
        begins = {"xs", "xnT_pe", "xnT", "xb", "y_pe", "y0", "y1", "x1", "x2"} | {n for n in s.names if n.startswith(("ln_", "xq"))}
        s.order("dve", ("xs ln_st0 qm3 qm2 qm1 qm0 qm7 v1 qm10 qm5 qm4 qm8 s_max0 qm6 v0 s_sub0 s_max1 ln_st1 s_sub1 qm9 ln_mv1 "
            "s_max2 qm11 s_sub2 ln_mv0 qm13 s_max3 s_sub3 s_max4 qm15 qm14 qm12 s_sub4 s_max5 s_sub5 ln_out1 s_max6 "
            "ln_out0 s_sub6 s_max7 xb s_sub7 xq0 xq1 xq2 xq3 xq4 xq5 xq6 xq7 xq8 xq9 rl1 rl0 ob1 ob0 y0 y1 x1 x2 x_out").split())
        s.order("act", ("q k s_exp0 t0 s_exp1 s_exp2 t1 t2 s_exp3 s_exp4 t3 ln_ln ln_rs s_exp5 t4 xnT t5 s_exp6 s_exp7 t6 t7 oT").split())
        s.order("pe", ("q_pe k_pe v_pe s_pe0 s_pe1 s_pe2 t_pe0 s_pe3 o_pe0 t_pe1 s_pe4 t_pe2 s_pe5 o_pe1 t_pe3 s_pe6 o_pe2 t_pe4 "
            "s_pe7 xnT_pe t_pe5 o_pe4 o_pe3 t_pe6 o_pe5 t_pe7 o_pe7 o_pe6 y_pe oT_pe p_pe").split())
        s.run(part=begins, at=-1, table=EXP_LN)
        s.run(NSEQ - 1, table=EXP_LN)
        s.run(part=s.names - begins, at=NSEQ - 1, table=EXP_LN)

    def L1(self):
        nc, d, PS, X = self.nc, self.d, self.PS, self.X
        H, HD = 8, 16
        FF, RANK = 512, 32
        FC = FF // P
        NB = 3
        wt = self.sb("wt", [P, 4, P])
        hmask = self.sb("hmask", [P, H])
        keep = self.sb("keep", [P, P])
        nw = self.sb("nw", [P, HD])
        u1 = self.sb("u1", [P, RANK])
        v1 = self.sb("v1", [RANK, FF])
        b1 = self.sb("b1", [P, FC])
        u2 = self.sb("u2", [P, FC, RANK])
        v2 = self.sb("v2", [RANK, P])
        b2 = self.sb("b2", [P, P])
        vaug = self.sb("vaug", [P, TILES, H, HD + 1])
        s = self.stage()
        s.step("sp", "in", lambda i: [nc.sync.dma_start(wt[:, n, :], d["L1_attn_" + w + "_T"]) for n, w in enumerate(("Wq", "Wk", "Wv", "Wo"))]
               + [nc.sync.dma_start(hmask[:, :], d["c_head8"]), nc.sync.dma_start(keep[:, :], d["c_causal01"]),
                  nc.sync.dma_start(nw[:, :], row(d["L1_attn_norm_w"], HD)), nc.sync.dma_start(u1[:, :], d["L1_ffn_U1"]),
                  nc.sync.dma_start(v1[:, :], d["L1_ffn_V1"]), nc.sync.dma_start(b1[:, :], d["L1_ffn_b1_T"]),
                  nc.sync.dma_start(u2[:, :, :], d["L1_ffn_U2"].rearrange("(c p) r -> p c r", p=P)),
                  nc.sync.dma_start(v2[:, :], d["L1_ffn_V2"]), nc.sync.dma_start(b2[:, :], row(d["L1_ffn_b2"], P))], dmas=13)
        s.step("pool", "ones", lambda i: nc.gpsimd.memset(vaug[:, :, :, HD], 1.0))
        s.run()

        xs = self.sb("xs", [P, TILES, P])
        xn = self.sb("xn", [P, TILES, P])
        x2 = self.sb("x2", [P, TILES, P])
        xnT = self.sb("xnT", [P, SEQ])
        qT = self.sb("qT", [P, SEQ])
        kT = self.sb("kT", [P, SEQ])
        qm = self.sb("qm", [P, H, SEQ])
        sT = self.sb("sT", [P, H, NB, P])
        dn = self.sb("dn", [P, TILES, H])
        dr = self.sb("dr", [P, TILES, H])
        o1 = self.sb("o1", [P, TILES, H, HD])
        sq = self.sb("sq", [P, TILES, H, HD])
        ms = self.sb("ms", [P, TILES, H])
        oT = self.sb("oT", [P, SEQ])
        pr = self.sb("pr", [RANK, SEQ])
        hT = self.sb("hT", [P, FC, SEQ])
        qr = self.sb("qr", [RANK, SEQ])

        s = self.stage()
        s.step("dve", "xs", lambda i: nc.vector.tensor_scalar(xs[:, :, :], seq_tiles(X, i + 1), 1.0, None, ALU.mult), prev=["x1"])
        self.layernorm(s, xs, xn, "ln", ["xs"], wprev=["xnT_pe"])
        s.step("pe", "xnT_pe", lambda i: [nc.tensor.transpose(PS[:, 4, t * P:t * P + P], xn[:, t, :], self.ident[:, :]) for t in range(TILES)][-1],
               after=["ln_out0", "ln_out1", "oT"], prev=["xnT"])
        s.step("act", "xnT", lambda i: nc.scalar.activation(xnT[:, :], PS[:, 4, 0:SEQ], ACT.Copy), after=["xnT_pe", "q_pe", "k_pe", "v_pe", "pr_pe"])
        for n, (w, to) in enumerate((("q", qT), ("k", kT))):
            s.step("pe", w + "_pe", lambda i, n=n: nc.tensor.matmul(PS[:, 5, n * SEQ:(n + 1) * SEQ], wt[:, n, :], xnT[:, :], start=True, stop=True),
                   prev=["xnT", "x2", "x_out"])
            s.step("act", w, lambda i, n=n, to=to: nc.scalar.activation(to[:, :], PS[:, 5, n * SEQ:(n + 1) * SEQ], ACT.Copy),
                   after=["q_pe", "k_pe"], prev=[f"{x}{h}" for x in ("qm", "s_pe") for h in range(H)])
        s.step("pe", "v_pe", lambda i: [nc.tensor.matmul(PS[:, 6, t * P:t * P + P], xnT[:, t * P:t * P + P], wt[:, 2, :], start=True, stop=True)
                                        for t in range(TILES)][-1], prev=["xnT", "o1_0", "o1_1", "qr"])
        s.step("dve", "v", lambda i: nc.vector.tensor_copy(
            vaug[:, :, :, 0:HD], PS[:, 6, 0:SEQ].rearrange("p (t h e) -> p t h e", t=TILES, e=HD)), after=["v_pe"], prev=["o_pe"])
        for h in range(H):
            s.step("dve", f"qm{h}", lambda i, h=h: nc.vector.tensor_scalar(qm[:, h, :], qT[:, :], hmask[:, h:h + 1], None, ALU.mult),
                   after=["q"], prev=[f"s_pe{h}"])
        for h in range(H):
            b = h % 4

            def scores(i, h=h, b=b):
                nc.tensor.matmul(PS[:, b, 0:SEQ], kT[:, 0:P], qm[:, h, :], start=True, stop=True)
                return nc.tensor.matmul(PS[:, b, SEQ:SEQ + P], kT[:, P:SEQ], qm[:, h, P:SEQ], start=True, stop=True)
            s.step("pe", f"s_pe{h}", scores, after=["k", f"qm{h}"] + ([f"sd{h - 4}", f"sf{h - 4}"] if h >= 4 else []),
                   prev=[f"sd{h + 4}", f"sf{h + 4}", "pr", "gelu"] if h < 4 else [])
            s.step("dve", f"sd{h}", lambda i, h=h, b=b: nc.vector.tensor_tensor(
                sT[:, h, 0:NB:2, :], PS[:, b, 0:NB * P].rearrange("p (n q) -> p n q", q=P)[:, 0:NB:2, :],
                keep[:, :].unsqueeze(1).broadcast_to((P, 2, P)), ALU.mult), after=[f"s_pe{h}"], prev=["o_pe"])
            s.step("act", f"sf{h}", lambda i, h=h, b=b: nc.scalar.activation(sT[:, h, 1, :], PS[:, b, P:SEQ], ACT.Copy),
                   after=[f"sd{h}"], prev=["o_pe"])

        def out(i):
            for t in range(TILES):
                for h in range(H):
                    o = PS[:, 6 + t, h * (HD + 1):(h + 1) * (HD + 1)]
                    if t == 0:
                        mm = nc.tensor.matmul(o, sT[:, h, 0, :], vaug[:, 0, h, :], start=True, stop=True)
                    else:
                        nc.tensor.matmul(o, sT[:, h, 1, :], vaug[:, 0, h, :], start=True, stop=False)
                        mm = nc.tensor.matmul(o, sT[:, h, 2, :], vaug[:, 1, h, :], start=False, stop=True)
            return mm
        s.step("pe", "o_pe", out, after=["v"] + [f"{x}{h}" for x in ("sd", "sf") for h in range(H)], prev=["o1_0", "o1_1"])
        s.step("pe", "pr_pe", lambda i: nc.tensor.matmul(PS[0:RANK, 0, 0:SEQ], u1[:, :], xnT[:, :], start=True, stop=True), after=["sd4", "sf4"], prev=["xnT"])
        s.step("dve", "pr", lambda i: nc.vector.tensor_copy(pr[:, :], PS[0:RANK, 0, 0:SEQ]), after=["pr_pe"], prev=[f"h_pe{c}" for c in range(FC)])
        for c in range(FC):
            s.step("pe", f"h_pe{c}", lambda i, c=c: nc.tensor.matmul(PS[:, (1, 2, 3, 0)[c], 0:SEQ], v1[:, c * P:c * P + P], pr[:, :], start=True, stop=True),
                   after=["pr", "sd7", "sf7", "sd6", "sf6", "sd5", "sf5"])
        for t in range(TILES):
            o = PS[:, 6 + t, 0:H * (HD + 1)].rearrange("p (h e) -> p h e", e=HD + 1)
            s.step("dve", f"dr{t}", lambda i, t=t, o=o: nc.vector.tensor_copy(dr[:, t, :], o[:, :, HD]), after=["o_pe"], prev=[f"dn{t}"])
            s.step("dve", f"dn{t}", lambda i, t=t: nc.vector.scalar_tensor_tensor(dn[:, t, :], dr[:, t, :], -1.0, dr[:, t, :], ALU.mult, ALU.max),
                   after=[f"dr{t}"], prev=["o1_0", "o1_1"])
        s.step("dve", "dm", lambda i: nc.vector.tensor_scalar(dn[:, :, :], dn[:, :, :], 1.0, None, ALU.max), after=["dn0", "dn1"])
        s.step("dve", "di", lambda i: nc.vector.reciprocal(dn[:, :, :], dn[:, :, :]), after=["dm"])
        for t in range(TILES):
            o = PS[:, 6 + t, 0:H * (HD + 1)].rearrange("p (h e) -> p h e", e=HD + 1)
            s.step("dve", f"o1_{t}", lambda i, t=t, o=o: nc.vector.tensor_tensor(
                o1[:, t, :, :], o[:, :, 0:HD], dn[:, t, :].unsqueeze(2).broadcast_to((P, H, HD)), ALU.mult), after=["di"], prev=["oT_pe"])
        s.step("dve", "sq", lambda i: nc.vector.tensor_tensor(sq[:, :, :, :], o1[:, :, :, :], o1[:, :, :, :], ALU.mult), after=["o1_0", "o1_1"], prev=["ms"])
        s.step("dve", "ms", lambda i: nc.vector.tensor_reduce(ms[:, :, :], sq[:, :, :, :], AX.X, ALU.add), after=["sq"], prev=["o2"])
        s.step("act", "ms_ln", lambda i: nc.scalar.activation(ms[:, :, :], ms[:, :, :], ACT.Ln, bias=self.eps[:, :], scale=1.0 / HD), after=["ms"])
        s.step("act", "ms_rs", lambda i: nc.scalar.activation(ms[:, :, :], ms[:, :, :], ACT.Exp, scale=-0.5), after=["ms_ln"])
        s.step("dve", "o2", lambda i: nc.vector.tensor_tensor(
            o1[:, :, :, :].rearrange("p t h e -> p (t h) e"), o1[:, :, :, :].rearrange("p t h e -> p (t h) e"),
            ms[:, :, :].rearrange("p t h -> p (t h)").unsqueeze(2).broadcast_to((P, TILES * H, HD)), ALU.mult), after=["ms_rs"])
        s.step("dve", "o3", lambda i: nc.vector.tensor_tensor(
            o1[:, :, :, :].rearrange("p t h e -> p (t h) e"), o1[:, :, :, :].rearrange("p t h e -> p (t h) e"),
            nw[:, :].unsqueeze(1).broadcast_to((P, TILES * H, HD)), ALU.mult), after=["o2"])
        s.step("pe", "oT_pe", lambda i: [nc.tensor.transpose(PS[:, 4, t * P:t * P + P], o1[:, t, :, :].rearrange("p h e -> p (h e)"),
                                                             self.ident[:, :]) for t in range(TILES)][-1], after=["o3"], prev=["xnT"])
        s.step("act", "oT", lambda i: nc.scalar.activation(oT[:, :], PS[:, 4, 0:SEQ], ACT.Copy), after=["oT_pe"], prev=["p_pe"])

        def gelu(i):
            for c in range(FC):
                op = nc.scalar.activation(hT[:, c, :], PS[:, (1, 2, 3, 0)[c], 0:SEQ], ACT.Gelu_apprx_tanh, bias=b1[:, c:c + 1])
            nc.scalar.preload_act_table_set(EXP_LN)
            return op
        s.step("act", "gelu", gelu, after=[f"h_pe{c}" for c in range(FC)], prev=["qr_pe"])
        s.step("pe", "qr_pe", lambda i: [nc.tensor.matmul(PS[0:RANK, 7, SEQ:2 * SEQ], u2[:, c, :], hT[:, c, :], start=(c == 0), stop=(c == FC - 1))
                                         for c in range(FC)][-1], after=["gelu", "o1_0", "o1_1"], prev=["qr"])
        s.step("dve", "qr", lambda i: nc.vector.tensor_copy(qr[:, :], PS[0:RANK, 7, SEQ:2 * SEQ]), after=["qr_pe"], prev=["p_pe"])

        def back(i):
            for t in range(TILES):
                nc.tensor.matmul(PS[:, 5, t * P:t * P + P], oT[:, t * P:t * P + P], wt[:, 3, :], start=True, stop=True)
            for t in range(TILES):
                mm = nc.tensor.matmul(PS[:, 5, SEQ + t * P:SEQ + t * P + P], qr[:, t * P:t * P + P], v2[:, :], start=True, stop=True)
            return mm
        s.step("pe", "p_pe", back, after=["oT", "qr", "q", "k"])
        s.step("dve", "x1", lambda i: nc.vector.tensor_tensor(seq_tiles(X, i + 1), xs[:, :, :], b2[:, :].unsqueeze(1).broadcast_to((P, TILES, P)), ALU.add), after=["ln_out0", "ln_out1"])
        s.step("dve", "x2", lambda i: nc.vector.tensor_tensor(x2[:, :, :], seq_tiles(X, i), PS[:, 5, 0:SEQ].rearrange("p (t d) -> p t d", t=TILES), ALU.add), after=["p_pe"], prev=["x1", "x_out"])
        s.step("dve", "x_out", lambda i: nc.vector.tensor_tensor(seq_tiles(X, i), x2[:, :, :], PS[:, 5, SEQ:2 * SEQ].rearrange("p (t d) -> p t d", t=TILES), ALU.add), after=["x2"])
        begins = {"xs", "xnT_pe", "xnT", "x1"} | {n for n in s.names if n.startswith("ln_")}
        s.order("pe", ("k_pe q_pe v_pe s_pe3 s_pe0 s_pe2 s_pe1 s_pe6 s_pe4 s_pe5 s_pe7 pr_pe o_pe h_pe1 h_pe2 h_pe3 h_pe0 oT_pe "
            "qr_pe xnT_pe p_pe").split())
        s.order("act", ("q k sf2 sf0 sf3 sf1 sf4 sf6 sf5 sf7 ms_ln ms_rs gelu oT ln_ln ln_rs xnT").split())
        s.order("dve", ("xs qm3 qm2 qm0 ln_st1 sd3 qm1 qm5 sd2 qm6 sd0 qm4 sd1 ln_st0 qm7 sd4 sd6 v sd5 sd7 pr dr0 dn0 dr1 dn1 dm "
            "di o1_0 o1_1 sq ms ln_mv0 ln_mv1 o2 o3 ln_out0 ln_out1 qr x2 x_out x1").split())
        s.run(part=begins, at=-1, table=EXP_LN)
        s.run(NSEQ - 1, table=EXP_LN)
        s.run(part=s.names - begins, at=NSEQ - 1, table=EXP_LN)

    def L2(self):
        nc, d, PS, X = self.nc, self.d, self.PS, self.X
        H, R = 8, 64
        G = 4
        PAIRS = H // 2
        LEAVES, DEPTH = 256, 8
        wq = self.sb("wq", [P, H * R])
        wk = self.sb("wk", [P, H * R])
        wv = self.sb("wv", [P, H * P])
        fq = self.sb("fq", [P, P])
        rt = self.sb("rt", [P, LEAVES - 1])
        lv = self.sb("lv", [P, 2, P])
        wo = self.sb("wo", [P, P])
        bo = self.sb("bo", [P, P])
        qz = self.sb("qz", [P, H, SEQ])
        s = self.stage()
        s.step("sp", "in", lambda i: [nc.sync.dma_start(wq[:, :], d["L2_attn_Wq_T"]), nc.sync.dma_start(wk[:, :], d["L2_attn_Wk_T"]),
                                      nc.sync.dma_start(wv[:, :], d["L2_attn_Wv_T"]), nc.sync.dma_start(fq[:, :], d["L2_ffn_Wq_T"]),
                                      nc.sync.dma_start(rt[:, :], d["L2_ffn_routers_T"]),
                                      nc.sync.dma_start(lv[:, :, :], d["L2_ffn_leaf_values"].rearrange("(c p) d -> p c d", p=P)),
                                      nc.sync.dma_start(wo[:, :], d["L2_ffn_Wout_w_T"]), nc.sync.dma_start(bo[:, :], row(d["L2_ffn_Wout_b"], P))], dmas=8)
        s.step("pool", "zero", lambda i: nc.gpsimd.memset(qz[:, :, :], 0.0))
        s.run()

        xs = self.sb("xs", [P, TILES, P])
        xn = self.sb("xn", [P, TILES, P])
        xnT = self.sb("xnT", [P, SEQ])
        kT = self.sb("kT", [P, PAIRS, SEQ])
        v = self.sb("v", [P, TILES, H * P])
        sm = self.sb("sm", [P, 2, G, SEQ])
        pn = self.sb("pn", [P, 2, G, SEQ])
        pT = self.sb("pT", [P, 2, G * SEQ])
        mx = self.sb("mx", [P, 2, G])
        sl = self.sb("sl", [P, 2, G])
        fqT = self.sb("fqT", [P, SEQ])
        gt = self.sb("gt", [P, TILES, LEAVES])
        gl = self.sb("gl", [P, TILES, LEAVES])
        lp = [self.sb(f"lp{n}", [P, TILES, LEAVES]) for n in range(2)]
        lpT = self.sb("lpT", [P, 2, SEQ])
        rT = self.sb("rT", [P, SEQ])

        s = self.stage()
        s.step("dve", "xs", lambda i: nc.vector.tensor_scalar(xs[:, :, :], seq_tiles(X, i + 1), 1.0, None, ALU.mult), prev=["x1"])
        self.layernorm(s, xs, xn, "ln", ["xs"], wprev=["xnT_pe"])
        s.step("pe", "xnT_pe", lambda i: [nc.tensor.transpose(PS[:, 1, t * P:t * P + P], xn[:, t, :], self.ident[:, :]) for t in range(TILES)][-1],
               after=["ln_out0", "ln_out1", "s_sub2"], prev=["xnT"])
        s.step("act", "xnT", lambda i: nc.scalar.activation(xnT[:, :], PS[:, 1, 0:SEQ], ACT.Copy), after=["xnT_pe", "q_pe0", "q_pe1", "k_pe0", "k_pe1", "v_pe0", "v_pe1", "fq_pe"])
        for b in range(2):
            s.step("pe", f"q_pe{b}", lambda i, b=b: [nc.tensor.matmul(PS[:, b, c * SEQ:(c + 1) * SEQ], wq[:, (2 * b + c) * P:(2 * b + c + 1) * P], xnT[:, :],
                                                                      start=True, stop=True) for c in range(2)][-1], prev=["xnT", "s_sub2", "s_sub3"])
            for half in range(2):
                r = slice(half * R, half * R + R)
                s.step("act", f"q{b}{half}", lambda i, b=b, half=half, r=r: nc.scalar.activation(
                    qz[r, 4 * b + half:4 * b + half + 3:2, :], PS[r, b, :].rearrange("p (c n) -> p c n", c=2), ACT.Copy),
                    after=[f"q_pe{b}"], prev=["s_pe3"])
        for b in range(2):
            s.step("pe", f"k_pe{b}", lambda i, b=b: [nc.tensor.matmul(PS[:, 2 + b, c * SEQ:(c + 1) * SEQ], wk[:, (2 * b + c) * P:(2 * b + c + 1) * P], xnT[:, :],
                                                                      start=True, stop=True) for c in range(2)][-1], prev=["xnT", "s_sub3"])
            s.step("act", f"k{b}", lambda i, b=b: nc.scalar.activation(
                kT[:, 2 * b:2 * b + 2, :], PS[:, 2 + b, :].rearrange("p (c n) -> p c n", c=2), ACT.Copy), after=[f"k_pe{b}"], prev=["s_pe3"])
        for t in range(TILES):
            s.step("pe", f"v_pe{t}", lambda i, t=t: [nc.tensor.matmul(PS[:, 4 + 2 * t + c, :], xnT[:, t * P:t * P + P], wv[:, c * 512:(c + 1) * 512],
                                                                      start=True, stop=True) for c in range(2)][-1], 
                   prev=["xnT"] + (["lpT", "rT"] if t == 0 else ["x_out"]))
            s.step("dve", f"v{t}", lambda i, t=t: nc.vector.tensor_copy(v[:, t, :], PS[:, 4 + 2 * t:6 + 2 * t, :].rearrange("p b n -> p (b n)")),
                   after=[f"v_pe{t}"], prev=["o_pe3"])
        s.step("pe", "fq_pe", lambda i: nc.tensor.matmul(PS[:, 4, 0:SEQ], fq[:, :], xnT[:, :], start=True, stop=True), after=["v0"])
        s.step("act", "fqT", lambda i: nc.scalar.activation(fqT[:, :], PS[:, 4, 0:SEQ], ACT.Copy), after=["fq_pe"], prev=["g_pe"])

        units = [(qt, g) for qt in range(TILES) for g in range(H // G)]

        def bank(u):
            b = 2 * (u % 2)
            return PS[:, b:b + 2, :].rearrange("p b (h k) -> p (b h) k", h=2)

        def scores(u, qt, g):
            def go(i):
                for h in range(G):
                    hh = g * G + h
                    mm = nc.tensor.matmul(bank(u)[:, h, :], qz[:, hh, qt * P:qt * P + P], kT[:, hh // 2, :], start=True, stop=True)
                return mm
            s.step("pe", f"s_pe{u}", go, after=["q00", "q01", "q10", "q11", "k0", "k1"] + ([f"s_sub{u - 2}"] if u >= 2 else []))

        def softmax(u):
            a = u % 2
            old = [f"s_sub{u - 2}"] if u >= 2 else []
            s.step("dve", f"s_max{u}", lambda i: nc.vector.tensor_reduce(mx[:, a, :], bank(u), AX.X, ALU.max),
                   after=[f"s_pe{u}"] + old, prev=[f"s_sub{2 + a}"])
            s.step("dve", f"s_sub{u}", lambda i: nc.vector.tensor_tensor(
                sm[:, a, :, :], bank(u), mx[:, a, :].unsqueeze(2).broadcast_to((P, G, SEQ)), ALU.subtract),
                after=[f"s_max{u}"] + ([f"s_mul{u - 2}"] if u >= 2 else []), prev=[f"s_mul{2 + a}"])
            s.step("act", f"s_exp{u}", lambda i: nc.scalar.activation(sm[:, a, :, :], sm[:, a, :, :], ACT.Exp), after=[f"s_sub{u}"])
            s.step("dve", f"s_sum{u}", lambda i: nc.vector.tensor_reduce(sl[:, a, :], sm[:, a, :, :], AX.X, ALU.add),
                   after=[f"s_exp{u}"] + ([f"s_mul{u - 2}"] if u >= 2 else []), prev=[f"s_mul{2 + a}"])
            s.step("dve", f"s_inv{u}", lambda i: nc.vector.reciprocal(sl[:, a, :], sl[:, a, :]), after=[f"s_sum{u}"])
            s.step("dve", f"s_mul{u}", lambda i: nc.vector.tensor_tensor(
                pn[:, a, :, :], sm[:, a, :, :], sl[:, a, :].unsqueeze(2).broadcast_to((P, G, SEQ)), ALU.mult),
                after=[f"s_inv{u}"] + ([f"t_pe{u - 2}"] if u >= 2 else []), prev=[f"t_pe{2 + a}"])

        def turn(u):
            a = u % 2

            def go(i):
                for c in range(2 * G):
                    mm = nc.tensor.transpose(PS[:, 4 + c // 4, (c % 4) * P:(c % 4 + 1) * P],
                                             pn[:, a, c // 2, (c % 2) * P:(c % 2) * P + P], self.ident[:, :])
                return mm
            s.step("pe", f"t_pe{u}", go, after=[f"s_mul{u}"] + ([f"t{u - 1}"] if u else ["v0", "fqT", "ge"]))
            s.step("act", f"t{u}", lambda i: nc.scalar.activation(pT[:, a, :], PS[:, 4:6, :].rearrange("p b k -> p (b k)"), ACT.Copy),
                   after=[f"t_pe{u}"] + ([f"o_pe{u - 2}"] if u >= 2 else []), prev=[f"o_pe{2 + a}"])

        def output(u, qt, g):
            def go(i):
                for c in range(2 * G):
                    hh, k = g * G + c // 2, c % 2
                    mm = nc.tensor.matmul(PS[:, 6 + qt, 0:P], pT[:, u % 2, c * P:c * P + P], v[:, k, hh * P:(hh + 1) * P],
                                          start=(g == 0 and c == 0), stop=False)
                return mm
            s.step("pe", f"o_pe{u}", go, after=[f"t{u}", "v0", "v1"] + ([f"o_pe{u - 1}"] if g else []))

        def gate():
            s.step("pe", "g_pe", lambda i: [nc.tensor.matmul(PS[:, 5, t * SEQ:t * SEQ + LEAVES - 1], fqT[:, t * P:t * P + P], rt[:, :], start=True, stop=True)
                                            for t in range(TILES)][-1], after=["fqT", "v0"])
            s.step("act", "ge", lambda i: nc.scalar.activation(gt[:, :, 0:LEAVES - 1], PS[:, 5, :].rearrange("p (t n) -> p t n", t=TILES)[:, :, 0:LEAVES - 1],
                                                               ACT.Exp, scale=-1.0), after=["g_pe"], prev=["lv7"])
            s.step("act", "g1", lambda i: nc.scalar.activation(gt[:, :, 0:LEAVES - 1], gt[:, :, 0:LEAVES - 1], ACT.Ln, bias=1.0), after=["ge"])
            s.step("act", "g2", lambda i: nc.scalar.activation(gt[:, :, 0:LEAVES - 1], gt[:, :, 0:LEAVES - 1], ACT.Exp, scale=-1.0), after=["g1"])
            s.step("pool", "g3", lambda i: nc.gpsimd.tensor_scalar(gl[:, :, 0:LEAVES - 1], gt[:, :, 0:LEAVES - 1], -1.0, 1.0, ALU.mult, ALU.add),
                   after=["g2"], prev=["lv7"], solo=True)
            for lev in range(DEPTH):
                n = 2 ** lev
                src = lp[lev % 2][:, :, 0:n]
                dst = lp[(lev + 1) % 2][:, :, 0:2 * n].rearrange("p t (n two) -> p t n two", two=2)

                def both(i, n=n, src=src, dst=dst):
                    for side, g in ((0, gl), (1, gt)):
                        if n == 1:
                            op = nc.gpsimd.tensor_copy(dst[:, :, :, side], g[:, :, 0:1])
                        else:
                            op = nc.gpsimd.tensor_tensor(dst[:, :, :, side], src, g[:, :, n - 1:2 * n - 1], ALU.mult)
                    return op
                s.step("pool", f"lv{lev}", both, after=["g3"] if lev == 0 else [f"lv{lev - 1}"], prev=["lpT_pe"], solo=True)

        for n in range(len(units) + 2):
            if n < len(units):
                scores(n, *units[n])
                softmax(n)
            if n == 0:
                gate()
            if 1 <= n <= len(units):
                turn(n - 1)
            if n >= 2:
                output(n - 2, *units[n - 2])
        leaf = lp[DEPTH % 2]
        s.step("pe", "lpT_pe", lambda i: [nc.tensor.transpose(PS[:, 4, (c * 2 + t) * P:(c * 2 + t + 1) * P], leaf[:, t, c * P:c * P + P], self.ident[:, :])
                                          for c in range(2) for t in range(TILES)][-1], after=["lv7", "t3"])
        s.step("act", "lpT", lambda i: nc.scalar.activation(lpT[:, :, :].rearrange("p c n -> p (c n)"), PS[:, 4, :], ACT.Copy), after=["lpT_pe"], prev=["rT_pe"])
        s.step("pe", "rT_pe", lambda i: [nc.tensor.matmul(PS[:, 5, 0:SEQ], lv[:, c, :], lpT[:, c, :], start=(c == 0), stop=(c == 1)) for c in range(2)][-1],
               after=["lpT"])
        s.step("act", "rT", lambda i: nc.scalar.activation(rT[:, :], PS[:, 5, 0:SEQ], ACT.Copy), after=["rT_pe"], prev=["w_pe"])
        s.step("pe", "w_pe", lambda i: [nc.tensor.matmul(PS[:, 6 + t, 0:P], rT[:, t * P:t * P + P], wo[:, :], start=False, stop=True) for t in range(TILES)][-1],
               after=["rT", "o_pe1", "o_pe3"])
        s.step("dve", "x1", lambda i: nc.vector.tensor_tensor(seq_tiles(X, i + 1), xs[:, :, :], bo[:, :].unsqueeze(1).broadcast_to((P, TILES, P)), ALU.add), after=["ln_out0", "ln_out1"])
        s.step("dve", "x_out", lambda i: nc.vector.tensor_tensor(seq_tiles(X, i), seq_tiles(X, i), PS[:, 6:8, 0:P], ALU.add), after=["w_pe"], prev=["x1"])
        begins = {"xs", "xnT_pe", "xnT", "x1"} | {n for n in s.names if n.startswith("ln_")}
        s.order("pool", ("g3 lv0 lv1 lv2 lv3 lv4 lv5 lv6 lv7").split())
        s.order("dve", ("v0 xs ln_st0 s_max0 s_sub0 s_max1 s_sum0 s_sub1 s_inv0 s_max2 s_sum1 s_mul0 s_inv1 s_sub2 s_max3 s_mul1 "
            "s_sum2 v1 s_inv2 s_sub3 ln_mv0 s_mul2 s_sum3 s_inv3 s_mul3 ln_st1 ln_mv1 ln_out0 ln_out1 x_out x1").split())
        s.order("act", ("q01 q00 k0 k1 q11 q10 fqT s_exp0 s_exp1 ge t0 s_exp2 g1 g2 t1 s_exp3 t2 t3 ln_ln ln_rs lpT rT xnT").split())
        s.order("pe", ("q_pe0 k_pe0 k_pe1 q_pe1 v_pe0 s_pe0 fq_pe s_pe1 v_pe1 s_pe2 s_pe3 g_pe t_pe0 t_pe1 o_pe0 t_pe2 o_pe1 t_pe3 "
            "o_pe2 lpT_pe o_pe3 rT_pe xnT_pe w_pe").split())
        s.run(part=begins, at=-1, table=EXP_LN)
        s.run(NSEQ - 1, table=EXP_LN)
        s.run(part=s.names - begins, at=NSEQ - 1, table=EXP_LN)

    def L3a(self):
        nc, d, PS, X, Z = self.nc, self.d, self.PS, self.X, self.Z
        CH, NS, TAPS, DR = 2, 16, 4, 8
        G = 4
        UN = NS // G
        PAD = TAPS - 1
        pre = "L3_attn_"
        lg = self.sb("lg", [P, 2])
        wi = self.sb("wi", [P, 4 * P])
        wx = self.sb("wx", [P, CH, DR + 2 * NS])
        wd = self.sb("wd", [P, CH * P])
        wo = self.sb("wo", [P, CH, P])
        cw = self.sb("cw", [P, CH, TAPS])
        cb, db, dd = (self.sb(n, [P, CH]) for n in ("cb", "db", "dd"))
        al = self.sb("al", [P, CH, NS])
        na = self.sb("na", [P, CH, NS])
        res = self.sb("res", [P, 1])
        xd = self.sb("xd", [P, SEQ])
        xp = self.sb("xp", [P, CH, PAD + SEQ])
        dA = self.sb("dA", [P, CH, G, SEQ])
        s = self.stage()
        s.step("pool", "z0", lambda i: nc.gpsimd.memset(wd[:, :], 0.0))
        s.step("pool", "z1", lambda i: nc.gpsimd.memset(xd[:, :], 0.0))
        s.step("pool", "z2", lambda i: nc.gpsimd.memset(xp[:, :, :], 0.0))
        s.step("pool", "z3", lambda i: nc.gpsimd.memset(dA[:, :, :, :], 0.0))
        s.step("sp", "in", lambda i: [
            nc.sync.dma_start(lg[:, 0:1], d[pre + "ln_g"].rearrange("(p a) -> p a", a=1)),
            nc.sync.dma_start(lg[:, 1:2], d[pre + "ln_b"].rearrange("(p a) -> p a", a=1)),
            nc.sync.dma_start(wi[:, :], d[pre + "in_proj_w_T"]), nc.sync.dma_start(wx[:, :, :], d[pre + "x_proj_w_T"]),
            nc.sync.dma_start(wd[0:DR, :], d[pre + "dt_proj_w_T"]), nc.sync.dma_start(wo[:, :, :], d[pre + "out_proj_w_T"]),
            nc.sync.dma_start(cw[:, :, :], d[pre + "conv_w_T"]), nc.sync.dma_start(cb[:, :], d[pre + "conv_b_T"]),
            nc.sync.dma_start(db[:, :], d[pre + "dt_proj_b_T"]), nc.sync.dma_start(dd[:, :], d[pre + "D_T"]),
            nc.sync.dma_start(al[:, :, :], d[pre + "A_log_T"]), nc.sync.dma_start(res[:, :], row(d[pre + "res_scale"], 1))],
            after=["z0"], dmas=12)
        s.step("act", "ea", lambda i: nc.scalar.activation(na[:, :, :], al[:, :, :], ACT.Exp), after=["in"])
        s.step("dve", "na", lambda i: nc.vector.tensor_scalar(na[:, :, :], na[:, :, :], -1.0, None, ALU.mult), after=["ea"])
        s.run()

        xs = self.sb("xs", [P, TILES, P])
        xn = self.sb("xn", [P, TILES, P])
        xm = self.sb("xm", [P, TILES, P])
        xmT = self.sb("xmT", [P, SEQ])
        zs = self.sb("zs", [P, CH, SEQ])
        zg = self.sb("zg", [P, CH, SEQ])
        xc = self.sb("xc", [P, CH, SEQ])
        xg = self.sb("xg", [P, CH, SEQ])
        dv = self.sb("dv", [P, CH, SEQ])
        de = self.sb("de", [P, CH, SEQ])
        dt = self.sb("dt", [P, CH, SEQ])
        dx = self.sb("dx", [P, CH, SEQ])
        db_x = self.sb("db_x", [P, CH, G, SEQ])
        hs = self.sb("hs", [P, CH, G, SEQ])
        hc = self.sb("hc", [P, CH, G, SEQ])
        yT = self.sb("yT", [P, CH, SEQ])

        def flat(t):
            return t.rearrange("p g n -> p (g n)")

        s = self.stage()
        s.step("dve", "xs", lambda i: nc.vector.tensor_scalar(xs[:, :, :], seq_tiles(X, i + 1), 1.0, None, ALU.mult), prev=["x1"])
        self.layernorm(s, xs, xn, "ln", ["xs"], wprev=["lm_out0", "lm_out1", "z_pe", "x1"])
        s.step("pe", "z_pe", lambda i: [nc.tensor.transpose(PS[:, 4, SEQ + t * P:SEQ + t * P + P], xn[:, t, :], self.ident[:, :]) for t in range(TILES)][-1],
               after=["ln_out0", "ln_out1", "dv0", "dv1"], prev=["xmT"])

        def z_put(i):
            for r, c in ((slice(0, P // 2), 0), (slice(P // 2, P), 1)):
                op = nc.vector.tensor_scalar(Z[r, bass.ds(i + 1, 1), c:c + SEQ], PS[r, 4, SEQ:2 * SEQ].unsqueeze(1), 1.0, None, ALU.mult)
            return op
        s.step("dve", "z_put", z_put, after=["z_pe"])
        self.layernorm(s, xn, xm, "lm", ["ln_out0", "ln_out1"], wprev=["xmT_pe"])
        s.step("pe", "xmT_pe", lambda i: [nc.tensor.transpose(PS[:, 4, t * P:t * P + P], xm[:, t, :], self.ident[:, :]) for t in range(TILES)][-1],
               after=["lm_out0", "lm_out1", "z_put"])
        s.step("act", "xmT", lambda i: nc.scalar.activation(xmT[:, :], PS[:, 4, 0:SEQ], ACT.Identity, bias=lg[:, 1:2], scale=lg[:, 0:1]),
               after=["xmT_pe", "in_pe0", "in_pe1"])
        for b in range(2):
            s.step("pe", f"in_pe{b}", lambda i, b=b: [nc.tensor.matmul(PS[:, b, c * SEQ:(c + 1) * SEQ], wi[:, (2 * b + c) * P:(2 * b + c + 1) * P], xmT[:, :],
                                                                       start=True, stop=True) for c in range(2)][-1], prev=["xmT", f"dbx{UN - 1}0", f"dbx{UN - 1}1"])
        s.step("act", "xp", lambda i: nc.scalar.activation(xp[:, :, PAD:PAD + SEQ], PS[:, 0, :].rearrange("p (c n) -> p c n", c=CH), ACT.Copy),
               after=["in_pe0"], prev=[f"cv{PAD}0", f"cv{PAD}1"])
        s.step("act", "ze", lambda i: nc.scalar.activation(zg[:, :, :], PS[:, 1, :].rearrange("p (c n) -> p c n", c=CH), ACT.Exp, scale=-1.0),
               after=["in_pe1"], prev=["z_s"])
        for c in range(CH):
            s.step("dve", f"cv0{c}", lambda i, c=c: nc.vector.tensor_scalar(xc[:, c, :], xp[:, c, 0:SEQ], cw[:, c, 0:1], cb[:, c:c + 1], ALU.mult, ALU.add),
                   after=["xp"], prev=["y1%d" % c, "xd_pe"])
        for k in range(1, TAPS):
            for c in range(CH):
                s.step("dve", f"cv{k}{c}", lambda i, c=c, k=k: nc.vector.scalar_tensor_tensor(
                    xc[:, c, :], xp[:, c, k:k + SEQ], cw[:, c, k:k + 1], xc[:, c, :], ALU.mult, ALU.add), after=[f"cv{k - 1}{c}"])
        s.step("act", "xe", lambda i: nc.scalar.activation(xg[:, :, :], xc[:, :, :], ACT.Exp, scale=-1.0), after=[f"cv{PAD}0", f"cv{PAD}1"], prev=["x_s"])
        s.step("act", "z_1", lambda i: nc.scalar.activation(zg[:, :, :], zg[:, :, :], ACT.Ln, bias=1.0), after=["ze"])
        s.step("act", "z_r", lambda i: nc.scalar.activation(zg[:, :, :], zg[:, :, :], ACT.Exp, scale=-1.0), after=["z_1"])
        s.step("dve", "z_s", lambda i: nc.vector.tensor_tensor(zs[:, :, :], zg[:, :, :], PS[:, 1, :].rearrange("p (c n) -> p c n", c=CH), ALU.mult),
               after=["z_r"], prev=["y2"])
        s.step("act", "x_1", lambda i: nc.scalar.activation(xg[:, :, :], xg[:, :, :], ACT.Ln, bias=1.0), after=["xe"])
        s.step("act", "x_r", lambda i: nc.scalar.activation(xg[:, :, :], xg[:, :, :], ACT.Exp, scale=-1.0), after=["x_1"])
        s.step("dve", "x_s", lambda i: nc.vector.tensor_tensor(xc[:, :, :], xc[:, :, :], xg[:, :, :], ALU.mult), after=["x_r"])
        s.step("pe", "xd_pe", lambda i: [nc.tensor.matmul(PS[0:DR + 2 * NS, 5, 0:SEQ], wx[:, c, :], xc[:, c, :], start=(c == 0), stop=(c == CH - 1))
                                         for c in range(CH)][-1], after=["x_s"], prev=["x_out"])
        s.step("act", "xd", lambda i: nc.scalar.activation(xd[0:DR + 2 * NS, :], PS[0:DR + 2 * NS, 5, 0:SEQ], ACT.Copy), after=["xd_pe"],
               prev=[f"c_pe{UN - 1}", f"b_pe{UN - 1}", "dt_pe"])
        s.step("pe", "dt_pe", lambda i: [nc.tensor.matmul(PS[:, 4, c * SEQ:(c + 1) * SEQ], wd[:, c * P:c * P + P], xd[:, :], start=True, stop=True)
                                         for c in range(CH)][-1], after=["xd"], prev=["xmT"])
        for c in range(CH):
            s.step("dve", f"dv{c}", lambda i, c=c: nc.vector.tensor_scalar(dv[:, c, :], PS[:, 4, c * SEQ:(c + 1) * SEQ], db[:, c:c + 1], None, ALU.add),
                   after=["dt_pe"], prev=["dt"])
        s.step("dve", "da", lambda i: nc.vector.scalar_tensor_tensor(de[:, :, :], dv[:, :, :], -1.0, dv[:, :, :], ALU.mult, ALU.max),
               after=["dv0", "dv1"], prev=["dt"])
        s.step("act", "de", lambda i: nc.scalar.activation(de[:, :, :], de[:, :, :], ACT.Exp, scale=-1.0), after=["da"])
        s.step("act", "dl", lambda i: nc.scalar.activation(de[:, :, :], de[:, :, :], ACT.Ln, bias=1.0), after=["de"])
        s.step("dve", "dt", lambda i: nc.vector.scalar_tensor_tensor(dt[:, :, :], dv[:, :, :], 0.0, de[:, :, :], ALU.max, ALU.add),
               after=["dl"], prev=["dx"] + [f"dA{u}" for u in range(UN)])
        s.step("dve", "dx", lambda i: nc.vector.tensor_tensor(dx[:, :, :], dt[:, :, :], xc[:, :, :], ALU.mult), after=["dt"], prev=[f"dbx{UN - 1}0", f"dbx{UN - 1}1"])

        def spread(u, first, b0):
            def go(i):
                for g in range(G):
                    r = first + u * G + g
                    mm = nc.tensor.matmul(PS[:, b0 + g // 2, (g % 2) * SEQ:(g % 2 + 1) * SEQ], self.ident[:, r:r + 1].broadcast_to((P, P)), xd[:, :],
                                          start=True, stop=True)
                return mm
            return go

        def sum_states(u):
            def go(i):
                for c in range(CH):
                    for g in range(G):
                        mm = nc.tensor.matmul(PS[:, 6 + c, 0:SEQ], self.ident[:, :], hc[:, c, g, :], start=(u == 0 and g == 0), stop=(u == UN - 1 and g == G - 1))
                return mm
            s.step("pe", f"y_pe{u}", go, after=[f"hc{u}0", f"hc{u}1"] + ([f"y_pe{u - 1}"] if u else []), prev=["y10", "y11"] if u == 0 else [])

        for u in range(UN):
            s.step("pe", f"b_pe{u}", spread(u, DR, 0), after=["xd"] + ([f"dbx{u - 1}0", f"dbx{u - 1}1"] if u else ["xp", "z_s"]))
            s.step("pe", f"c_pe{u}", spread(u, DR + NS, 2), after=["xd"] + ([f"hc{u - 1}0", f"hc{u - 1}1"] if u else []), prev=[] if u else [f"hc{UN - 1}0", f"hc{UN - 1}1"])
            if u:
                sum_states(u - 1)

            def decay(i, u=u):
                for c in range(CH):
                    for g in range(G):
                        k = u * G + g
                        op = nc.scalar.activation(dA[:, c, g, 1:SEQ], dt[:, c, 1:SEQ], ACT.Exp, scale=na[:, c, k:k + 1])
                return op
            s.step("act", f"dA{u}", decay, after=["dt"] + ([f"h{u - 1}0", f"h{u - 1}1"] if u else []), prev=[] if u else [f"h{UN - 1}0", f"h{UN - 1}1"])
            for c in range(CH):
                s.step("dve", f"dbx{u}{c}", lambda i, c=c: nc.vector.tensor_tensor(
                    db_x[:, c, :, :], dx[:, c, :].unsqueeze(1).broadcast_to((P, G, SEQ)),
                    PS[:, 0:2, :].rearrange("p b (g n) -> p (b g) n", g=2), ALU.mult),
                    after=["dx", f"b_pe{u}"] + ([f"h{u - 1}{c}"] if u else []), prev=[] if u else [f"h{UN - 1}{c}"])
            for c in range(CH):
                s.step("dve", f"h{u}{c}", lambda i, c=c: nc.vector.tensor_tensor_scan(
                    flat(hs[:, c, :, :]), flat(dA[:, c, :, :]), flat(db_x[:, c, :, :]), 0.0, ALU.mult, ALU.add),
                    after=[f"dbx{u}{c}", f"dA{u}"] + ([f"hc{u - 1}{c}"] if u else []), prev=[] if u else [f"hc{UN - 1}{c}"])
            for c in range(CH):
                s.step("dve", f"hc{u}{c}", lambda i, c=c: nc.vector.tensor_tensor(
                    hc[:, c, :, :], hs[:, c, :, :], PS[:, 2:4, :].rearrange("p b (g n) -> p (b g) n", g=2), ALU.mult),
                    after=[f"h{u}{c}", f"c_pe{u}"] + ([f"y_pe{u - 1}"] if u else []), prev=[] if u else [f"y_pe{UN - 1}"])
        sum_states(UN - 1)
        for c in range(CH):
            s.step("dve", f"y1{c}", lambda i, c=c: nc.vector.scalar_tensor_tensor(
                yT[:, c, :], xc[:, c, :], dd[:, c:c + 1], PS[:, 6 + c, 0:SEQ], ALU.mult, ALU.add), after=[f"y_pe{UN - 1}"], prev=["o_pe"])
        s.step("dve", "y2", lambda i: nc.vector.tensor_tensor(yT[:, :, :], yT[:, :, :], zs[:, :, :], ALU.mult), after=["y10", "y11"])
        s.step("pe", "o_pe", lambda i: [nc.tensor.matmul(PS[:, 5, t * P:t * P + P], yT[:, c, t * P:t * P + P], wo[:, c, :], start=(c == 0), stop=(c == CH - 1))
                                        for t in range(TILES) for c in range(CH)][-1], after=["y2", "xd"])
        s.step("dve", "x1", lambda i: nc.vector.tensor_tensor(seq_tiles(X, i + 1), xs[:, :, :], xn[:, :, :], ALU.add), after=["lm_out0", "lm_out1"])
        s.step("dve", "x_out", lambda i: nc.vector.scalar_tensor_tensor(
            seq_tiles(X, i).rearrange("p t d -> p (t d)"), PS[:, 5, 0:SEQ], res[:, :], seq_tiles(X, i).rearrange("p t d -> p (t d)"), ALU.mult, ALU.add),
            after=["o_pe"], prev=["x1"])
        begins = {"xs", "z_pe", "z_put", "xmT_pe", "xmT", "x1"} | {n for n in s.names if n.startswith(("ln_", "lm_"))}
        s.order("dve", ("xs ln_st1 ln_st0 ln_mv1 ln_mv0 cv00 cv01 cv10 cv11 cv20 cv21 cv30 cv31 x_s ln_out0 z_s dv1 "
            "dv0 da ln_out1 lm_st1 lm_st0 lm_mv1 dt dx dbx01 lm_mv0 dbx00 h01 h00 hc01 hc00 dbx10 dbx11 z_put h11 h10 "
            "hc11 hc10 lm_out1 dbx21 lm_out0 dbx20 h21 h20 hc21 hc20 dbx31 dbx30 h30 h31 hc31 hc30 y11 y10 y2 x1 x_out").split())
        s.order("act", ("xp ze z_1 z_r ln_ln ln_rs xe x_1 x_r xd de dl dA0 lm_ln dA1 lm_rs dA2 dA3 xmT").split())
        s.order("pe", ("in_pe0 in_pe1 xd_pe dt_pe b_pe0 z_pe c_pe0 b_pe1 c_pe1 y_pe0 b_pe2 y_pe1 c_pe2 b_pe3 y_pe2 c_pe3 xmT_pe "
            "y_pe3 o_pe").split())
        s.run(part=begins, at=-1, table=EXP_LN)
        s.run(NSEQ - 1, table=EXP_LN)
        s.run(part=s.names - begins, at=NSEQ - 1, table=EXP_LN)

    def L3f(self):
        nc, d, PS, X, Z = self.nc, self.d, self.PS, self.X, self.Z
        DEPTH, H, HD, WIN = 6, 16, 64, 32
        INNER = H * HD
        KEYS = 2 * WIN
        PAIRS = H // 2
        NW = P // WIN
        DI = int(P * 4 * 2 / 3)
        CHK = [(0, P), (P, P), (2 * P, DI - 2 * P)]
        QK_SCALE = 8.0
        GRP = 4 * P
        pre = "L3_ffn_"

        wqkv = self.sb("wqkv", [P, 3 * INNER])
        wo = self.sb("wo", [P, PAIRS // 2, 2, P])
        w1 = self.sb("w1", [P, 2 * DI])
        w2 = self.sb("w2", [P, 3, P])
        b1 = self.sb("b1", [P, 2, 3])
        b2 = self.sb("b2", [P, 1])
        gb = self.sb("gb", [P, 2])
        qks = self.sb("qks", [P, 4, HD])
        rotc = self.sb("rotc", [P, TILES, 4, HD])
        rot = self.sb("rot", [P, TILES, 4, HD])
        lmask = self.sb("lmask", [P, TILES, 2, KEYS])
        lmaskb = self.sb("lmaskb", [P, TILES, 2, PAIRS, KEYS], BF16)
        mean = self.sb("mean", [P, P])
        fn = self.sb("fn", [P, NT * P])
        sT = self.sb("sT", [P, SEQ + 1])
        qz = self.sb("qz", [P, TILES, PAIRS, NW, 2, WIN])
        kT = self.sb("kT", [P, PAIRS, WIN + SEQ])
        vw = self.sb("vw", [P, TILES * NW + 1, PAIRS * HD])
        pT = self.sb("pT", [P, 2 * PAIRS, 2, 2, WIN])
        s = self.stage()
        s.step("sp", "in", lambda i: [nc.sync.dma_start(rotc[:, :, :, :], d["c_rot"]), nc.sync.dma_start(lmask[:, :, :, :], d["c_local"])], dmas=2)
        s.step("pool", "m0", lambda i: nc.gpsimd.memset(mean[:, :], 1.0 / P))
        s.step("pool", "m2", lambda i: nc.gpsimd.memset(sT[:, :], 0.0))
        s.step("pool", "m3", lambda i: nc.gpsimd.memset(qz[:, :, :, :, :, :], 0.0))
        s.step("pool", "m4", lambda i: nc.gpsimd.memset(kT[:, :, :], 0.0))
        s.step("pool", "m5", lambda i: nc.gpsimd.memset(vw[:, :, :], 0.0))
        s.step("pool", "m6", lambda i: nc.gpsimd.memset(pT[:, :, :, :, :], 0.0))
        for t in range(TILES):
            for b in range(2):
                s.step("dve", f"lmaskb{t}_{b}", lambda i, t=t, b=b: nc.vector.tensor_copy(lmaskb[:, t, b, :, :], lmask[:, t, b, :].unsqueeze(1).broadcast_to((P, PAIRS, KEYS))), after=["in"])
        s.run()

        zc = self.sb("zc", [P, SEQ])
        raw = self.sb("raw", [P, 2, 2 * INNER])
        sqr = self.sb("sqr", [P, 2 * INNER])
        ss = self.sb("ss", [P, 2, 2 * H])
        t2 = self.sb("t2", [P, 2 * INNER])
        v2 = self.sb("v2", [P, TILES, 2, PAIRS * HD])
        sm = self.sb("sm", [P, 2 * PAIRS, KEYS])
        mx = self.sb("mx", [P, 2 * PAIRS])
        sl = self.sb("sl", [P, 2 * PAIRS])
        ob = self.sb("ob", [P, 2, PAIRS, HD])
        oT = self.sb("oT", [P, TILES * 2, PAIRS // 2, 2, 2, WIN])
        xc = self.sb("xc", [P, SEQ])
        xq = self.sb("xq", [P, SEQ])
        rs = self.sb("rs", [P, SEQ])
        gg = self.sb("gg", [P, 3, GRP])
        hh = self.sb("hh", [P, 3, GRP])

        def at(name, l):
            a = d[pre + name][bass.ds(l, 1)]
            return a

        with nc.Fori(0, DEPTH) as l:
            s = self.stage()

            def loads(i):
                out = [nc.sync.dma_start(wqkv[:, :], at("Wqkv", l).rearrange("a p n -> (a p) n")),
                       *(nc.sync.dma_start(wo[r * HD:(r + 1) * HD, c, :, :], at("Wo", l).rearrange("a (c r h e) n -> (a c) r e h n", r=2, h=2, e=HD)[c, r])
                         for r in range(2) for c in range(PAIRS // 2)),
                       nc.sync.dma_start(w1[:, :], at("W1", l).rearrange("a p n -> (a p) n")),
                       nc.sync.dma_start(b2[:, :], at("b2", l).rearrange("a (p b) -> (a p) b", b=1)),
                       nc.sync.dma_start(gb[:, 0:1], at("ln_g", l).rearrange("a (p b) -> (a p) b", b=1)),
                       nc.sync.dma_start(gb[:, 1:2], at("ln_b", l).rearrange("a (p b) -> (a p) b", b=1))]
                for c, (o, m) in enumerate(CHK):
                    out.append(nc.sync.dma_start(w2[0:m, c, :], at("W2", l)[:, o:o + m, :].rearrange("a p n -> (a p) n")))
                    for half in range(2):
                        out.append(nc.sync.dma_start(b1[0:m, half, c:c + 1], at("b1", l)[:, half * DI + o:half * DI + o + m].rearrange("a (p b) -> (a p) b", b=1)))
                for n, w in enumerate(("q_scale", "k_scale")):
                    out.append(nc.sync.dma_start(qks[:, 2 * n, :], at(w, l).broadcast_to((P, HD))))
                    for half in range(2):
                        to, fr = half * HD // 2, (1 - half) * HD // 2
                        out.append(nc.sync.dma_start(qks[:, 2 * n + 1, to:to + HD // 2], at(w, l)[:, fr:fr + HD // 2].broadcast_to((P, HD // 2))))
                return out
            s.step("sp", "w", loads, dmas=5 + PAIRS + 9 + 6)
            for t in range(TILES):
                s.step("dve", f"rot{t}", lambda i, t=t: nc.vector.tensor_tensor(rot[:, t, :, :], rotc[:, t, :, :], qks[:, :, :], ALU.mult), after=["w"])
            s.run()

            s = self.stage()
            s.step("dve", "zc", lambda i: nc.vector.tensor_scalar(zc[:, :].unsqueeze(1), Z[:, bass.ds(i + 1, 1), 0:SEQ], 1.0, None, ALU.mult), prev=["p_pe1_5"])

            def front(t):
                for j in range(6):
                    n = 6 * t + j
                    b = n % 3
                    last = (n - 3) % 12
                    freed = [f"raw{last // 6}_{last % 6}"]
                    if j < 4:
                        w = wqkv[:, j * 512:(j + 1) * 512]
                    else:
                        w = wqkv[:, 2 * INNER:].rearrange("p (a h e) -> p h a e", h=2, e=HD)[:, j - 4, :, :]
                    s.step("pe", f"p_pe{t}_{j}", lambda i, b=b, w=w, t=t: nc.tensor.matmul(PS[:, b, :], zc[:, t * P:t * P + P], w, start=True, stop=True),
                           after=["zc"] + (freed if n >= 3 else []), prev=freed if n < 3 else [])
                    if j < 4:
                        s.step("act", f"raw{t}_{j}", lambda i, b=b, j=j, t=t: nc.scalar.activation(raw[:, t, j * 512:(j + 1) * 512], PS[:, b, :], ACT.Copy),
                               after=[f"p_pe{t}_{j}", f"qk_pe{t}_{j}"])
                    else:
                        s.step("act", f"raw{t}_{j}", lambda i, b=b, j=j, t=t: nc.scalar.activation(v2[:, t, j - 4, :], PS[:, b, :], ACT.Copy),
                               after=[f"p_pe{t}_{j}"], prev=["vlow", "vhigh"])
                s.step("act", f"sqr{t}", lambda i, t=t: nc.scalar.activation(sqr[:, :], raw[:, t, :], ACT.Square),
                       after=[f"raw{t}_{j}" for j in range(4)] + (["ss0"] if t else []), prev=[] if t else ["ss1"])
                s.step("dve", f"ss{t}", lambda i, t=t: nc.vector.tensor_reduce(ss[:, t, :], sqr[:, :].rearrange("p (h e) -> p h e", e=HD), AX.X, ALU.add),
                       after=[f"sqr{t}"], prev=[f"rq{t}"])
                s.step("dve", f"sc{t}", lambda i, t=t: nc.vector.tensor_scalar(ss[:, t, :], ss[:, t, :], 1e-24, None, ALU.max), after=[f"ss{t}"])
                s.step("act", f"sl{t}", lambda i, t=t: nc.scalar.activation(ss[:, t, :], ss[:, t, :], ACT.Ln), after=[f"sc{t}"])
                s.step("act", f"sr{t}", lambda i, t=t: nc.scalar.activation(ss[:, t, :], ss[:, t, :], ACT.Exp, scale=-0.5), after=[f"sl{t}"])

                def heads(a):
                    return a.rearrange("p (h e) -> p h e", e=HD)
                s.step("dve", f"rq{t}", lambda i, t=t: nc.vector.tensor_tensor(
                    heads(raw[:, t, :]), heads(raw[:, t, :]), ss[:, t, :].unsqueeze(2).broadcast_to((P, 2 * H, HD)), ALU.mult), after=[f"sr{t}"])

                def sine(i, t=t):
                    for n in range(2):
                        for half in range(2):
                            to = slice(half * HD // 2, (half + 1) * HD // 2)
                            fr = slice((1 - half) * HD // 2, (2 - half) * HD // 2)
                            op = nc.gpsimd.tensor_tensor(heads(t2[:, n * INNER:(n + 1) * INNER])[:, :, to], heads(raw[:, t, n * INNER:(n + 1) * INNER])[:, :, fr],
                                                         rot[:, t, 2 * n + 1, to].unsqueeze(1).broadcast_to((P, H, HD // 2)), ALU.mult)
                    return op

                def cosine(i, t=t):
                    for n in range(2):
                        a = heads(raw[:, t, n * INNER:(n + 1) * INNER])
                        op = nc.vector.tensor_tensor(a, a, rot[:, t, 2 * n, :].unsqueeze(1).broadcast_to((P, H, HD)), ALU.mult)
                    return op
                s.step("pool", f"rn{t}", sine, after=[f"rq{t}"] + (["ra0"] if t else []), prev=[] if t else ["ra1"])
                s.step("dve", f"rc{t}", cosine, after=[f"rn{t}"])
                s.step("pool", f"ra{t}", lambda i, t=t: nc.gpsimd.tensor_tensor(raw[:, t, :], raw[:, t, :], t2[:, :], ALU.add), after=[f"rc{t}"])

            def turned(t):
                for g in range(4):
                    b = 3 + g % 2
                    s.step("pe", f"qk_pe{t}_{g}", lambda i, g=g, b=b, t=t: [nc.tensor.transpose(
                        PS[:, b, c * P:c * P + P], raw[:, t, (4 * g + c) * P:(4 * g + c + 1) * P], self.ident[:, :]) for c in range(4)][-1],
                        after=([f"qk{t}_{g - 2}"] if g >= 2 else ["qk0_2", "qk0_3"] if t else []), prev=[f"ra{t}"] + (["oT1"] if t == 0 and g < 2 else []))
                    src = PS[:, b, :].rearrange("p (c n) -> p c n", n=P)
                    if g < 2:
                        def put(i, g=g, src=src, t=t):
                            for half in range(2):
                                r = slice(half * HD, half * HD + HD)
                                op = nc.scalar.activation(qz[r, t, 4 * g:4 * g + 4, :, half, :], src[r, :, :].rearrange("p c (w q) -> p c w q", q=WIN), ACT.Copy)
                            return op
                        s.step("act", f"qk{t}_{g}", put, after=[f"qk_pe{t}_{g}"], prev=[f"s_pe{t}"])
                    else:
                        s.step("act", f"qk{t}_{g}", lambda i, g=g, t=t, src=src: nc.scalar.activation(
                            kT[:, 4 * (g - 2):4 * (g - 1), WIN + t * P:WIN + (t + 1) * P], src, ACT.Copy), after=[f"qk_pe{t}_{g}"], prev=["s_pe1"])

            def scores(t):
                def go(i):
                    for b in range(2):
                        nc.tensor.matmul(PS[:, 5 + b, :], self.identb[:, :], lmaskb[:, t, b, :, :].rearrange("p a k -> p (a k)"), start=True, stop=False,
                                         skip_group_check=True)
                    for a in range(PAIRS):
                        for w in range(NW):
                            r = slice(w % 2 * HD, w % 2 * HD + HD)
                            mm = nc.tensor.matmul(PS[r, 5 + w // 2, a * KEYS:(a + 1) * KEYS], qz[:, t, a, w, :, :].rearrange("p h q -> p (h q)"),
                                                  kT[:, a, t * P + w * WIN:t * P + w * WIN + KEYS], start=False, stop=True, skip_group_check=True)
                    return mm
                s.step("pe", f"s_pe{t}", go, after=[f"qk{t}_{g}" for g in range(4)] + (["s_sub0"] if t else []), prev=[] if t else ["on1"])

            def softmax(t):
                sc = PS[:, 5:7, :].rearrange("p b (a k) -> p (b a) k", k=KEYS)
                s.step("dve", f"s_max{t}", lambda i: nc.vector.tensor_reduce(mx[:, :], sc, AX.X, ALU.max), after=[f"s_pe{t}"] + (["s_sub0"] if t else []), prev=[] if t else ["s_sub1"])
                s.step("dve", f"s_sub{t}", lambda i: nc.vector.tensor_tensor(sm[:, :, :], sc, mx[:, :].unsqueeze(2).broadcast_to((P, H, KEYS)), ALU.subtract),
                       after=[f"s_max{t}"] + (["pT_pe0", "s_sum0"] if t else []), prev=[] if t else ["pT_pe1", "s_sum1"])
                s.step("act", f"s_exp{t}", lambda i: nc.scalar.activation(sm[:, :, :], sm[:, :, :], ACT.Exp, scale=QK_SCALE), after=[f"s_sub{t}"])
                s.step("dve", f"s_sum{t}", lambda i: nc.vector.tensor_reduce(sl[:, :], sm[:, :, :], AX.X, ALU.add), after=[f"s_exp{t}"] + (["on0"] if t else []), prev=[] if t else ["on1"])
                s.step("dve", f"s_inv{t}", lambda i: nc.vector.reciprocal(sl[:, :], sl[:, :]), after=[f"s_sum{t}"])

            def windows():
                for nm, part, shift in (("vhigh", WIN, 0), ("vlow", 0, 1)):
                    def go(i, part=part, shift=shift):
                        out = []
                        for half in range(2):
                            for k in range(NW):
                                dst = vw[half * HD + part:half * HD + part + WIN, k + shift:k + shift + NW * (TILES - 1) + 1:NW, :]
                                out.append(nc.sync.dma_start(dst, v2[k * WIN:(k + 1) * WIN, :, half, :]))
                        return out
                    s.step("sp", nm, go, after=["raw0_4", "raw0_5", "raw1_4", "raw1_5", "o_pe1"], dmas=2 * NW, dma=nm)

            def back(t):
                def turned_back(src):
                    return [nc.tensor.transpose(PS[:, 3 + n // 4, (n % 4) * P:(n % 4 + 1) * P], src[:, 2 * n:2 * n + 2, :].rearrange("p a k -> p (a k)"), self.ident[:, :])
                            for n in range(PAIRS)][-1]
                s.step("pe", f"pT_pe{t}", lambda i: turned_back(sm), after=[f"s_exp{t}", "qk1_2", "qk1_3"] + (["oT0"] if t else []))

                def spread(i):
                    for p in range(2):
                        for half in range(2):
                            op = nc.scalar.activation(pT[half * HD:(half + 1) * HD, p:2 * PAIRS:2, :, half, :],
                                                      PS[p * HD:(p + 1) * HD, 3:5, :].rearrange("p b (n w h q) -> p (b n) w h q", w=2, h=2, q=WIN)[:, :, :, half, :], ACT.Copy)
                    return op
                s.step("act", f"pT{t}", spread, after=[f"pT_pe{t}"] + (["o_pe0"] if t else []), prev=[] if t else ["o_pe1"])

                def values(i):
                    for a in range(PAIRS):
                        for w in range(NW):
                            mm = nc.tensor.matmul(PS[w % 2 * HD:w % 2 * HD + HD, 5 + w // 2, a * HD:(a + 1) * HD],
                                                  pT[:, w // 2 * PAIRS + a, w % 2, :, :].rearrange("p h q -> p (h q)"),
                                                  vw[:, t * NW + w, a * HD:(a + 1) * HD], start=True, stop=True)
                    return mm
                s.step("pe", f"o_pe{t}", values, after=[f"pT{t}", "s_sub1"] + (["on0"] if t else []), prev=["vlow", "vhigh"], solo=True)
                s.step("dve", f"on{t}", lambda i: nc.vector.tensor_tensor(
                    ob[:, :, :, :].rearrange("p b a e -> p (b a) e"), PS[:, 5:7, :].rearrange("p b (a e) -> p (b a) e", e=HD),
                    sl[:, :].unsqueeze(2).broadcast_to((P, H, HD)), ALU.mult),
                    after=[f"o_pe{t}", f"s_inv{t}"] + (["oT_pe0"] if t else []), prev=[] if t else ["oT_pe1"])
                s.step("pe", f"oT_pe{t}", lambda i: turned_back(ob[:, :, :, :].rearrange("p b a e -> p (b a) e")), after=[f"on{t}", f"pT{t}"])
                s.step("act", f"oT{t}", lambda i: nc.scalar.activation(oT[:, 2 * t:2 * t + 2, :, :, :, :].rearrange("p b n w h q -> p (b n w h q)"),
                                                                       PS[:, 3:5, :].rearrange("p b n -> p (b n)"), ACT.Copy), after=[f"oT_pe{t}"], prev=["w_pe"])

            for t in range(TILES):
                front(t)
            windows()
            begins = set(s.names)
            for t in range(TILES):
                turned(t)
            for t in range(TILES):
                scores(t)
                softmax(t)
                back(t)
            s.step("pe", "w_pe", lambda i: [nc.tensor.matmul(PS[:, 7, 0:SEQ], wo[:, n, h, :], oT[:, :, n, :, h, :], start=(n + h == 0), stop=(n + h == PAIRS // 2))
                                            for n in range(PAIRS // 2) for h in range(2)][-1], after=["oT0", "oT1"], prev=["var"])

            def residual(i):
                for r, c in ((slice(0, HD), slice(0, SEQ)), (slice(HD, P), slice(1, SEQ + 1))):
                    op = nc.vector.tensor_tensor(sT[r, c].unsqueeze(1), Z[r, bass.ds(i, 1), c], PS[r, 7, 0:SEQ].unsqueeze(1), ALU.add)
                return op
            s.step("dve", "zn", residual, after=["w_pe"], prev=["zput", "cent", "m_pe"])
            s.step("dve", "zput", lambda i: nc.vector.tensor_scalar(Z[:, bass.ds(i, 1), :], sT[:, :].unsqueeze(1), 1.0, None, ALU.mult), after=["zn"])
            s.step("pe", "m_pe", lambda i: nc.tensor.matmul(PS[:, 7, SEQ:2 * SEQ], mean[:, :], sT[:, 0:SEQ], start=True, stop=True), after=["zn"])
            s.step("dve", "cent", lambda i: nc.vector.tensor_tensor(xc[:, :], sT[:, 0:SEQ], PS[:, 7, SEQ:2 * SEQ], ALU.subtract), after=["m_pe"], prev=["fn2"])
            s.step("dve", "xq", lambda i: nc.vector.tensor_tensor(xq[:, :], xc[:, :], xc[:, :], ALU.mult), after=["cent"], prev=["v_pe"])
            s.step("pe", "v_pe", lambda i: nc.tensor.matmul(PS[:, 7, SEQ:2 * SEQ], mean[:, :], xq[:, :], start=True, stop=True), after=["xq"])
            s.step("act", "var", lambda i: nc.scalar.activation(rs[:, :], PS[:, 7, SEQ:2 * SEQ], ACT.Ln, bias=self.eps[:, :]), after=["v_pe"], prev=["fn1"])
            s.step("act", "rstd", lambda i: nc.scalar.activation(rs[:, :], rs[:, :], ACT.Exp, scale=-0.5), after=["var"])
            s.step("dve", "fn1", lambda i: nc.vector.tensor_tensor(xc[:, :], xc[:, :], rs[:, :], ALU.mult), after=["rstd"])
            s.step("dve", "fn2", lambda i: nc.vector.tensor_scalar(fn[:, bass.ds(i * SEQ, SEQ)], xc[:, :], gb[:, 0:1], gb[:, 1:2], ALU.mult, ALU.add), after=["fn1"])
            s.order("dve", ("zc s_max0 s_sub0 ss0 s_sum0 sc0 s_inv0 s_max1 s_sub1 rq0 on0 s_sum1 ss1 rc0 sc1 rq1 s_inv1 on1 rc1 zn "
                "zput cent xq fn1 fn2").split())
            s.order("act", ("qk0_1 qk0_0 qk0_3 raw0_0 qk0_2 raw0_3 qk1_0 qk1_1 raw0_2 raw0_1 sqr0 qk1_2 qk1_3 raw1_0 s_exp0 raw0_4 "
                "sl0 sr0 raw0_5 pT0 raw1_2 s_exp1 raw1_1 raw1_3 sqr1 oT0 pT1 sl1 sr1 raw1_4 oT1 raw1_5 var rstd").split())
            s.order("pe", ("qk_pe0_1 qk_pe0_0 qk_pe0_3 p_pe0_0 qk_pe0_2 p_pe0_1 p_pe0_3 qk_pe1_0 qk_pe1_1 p_pe0_2 s_pe0 qk_pe1_2 "
                "qk_pe1_3 p_pe0_4 p_pe1_0 p_pe0_5 s_pe1 pT_pe0 p_pe1_3 p_pe1_2 p_pe1_1 o_pe0 p_pe1_4 oT_pe0 pT_pe1 "
                "p_pe1_5 o_pe1 oT_pe1 w_pe m_pe v_pe").split())
            s.order("pool", ("rn0 ra0 rn1 ra1").split())
            s.run(part=begins, at=-1, table=EXP_LN)
            s.run(NSEQ - 1, table=EXP_LN)
            s.run(part=s.names - begins, at=NSEQ - 1, table=EXP_LN)

            s = self.stage()
            for c, (o, m) in enumerate(CHK):
                s.step("pe", f"g_pe{c}", lambda i, c=c, o=o, m=m: nc.tensor.matmul(PS[0:m, 3 + c, :], w1[:, DI + o:DI + o + m], fn[:, bass.ds(i * GRP, GRP)],
                                                                                   start=True, stop=True), prev=[f"gg{c}"])
                s.step("pe", f"a_pe{c}", lambda i, c=c, o=o, m=m: nc.tensor.matmul(PS[0:m, c, :], w1[:, o:o + m], fn[:, bass.ds(i * GRP, GRP)],
                                                                                   start=True, stop=True), prev=[f"hh{c}"])
                s.step("act", f"gg{c}", lambda i, c=c, m=m: nc.scalar.activation(gg[0:m, c, :], PS[0:m, 3 + c, :], ACT.Gelu, bias=b1[0:m, 1, c:c + 1]),
                       after=[f"g_pe{c}"], prev=[f"hh{c}"])
                s.step("dve", f"hh{c}", lambda i, c=c, m=m: nc.vector.scalar_tensor_tensor(hh[0:m, c, :], PS[0:m, c, :], b1[0:m, 0, c:c + 1], gg[0:m, c, :], ALU.add, ALU.mult),
                       after=[f"a_pe{c}", f"gg{c}"], prev=["o_pe"])
            s.step("pe", "o_pe", lambda i: [nc.tensor.matmul(PS[:, 6, :], w2[0:m, c, :], hh[0:m, c, :], start=(c == 0), stop=(c == 2))
                                            for c, (o, m) in enumerate(CHK)][-1], after=["hh0", "hh1", "hh2"], prev=["z_out"])

            def add(i):
                for r, c in ((slice(0, HD), 0), (slice(HD, P), 1)):
                    for q in range(GRP // SEQ):
                        z = Z[r, bass.ds(i * (GRP // SEQ) + q, 1), c:c + SEQ].rearrange("p a n -> p (a n)")
                        op = nc.vector.scalar_tensor_tensor(z, PS[r, 6, q * SEQ:(q + 1) * SEQ], b2[r, :], z, ALU.add, ALU.add)
                return op
            s.step("dve", "z_out", add, after=["o_pe"])
            s.run(NT * P // GRP, table="gelu_and_others")
        zu = self.sb("zu", [P, SEQ])
        s = self.stage()

        def unshift(i):
            for r, c in ((slice(0, HD), 0), (slice(HD, P), 1)):
                op = nc.vector.tensor_scalar(zu[r, :].unsqueeze(1), Z[r, bass.ds(i, 1), c:c + SEQ], 1.0, None, ALU.mult)
            return op
        s.step("dve", "zu", unshift, prev=["pe"])
        s.step("pe", "pe", lambda i: [nc.tensor.transpose(PS[:, 0, t * P:t * P + P], zu[:, t * P:t * P + P], self.ident[:, :]) for t in range(TILES)][-1],
               after=["zu"], prev=["x_out"])
        s.step("dve", "x_out", lambda i: nc.vector.tensor_tensor(seq_tiles(X, i), seq_tiles(X, i), PS[:, 0, 0:SEQ].rearrange("p (t d) -> p t d", t=TILES), ALU.add),
               after=["pe"])
        s.run(NSEQ)


def constants():
    p = np.arange(P)
    c = {"c_ident": np.eye(P, dtype=np.float32)}
    c["c_causal"] = np.where(p[None, :] <= p[:, None], 0.0, NEG).astype(np.float32)
    c["c_causal01"] = (p[:, None] <= p[None, :]).astype(np.float32)
    c["c_head16"] = (p[:, None] // 8 == np.arange(16)[None, :]).astype(np.float32)
    c["c_head8"] = (p[:, None] // 16 == np.arange(8)[None, :]).astype(np.float32)
    q, k = p[:, None] % 32, np.arange(64)[None, :]
    seen = (k >= q) & (k <= q + 32)
    first = seen & ((p[:, None] >= 32) | (k >= 32))
    local = np.where(np.stack([first, seen], 1), 0.0, NEG).astype(np.float32)
    local = local.reshape(2, 2, 1, 32, TILES, 64).repeat(2, axis=2)
    c["c_local"] = np.ascontiguousarray(local.transpose(1, 2, 3, 4, 0, 5)).reshape(P, TILES, 2, 64)
    hd, win = 64, 32
    half = np.arange(0, hd, 2, dtype=np.float32)
    pos = np.arange(SEQ, dtype=np.float32)
    freqs = np.tile(pos[:, None] * (1.0 / 10000.0 ** (half / hd)).astype(np.float32)[None, :], (1, 2))
    power = ((pos - SEQ // 2) / (win // 2)).astype(np.float32)
    scale = np.tile(((half + 0.4 * hd) / (1.4 * hd)).astype(np.float32)[None, :] ** power[:, None], (1, 2))
    sign = np.where(np.arange(hd) < hd // 2, -1.0, 1.0).astype(np.float32)
    rot = np.stack([np.cos(freqs) * scale, np.sin(freqs) * scale * sign, np.cos(freqs) / scale, np.sin(freqs) / scale * sign], 1)
    c["c_rot"] = rot.reshape(TILES, P, 4, hd).swapaxes(0, 1).astype(np.float32)
    return c


def laid_out(x):
    def turn(a):
        return a.T

    def cols(n):
        return lambda a: a.reshape(n, -1, *a.shape[1:]).swapaxes(0, 1)

    def cols_t(n):
        return lambda a: a.T.reshape(n, -1, a.shape[0]).swapaxes(0, 1)

    how = {f"L{n}_attn_{w}": turn for n, ws in ((0, ("Wq", "Wk", "Wv", "Wp")), (1, ("Wq", "Wk", "Wv", "Wo")),
                                                  (2, ("Wq", "Wk", "Wv"))) for w in ws}
    how.update(L1_ffn_b1=cols(4), L2_ffn_Wq=turn, L2_ffn_routers=turn, L2_ffn_Wout_w=turn,
               L3_attn_in_proj_w=turn, L3_attn_x_proj_w=cols_t(2), L3_attn_dt_proj_w=turn,
               L3_attn_out_proj_w=cols_t(2), L3_attn_conv_w=cols(2), L3_attn_conv_b=cols(2), L3_attn_dt_proj_b=cols(2),
               L3_attn_A_log=cols(2), L3_attn_D=cols(2))
    return {(k + "_T" if k in how else k): how.get(k, lambda a: a)(np.asarray(v)) for k, v in x.items()
            if k != "L2_ffn_leaf_keys"}


def kernel(**inputs):
    import concourse.bacc as _bacc
    from concourse.bass_utils import run_bass_kernel_spmd as _run

    nc = _bacc.Bacc("TRN2", target_bir_lowering=False, num_devices=1)
    arrays, aps = {}, {}
    given = {k: np.ascontiguousarray(v) for k, v in laid_out(inputs).items()}
    for name, a in list(given.items()) + list(constants().items()):
        a = a.reshape(a.shape or (1,))
        arrays[f"in_{name}"] = a
        aps[name] = nc.dram_tensor(f"in_{name}", a.shape, mybir.dt.from_np(a.dtype), kind="ExternalInput").ap()
    out = nc.dram_tensor("out", (NSEQ, SEQ, P), F32, kind="ExternalOutput").ap()
    Kernel(nc, aps, out, ('L0', 'L1', 'L2', 'L3a', 'L3f')).build()
    r = _run(nc, [arrays], core_ids=[0])
    return r.results[0]["out"]
```
